# Optimizing a Trainium2 kernel written in Bass

```python
import numpy as np
import jax
import jax.numpy as jnp

def _softmax(x, axis=-1):
    return jax.nn.softmax(x, axis=axis)

def _gelu(x):
    return jax.nn.gelu(x, approximate=True)

def _silu(x):
    return jax.nn.silu(x)

def _sigmoid(x):
    return jax.nn.sigmoid(x)

def _layernorm(x, axis=-1, eps=1e-05):
    m = jnp.mean(x, axis=axis, keepdims=True)
    v = jnp.var(x, axis=axis, keepdims=True)
    return (x - m) / jnp.sqrt(v + eps)

def _scatter_add(tgt, idx, src, axis=0):
    return tgt.at[idx].add(src)

def _segment_sum(src, seg, n):
    return jax.ops.segment_sum(src, seg, n)
kernel_name = 'mk_cond_seq_d4_seqx_r4_a32db9'

def setup_inputs(seed: int=0):
    np.random.seed(seed)
    _w = jnp.asarray

    def _rec_inputs():
        import jax
        import jax.numpy as jnp
        _rk = jax.random.key(seed)
        x = -0.000125 + 0.9999 * jax.random.normal(jax.random.fold_in(_rk, 1), (32, 64, 256), jnp.float32)
        _lenS = 64 - jax.random.randint(jax.random.fold_in(_rk, 7), (32,), 0, max(1, 64 // 4) + 1, jnp.int32)
        _lenS2 = 64 - jax.random.randint(jax.random.fold_in(_rk, 8), (32,), 0, max(1, 64 // 4) + 1, jnp.int32)
        itok_B_0_15 = jax.random.randint(jax.random.fold_in(_rk, 11), (32,), 0, 16, jnp.int32)
        itok_B_34_63 = jax.random.randint(jax.random.fold_in(_rk, 13), (32,), 34, 64, jnp.int32)
        fside_Bx16xSxS_0 = -1.47943e-05 + 1.00017 * jax.random.normal(jax.random.fold_in(_rk, 14), (32, 16, 64, 64), jnp.float32)
        condB_theta = jax.random.uniform(jax.random.fold_in(_rk, 15), (32,), jnp.float32, 0.0, 0.983423)
        condB_phi = jax.random.uniform(jax.random.fold_in(_rk, 16), (32,), jnp.float32, 0.0, 0.961312)
        itok_B_6_14 = jax.random.randint(jax.random.fold_in(_rk, 17), (32,), 6, 15, jnp.int32)
        _validS = jnp.arange(64)[None, :] < _lenS[:, None]
        _validS2 = jnp.arange(64)[None, :] < _lenS2[:, None]
        _causal = jnp.tril(jnp.ones((64, 64), dtype=bool))
        mask_Bx1xSxS_bk0 = jnp.logical_not(jnp.broadcast_to(_validS[:, None, None, :], (32, 1, 64, 64)))
        return (x, itok_B_0_15, itok_B_34_63, fside_Bx16xSxS_0, condB_theta, condB_phi, itok_B_6_14, mask_Bx1xSxS_bk0)
    x, itok_B_0_15, itok_B_34_63, fside_Bx16xSxS_0, condB_theta, condB_phi, itok_B_6_14, mask_Bx1xSxS_bk0 = _rec_inputs()

    def _L0_cond_setup():
        import jax, jax.numpy as jnp
        import numpy as np
        B, S, D = (32, 256, 256)
        A = 64
        E = 16
        LN_EPS = 1e-05
        key = jax.random.key(seed)
        ks = jax.random.split(key, 10)
        s = lambda fan_in: 1.0 / np.sqrt(fan_in)
        return {'hidden_states': jax.random.normal(ks[0], (B, S, D), dtype=jnp.float32), 'domain_id': jax.random.randint(ks[1], (B,), 0, E, dtype=jnp.int64), 'down_W': jax.random.uniform(ks[2], (A, D), jnp.float32, -s(D), s(D)), 'down_b': jax.random.uniform(ks[3], (A,), jnp.float32, -s(D), s(D)), 'up_W': jax.random.uniform(ks[4], (D, A), jnp.float32, -s(A), s(A)), 'up_b': jax.random.uniform(ks[5], (D,), jnp.float32, -s(A), s(A)), 'expert_W': jax.random.uniform(ks[6], (E, A, A), jnp.float32, -s(A), s(A)), 'expert_b': jax.random.uniform(ks[7], (E, A), jnp.float32, -s(A), s(A)), 'domain_emb': jax.random.normal(ks[8], (E, A), dtype=jnp.float32), 'ln_gamma': jnp.ones((D,), jnp.float32), 'ln_beta': jnp.zeros((D,), jnp.float32)}
    _L0_cond_all = _L0_cond_setup()
    _L0_cond_in = {k: v for k, v in _L0_cond_all.items() if k in ('down_W', 'down_b', 'up_W', 'up_b', 'expert_W', 'expert_b', 'domain_emb', 'ln_gamma', 'ln_beta')}
    del _L0_cond_all

    def _L1_cond_setup():
        import jax, jax.numpy as jnp
        import numpy as np
        import math
        D_MODEL = 256
        N_HEAD = 16
        HEAD_DIM = D_MODEL // N_HEAD
        D_FF = 1024
        NUM_STEPS = 100.0
        RESCALE = 4000.0
        EPS = 1e-05

        def _sin_emb(t):
            half = D_MODEL // 2
            x = t.astype(jnp.float32) / NUM_STEPS * RESCALE
            freqs = jnp.exp(jnp.arange(half, dtype=jnp.float32) * (-math.log(10000.0) / (half - 1)))
            e = x[:, None] * freqs[None, :]
            return jnp.concatenate([jnp.sin(e), jnp.cos(e)], axis=-1)

        def _ln(x):
            m = jnp.mean(x, axis=-1, keepdims=True)
            v = jnp.var(x, axis=-1, keepdims=True)
            return (x - m) / jnp.sqrt(v + EPS)

        def _gelu2(x):
            return x * jax.nn.sigmoid(1.702 * x)
        key = jax.random.key(seed)
        ks = jax.random.split(key, 24)
        B, S, D, F = (4, 128, D_MODEL, D_FF)
        std = 0.02
        inp = {'src': jax.random.normal(ks[0], (B, S, D), dtype=jnp.float32), 'src_mask': jax.random.randint(ks[1], (B, 1, S, S), 0, 2).astype(bool), 'timestep': jax.random.randint(ks[2], (B,), 0, 100, dtype=jnp.int32), 'attention_bias': jax.random.normal(ks[3], (B, N_HEAD, S, S), dtype=jnp.float32), 'W_ada': jax.random.normal(ks[4], (D, 2 * D), dtype=jnp.float32) * std, 'b_ada': jnp.zeros((2 * D,), dtype=jnp.float32), 'Wq': jax.random.normal(ks[5], (D, D), dtype=jnp.float32) * std, 'bq': jnp.zeros((D,), dtype=jnp.float32), 'Wk': jax.random.normal(ks[6], (D, D), dtype=jnp.float32) * std, 'bk': jnp.zeros((D,), dtype=jnp.float32), 'Wv': jax.random.normal(ks[7], (D, D), dtype=jnp.float32) * std, 'bv': jnp.zeros((D,), dtype=jnp.float32), 'Wo': jax.random.normal(ks[8], (D, D), dtype=jnp.float32) * std, 'bo': jnp.zeros((D,), dtype=jnp.float32), 'W1': jax.random.normal(ks[9], (D, F), dtype=jnp.float32) * std, 'b1': jnp.zeros((F,), dtype=jnp.float32), 'W2': jax.random.normal(ks[10], (F, D), dtype=jnp.float32) * std, 'b2': jnp.zeros((D,), dtype=jnp.float32), 'g2': jnp.ones((D,), dtype=jnp.float32), 'beta2': jnp.zeros((D,), dtype=jnp.float32)}
        return inp
    _L1_cond_all = _L1_cond_setup()
    _L1_cond_in = {k: v for k, v in _L1_cond_all.items() if k in ('W_ada', 'b_ada', 'Wq', 'bq', 'Wk', 'bk', 'Wv', 'bv', 'Wo', 'bo', 'W1', 'b1', 'W2', 'b2', 'g2', 'beta2')}
    del _L1_cond_all

    def _L2_cond_setup():
        import jax, jax.numpy as jnp
        import numpy as np
        key = jax.random.key(seed)
        k1, k2, k3 = jax.random.split(key, 3)
        B, N, D = (16, 1024, 256)
        embeddings = jax.random.normal(k1, (B, N, D), dtype=jnp.float32)
        theta = jax.random.uniform(k2, (B,), dtype=jnp.float32)
        phi = jax.random.uniform(k3, (B,), dtype=jnp.float32)
        return {'embeddings': embeddings, 'theta': theta, 'phi': phi}
    _L2_cond_all = _L2_cond_setup()
    _L2_cond_in = {k: v for k, v in _L2_cond_all.items() if k in ()}
    del _L2_cond_all

    def _L3_cond_setup():
        import jax, jax.numpy as jnp
        import numpy as np
        D = 256
        E = 8
        FF = 1024
        TOPK = 2
        S = 32
        SE = 64
        SH = 128
        B, T = (2, 512)

        def _forward(x, subject_ids, ln_g, ln_b, subj_emb, hyp_w1, hyp_b1, hyp_w2, hyp_b2, sty_w1, sty_b1, sty_w2, sty_b2, router_w, exp_w1, exp_b1, exp_w2, exp_b2):
            mu = x.mean(-1, keepdims=True)
            var = x.var(-1, keepdims=True)
            h = (x - mu) * jax.lax.rsqrt(var + 1e-05) * ln_g + ln_b
            m_t = h.mean(1, keepdims=True)
            v_t = h.var(1, keepdims=True)
            h_norm = (h - m_t) * jax.lax.rsqrt(v_t + 1e-08)
            se = subj_emb[subject_ids]
            hyp = jax.nn.relu(se @ hyp_w1 + hyp_b1) @ hyp_w2 + hyp_b2
            sty = jax.nn.relu(hyp @ sty_w1 + sty_b1) @ sty_w2 + sty_b2
            gamma, beta = jnp.split(sty, 2, axis=-1)
            gamma = jax.nn.softplus(gamma) + 1e-08
            h = h_norm * gamma[:, None, :] + beta[:, None, :]
            h_flat = h.reshape(-1, D)
            probs = jax.nn.softmax(h_flat @ router_w, axis=-1)
            gates, idx = jax.lax.top_k(probs, TOPK)
            gates = gates / gates.sum(-1, keepdims=True)
            N = h_flat.shape[0]
            combine = jnp.zeros((N, E), h_flat.dtype).at[jnp.arange(N)[:, None], idx].add(gates)
            hid = jax.nn.relu(jnp.einsum('nd,edf->nef', h_flat, exp_w1) + exp_b1)
            eout = jnp.einsum('nef,efd->ned', hid, exp_w2) + exp_b2
            y = jnp.einsum('ned,ne->nd', eout, combine)
            return x + y.reshape(x.shape)
        key = jax.random.key(seed)
        ks = jax.random.split(key, 16)
        n = lambda k, sh, s=0.02: jax.random.normal(k, sh, dtype=jnp.float32) * s
        return {'x': jax.random.normal(ks[0], (B, T, D), dtype=jnp.float32), 'subject_ids': jax.random.randint(ks[1], (B,), 0, S), 'ln_g': jnp.ones((D,), jnp.float32), 'ln_b': jnp.zeros((D,), jnp.float32), 'subj_emb': n(ks[2], (S, SE)), 'hyp_w1': n(ks[3], (SE, SH), 1.0 / np.sqrt(SE)), 'hyp_b1': jnp.zeros((SH,), jnp.float32), 'hyp_w2': n(ks[4], (SH, SH), 1.0 / np.sqrt(SH)), 'hyp_b2': jnp.zeros((SH,), jnp.float32), 'sty_w1': n(ks[5], (SH, SH // 2), 1.0 / np.sqrt(SH)), 'sty_b1': jnp.zeros((SH // 2,), jnp.float32), 'sty_w2': n(ks[6], (SH // 2, 2 * D), 1.0 / np.sqrt(SH // 2)), 'sty_b2': jnp.zeros((2 * D,), jnp.float32), 'router_w': n(ks[7], (D, E), 1.0 / np.sqrt(D)), 'exp_w1': n(ks[8], (E, D, FF), 1.0 / np.sqrt(D)), 'exp_b1': jnp.zeros((E, FF), jnp.float32), 'exp_w2': n(ks[9], (E, FF, D), 1.0 / np.sqrt(FF)), 'exp_b2': jnp.zeros((E, D), jnp.float32)}
    _L3_cond_all = _L3_cond_setup()
    _L3_cond_in = {k: v for k, v in _L3_cond_all.items() if k in ('ln_g', 'ln_b', 'subj_emb', 'hyp_w1', 'hyp_b1', 'hyp_w2', 'hyp_b2', 'sty_w1', 'sty_b1', 'sty_w2', 'sty_b2', 'router_w', 'exp_w1', 'exp_b1', 'exp_w2', 'exp_b2')}
    del _L3_cond_all
    return {'x': x, 'itok_B_0_15': itok_B_0_15, 'itok_B_34_63': itok_B_34_63, 'fside_Bx16xSxS_0': fside_Bx16xSxS_0, 'condB_theta': condB_theta, 'condB_phi': condB_phi, 'itok_B_6_14': itok_B_6_14, 'mask_Bx1xSxS_bk0': mask_Bx1xSxS_bk0, 'L0_cond_down_W': _L0_cond_in['down_W'], 'L0_cond_down_b': _L0_cond_in['down_b'], 'L0_cond_up_W': _L0_cond_in['up_W'], 'L0_cond_up_b': _L0_cond_in['up_b'], 'L0_cond_expert_W': _L0_cond_in['expert_W'], 'L0_cond_expert_b': _L0_cond_in['expert_b'], 'L0_cond_domain_emb': _L0_cond_in['domain_emb'], 'L0_cond_ln_gamma': _L0_cond_in['ln_gamma'], 'L0_cond_ln_beta': _L0_cond_in['ln_beta'], 'L1_cond_W_ada': _L1_cond_in['W_ada'], 'L1_cond_b_ada': _L1_cond_in['b_ada'], 'L1_cond_Wq': _L1_cond_in['Wq'], 'L1_cond_bq': _L1_cond_in['bq'], 'L1_cond_Wk': _L1_cond_in['Wk'], 'L1_cond_bk': _L1_cond_in['bk'], 'L1_cond_Wv': _L1_cond_in['Wv'], 'L1_cond_bv': _L1_cond_in['bv'], 'L1_cond_Wo': _L1_cond_in['Wo'], 'L1_cond_bo': _L1_cond_in['bo'], 'L1_cond_W1': _L1_cond_in['W1'], 'L1_cond_b1': _L1_cond_in['b1'], 'L1_cond_W2': _L1_cond_in['W2'], 'L1_cond_b2': _L1_cond_in['b2'], 'L1_cond_g2': _L1_cond_in['g2'], 'L1_cond_beta2': _L1_cond_in['beta2'], 'L3_cond_ln_g': _L3_cond_in['ln_g'], 'L3_cond_ln_b': _L3_cond_in['ln_b'], 'L3_cond_subj_emb': _L3_cond_in['subj_emb'], 'L3_cond_hyp_w1': _L3_cond_in['hyp_w1'], 'L3_cond_hyp_b1': _L3_cond_in['hyp_b1'], 'L3_cond_hyp_w2': _L3_cond_in['hyp_w2'], 'L3_cond_hyp_b2': _L3_cond_in['hyp_b2'], 'L3_cond_sty_w1': _L3_cond_in['sty_w1'], 'L3_cond_sty_b1': _L3_cond_in['sty_b1'], 'L3_cond_sty_w2': _L3_cond_in['sty_w2'], 'L3_cond_sty_b2': _L3_cond_in['sty_b2'], 'L3_cond_router_w': _L3_cond_in['router_w'], 'L3_cond_exp_w1': _L3_cond_in['exp_w1'], 'L3_cond_exp_b1': _L3_cond_in['exp_b1'], 'L3_cond_exp_w2': _L3_cond_in['exp_w2'], 'L3_cond_exp_b2': _L3_cond_in['exp_b2']}

def reference(x, itok_B_0_15, itok_B_34_63, fside_Bx16xSxS_0, condB_theta, condB_phi, itok_B_6_14, mask_Bx1xSxS_bk0, L0_cond_down_W, L0_cond_down_b, L0_cond_up_W, L0_cond_up_b, L0_cond_expert_W, L0_cond_expert_b, L0_cond_domain_emb, L0_cond_ln_gamma, L0_cond_ln_beta, L1_cond_W_ada, L1_cond_b_ada, L1_cond_Wq, L1_cond_bq, L1_cond_Wk, L1_cond_bk, L1_cond_Wv, L1_cond_bv, L1_cond_Wo, L1_cond_bo, L1_cond_W1, L1_cond_b1, L1_cond_W2, L1_cond_b2, L1_cond_g2, L1_cond_beta2, L3_cond_ln_g, L3_cond_ln_b, L3_cond_subj_emb, L3_cond_hyp_w1, L3_cond_hyp_b1, L3_cond_hyp_w2, L3_cond_hyp_b2, L3_cond_sty_w1, L3_cond_sty_b1, L3_cond_sty_w2, L3_cond_sty_b2, L3_cond_router_w, L3_cond_exp_w1, L3_cond_exp_b1, L3_cond_exp_w2, L3_cond_exp_b2):
    import jax
    import jax.numpy as jnp

    def _L0_cond_ref(hidden_states, domain_id, down_W, down_b, up_W, up_b, expert_W, expert_b, domain_emb, ln_gamma, ln_beta):
        import jax, jax.numpy as jnp
        import numpy as np
        B, S, D = (32, 256, 256)
        A = 64
        E = 16
        LN_EPS = 1e-05
        residual = hidden_states
        hidden = jnp.einsum('bsd,ad->bsa', hidden_states, down_W) + down_b
        hidden = jax.nn.gelu(hidden, approximate=False)
        valid = (domain_id >= 0) & (domain_id < E)
        idx = jnp.clip(domain_id, 0, E - 1)
        Wsel = expert_W[idx]
        bsel = expert_b[idx]
        expert_out = jnp.einsum('bsa,boa->bso', hidden, Wsel) + bsel[:, None, :]
        domain_output = jnp.where(valid[:, None, None], expert_out, hidden)
        hidden = domain_output + domain_emb[idx][:, None, :]
        hidden = jnp.einsum('bsa,da->bsd', hidden, up_W) + up_b
        x = hidden + residual
        mu = jnp.mean(x, axis=-1, keepdims=True)
        var = jnp.mean(jnp.square(x - mu), axis=-1, keepdims=True)
        return (x - mu) * jax.lax.rsqrt(var + LN_EPS) * ln_gamma + ln_beta

    def _L1_cond_ref(src, src_mask, timestep, attention_bias, W_ada, b_ada, Wq, bq, Wk, bk, Wv, bv, Wo, bo, W1, b1, W2, b2, g2, beta2):
        import jax, jax.numpy as jnp
        import numpy as np
        import math
        D_MODEL = 256
        N_HEAD = 16
        HEAD_DIM = D_MODEL // N_HEAD
        D_FF = 1024
        NUM_STEPS = 100.0
        RESCALE = 4000.0
        EPS = 1e-05

        def _sin_emb(t):
            half = D_MODEL // 2
            x = t.astype(jnp.float32) / NUM_STEPS * RESCALE
            freqs = jnp.exp(jnp.arange(half, dtype=jnp.float32) * (-math.log(10000.0) / (half - 1)))
            e = x[:, None] * freqs[None, :]
            return jnp.concatenate([jnp.sin(e), jnp.cos(e)], axis=-1)

        def _ln(x):
            m = jnp.mean(x, axis=-1, keepdims=True)
            v = jnp.var(x, axis=-1, keepdims=True)
            return (x - m) / jnp.sqrt(v + EPS)

        def _gelu2(x):
            return x * jax.nn.sigmoid(1.702 * x)
        B, S, D = src.shape
        emb = jax.nn.silu(_sin_emb(timestep)) @ W_ada + b_ada
        scale, shift = jnp.split(emb[:, None, :], 2, axis=-1)
        x = _ln(src) * (1.0 + scale) + shift
        q = (x @ Wq + bq).reshape(B, S, N_HEAD, HEAD_DIM).transpose(0, 2, 1, 3)
        k = (x @ Wk + bk).reshape(B, S, N_HEAD, HEAD_DIM).transpose(0, 2, 1, 3)
        v = (x @ Wv + bv).reshape(B, S, N_HEAD, HEAD_DIM).transpose(0, 2, 1, 3)
        scores = jnp.einsum('bhqd,bhkd->bhqk', q / math.sqrt(HEAD_DIM), k)
        scores = scores + attention_bias
        scores = jnp.where(src_mask, -jnp.inf, scores.astype(jnp.float32))
        probs = jax.nn.softmax(scores, axis=-1).astype(v.dtype)
        ctx = jnp.einsum('bhqk,bhkd->bhqd', probs, v)
        ctx = ctx.transpose(0, 2, 1, 3).reshape(B, S, D)
        x = x + (ctx @ Wo + bo)
        h = _ln(x) * g2 + beta2
        ff = _gelu2(h @ W1 + b1) @ W2 + b2
        return x + ff

    def _L2_cond_ref(embeddings, theta, phi):
        import jax, jax.numpy as jnp
        import numpy as np
        B, N, D = embeddings.shape
        e = embeddings.reshape(B, N, D // 4, 4)
        ct = jnp.cos(theta)[:, None, None]
        st = jnp.sin(theta)[:, None, None]
        cp = jnp.cos(phi)[:, None, None]
        sp = jnp.sin(phi)[:, None, None]
        x0, x1, x2, x3 = (e[..., 0], e[..., 1], e[..., 2], e[..., 3])
        out = jnp.stack([x0 * ct + x1 * st, -x0 * st + x1 * ct, x2 * cp + x3 * sp, -x2 * sp + x3 * cp], axis=-1)
        return out.reshape(B, N, D)

    def _L3_cond_ref(x, subject_ids, ln_g, ln_b, subj_emb, hyp_w1, hyp_b1, hyp_w2, hyp_b2, sty_w1, sty_b1, sty_w2, sty_b2, router_w, exp_w1, exp_b1, exp_w2, exp_b2):
        import jax, jax.numpy as jnp
        import numpy as np
        D = 256
        E = 8
        FF = 1024
        TOPK = 2
        S = 32
        SE = 64
        SH = 128
        B, T = (2, 512)

        def _forward(x, subject_ids, ln_g, ln_b, subj_emb, hyp_w1, hyp_b1, hyp_w2, hyp_b2, sty_w1, sty_b1, sty_w2, sty_b2, router_w, exp_w1, exp_b1, exp_w2, exp_b2):
            mu = x.mean(-1, keepdims=True)
            var = x.var(-1, keepdims=True)
            h = (x - mu) * jax.lax.rsqrt(var + 1e-05) * ln_g + ln_b
            m_t = h.mean(1, keepdims=True)
            v_t = h.var(1, keepdims=True)
            h_norm = (h - m_t) * jax.lax.rsqrt(v_t + 1e-08)
            se = subj_emb[subject_ids]
            hyp = jax.nn.relu(se @ hyp_w1 + hyp_b1) @ hyp_w2 + hyp_b2
            sty = jax.nn.relu(hyp @ sty_w1 + sty_b1) @ sty_w2 + sty_b2
            gamma, beta = jnp.split(sty, 2, axis=-1)
            gamma = jax.nn.softplus(gamma) + 1e-08
            h = h_norm * gamma[:, None, :] + beta[:, None, :]
            h_flat = h.reshape(-1, D)
            probs = jax.nn.softmax(h_flat @ router_w, axis=-1)
            gates, idx = jax.lax.top_k(probs, TOPK)
            gates = gates / gates.sum(-1, keepdims=True)
            N = h_flat.shape[0]
            combine = jnp.zeros((N, E), h_flat.dtype).at[jnp.arange(N)[:, None], idx].add(gates)
            hid = jax.nn.relu(jnp.einsum('nd,edf->nef', h_flat, exp_w1) + exp_b1)
            eout = jnp.einsum('nef,efd->ned', hid, exp_w2) + exp_b2
            y = jnp.einsum('ned,ne->nd', eout, combine)
            return x + y.reshape(x.shape)
        return _forward(x, subject_ids, ln_g, ln_b, subj_emb, hyp_w1, hyp_b1, hyp_w2, hyp_b2, sty_w1, sty_b1, sty_w2, sty_b2, router_w, exp_w1, exp_b1, exp_w2, exp_b2)
    x = _L0_cond_ref(x, itok_B_0_15, L0_cond_down_W, L0_cond_down_b, L0_cond_up_W, L0_cond_up_b, L0_cond_expert_W, L0_cond_expert_b, L0_cond_domain_emb, L0_cond_ln_gamma, L0_cond_ln_beta)
    x = _L1_cond_ref(x, mask_Bx1xSxS_bk0, itok_B_34_63, fside_Bx16xSxS_0, L1_cond_W_ada, L1_cond_b_ada, L1_cond_Wq, L1_cond_bq, L1_cond_Wk, L1_cond_bk, L1_cond_Wv, L1_cond_bv, L1_cond_Wo, L1_cond_bo, L1_cond_W1, L1_cond_b1, L1_cond_W2, L1_cond_b2, L1_cond_g2, L1_cond_beta2)
    x = _L2_cond_ref(x, condB_theta, condB_phi)
    x = _L3_cond_ref(x, itok_B_6_14, L3_cond_ln_g, L3_cond_ln_b, L3_cond_subj_emb, L3_cond_hyp_w1, L3_cond_hyp_b1, L3_cond_hyp_w2, L3_cond_hyp_b2, L3_cond_sty_w1, L3_cond_sty_b1, L3_cond_sty_w2, L3_cond_sty_b2, L3_cond_router_w, L3_cond_exp_w1, L3_cond_exp_b1, L3_cond_exp_w2, L3_cond_exp_b2)
    return x

_drawn_inputs = setup_inputs


def setup_inputs(seed=0):
    import zlib

    import numpy as np

    out = dict(_drawn_inputs(seed))
    spreads = {'L0_cond_ln_gamma': (1.0, 0.2),
     'L0_cond_ln_beta': (0.0, 0.1),
     'L1_cond_b_ada': (0.0, 0.1),
     'L1_cond_bq': (0.0, 0.8),
     'L1_cond_bk': (0.0, 0.8),
     'L1_cond_bv': (0.0, 0.1),
     'L1_cond_bo': (0.0, 0.1),
     'L1_cond_b1': (0.0, 0.1),
     'L1_cond_b2': (0.0, 0.1),
     'L1_cond_g2': (1.0, 0.2),
     'L1_cond_beta2': (0.0, 0.384),
     'L3_cond_ln_g': (1.0, 0.6),
     'L3_cond_ln_b': (0.0, 0.8),
     'L3_cond_hyp_b1': (0.0, 0.1),
     'L3_cond_hyp_b2': (0.0, 0.1),
     'L3_cond_sty_b1': (0.0, 0.1),
     'L3_cond_sty_b2': (0.0, 0.1),
     'L3_cond_exp_b1': (0.0, 0.1),
     'L3_cond_exp_b2': (0.0, 0.1)}
    factors = {'L0_cond_down_b': 2.675, 'L1_cond_Wq': 4.208, 'L1_cond_Wk': 4.332}
    for name, (base, spread) in spreads.items():
        noise = np.random.default_rng([zlib.crc32(name.encode()), seed]).standard_normal(out[name].shape)
        drawn = base * np.exp(spread * noise) if base else spread * noise
        out[name] = jnp.asarray(drawn.astype(out[name].dtype))
    for name, factor in factors.items():
        out[name] = (out[name] * factor).astype(out[name].dtype)
    return out
```

```python
from contextlib import ExitStack

import numpy as np

import concourse.bass as bass
import concourse.mybir as mybir

F32 = mybir.dt.float32
I32 = mybir.dt.int32
U8 = mybir.dt.uint8
ALU = mybir.AluOpType
ACT = mybir.ActivationFunctionType
AX = mybir.AxisListType

P = 128
B, S, D = 32, 64, 256
N = B * S
A = 64
NDOM = 16
H, HD = 16, 16
FF = 1024
E = 8
NSUB, SE, SH = 32, 64, 128
CT = 512
NCH = N // CT
CB = CT // S
TT = CT // P
NT = N // P
KD = D // P
KF = FF // P
HALF_PI = float(np.pi / 2)
INV_2PI = float(1.0 / (2 * np.pi))
ROUND = 12582912.0
TWO_PI_PARTS = (6.28125, 0.0019350051879882812, 3.0199159819460083e-07)
MASKED = -1.0e30
RSQRT_SEED = 1597463007.0


class Count:

    def __init__(self, sem, per, start):
        self.sem, self.per, self.start = sem, per, start

    def of(self, c, n):
        return c * self.per + n + self.start


def build(nc, t, out):
    with ExitStack() as ctx:
        def sb(name, shape, dt=F32):
            return ctx.enter_context(nc.sbuf_tensor(name, shape, dt))

        def sem(name):
            return ctx.enter_context(nc.semaphore(name))

        def count(name, per):
            return Count(sem(name), per, 0)

        def free(name, per):
            return Count(sem(name), per, 1)

        bank = [ctx.enter_context(nc.psum_tensor(f"bank{i}", [P, 512], F32)) for i in range(8)]

        ident = sb("ident", [P, P])
        iota_p = sb("iota_p", [P, 1])
        iota_e = sb("iota_e", [P, E])
        parity = sb("parity", [P, 2])
        freqs = sb("freqs", [P, 1])
        down_w = sb("down_w", [P, KD, A])
        down_b = sb("down_b", [A, 1])
        up_w = sb("up_w", [A + 1, D])
        dom_emb = sb("dom_emb", [NDOM, A])
        exp_b = sb("exp_b", [NDOM, A])
        gamma0 = sb("gamma0", [P, D])
        beta0 = sb("beta0", [P, D])
        w_ada = sb("w_ada", [P, KD, 2 * D])
        b_ada = sb("b_ada", [P, 2 * KD])
        wq = sb("wq", [P, KD, D])
        wk = sb("wk", [P, KD, D])
        wv = sb("wv", [P, KD, D])
        wo = sb("wo", [P, KD, D])
        bq = sb("bq", [P, KD])
        bk = sb("bk", [P, KD])
        bv = sb("bv", [P, KD])
        bo = sb("bo", [P, D])
        w1 = sb("w1", [P, KD, FF])
        b1 = sb("b1", [P, KF])
        w2 = sb("w2", [P, KF, D])
        b2 = sb("b2", [P, D])
        g2 = sb("g2", [P, KD])
        beta2 = sb("beta2", [P, KD])
        ln_g = sb("ln_g", [P, KD])
        ln_b = sb("ln_b", [P, KD])
        subj_emb = sb("subj_emb", [NSUB, SE])
        hyp_w1 = sb("hyp_w1", [SE, SH])
        hyp_b1 = sb("hyp_b1", [SH, 1])
        hyp_w2 = sb("hyp_w2", [SH, SH])
        hyp_b2 = sb("hyp_b2", [SH, 1])
        sty_w1 = sb("sty_w1", [SH, SH // 2])
        sty_b1 = sb("sty_b1", [SH // 2, 1])
        sty_w2 = sb("sty_w2", [SH // 2, 2 * D])
        sty_b2 = sb("sty_b2", [P, 2 * KD])
        router = sb("router", [P, KD, E])
        moe_b1 = sb("moe_b1", [P, E, KF])
        moe_b2 = sb("moe_b2", [E, D])
        mask_u8 = sb("mask_u8", [P, NT, S], U8)
        mask_add = sb("mask_add", [P, NT, S])

        dom_i = sb("dom_i", [P, B], I32)
        dom_f = sb("dom_f", [P, B])
        dom_c = sb("dom_c", [P, B])
        dom_at = sb("dom_at", [1, B], I32)
        valid = sb("valid", [P, B])
        invalid = sb("invalid", [P, B])
        hot_dom = sb("hot_dom", [NDOM, B])
        hot_val = sb("hot_val", [NDOM, B])
        add_o = sb("add_o", [A, B])
        w_all = sb("w_all", [A, B, A])
        sub_i = sb("sub_i", [P, B], I32)
        sub_f = sb("sub_f", [P, B])
        hot_sub = sb("hot_sub", [NSUB, B])
        se = sb("se", [SE, B])
        hyp1 = sb("hyp1", [SH, B])
        hyp2 = sb("hyp2", [SH, B])
        sty1 = sb("sty1", [SH // 2, B])
        sty = sb("sty", [P, 2 * KD, B])
        soft = sb("soft", [P, 4, KD, B])
        gamma3 = sb("gamma3", [P, KD, B])
        time_i = sb("time_i", [P, B], I32)
        time_f = sb("time_f", [P, B])
        quot, q_hi, q_lo = sb("quot", [P, B]), sb("q_hi", [P, B]), sb("q_lo", [P, B])
        angle = sb("angle", [P, B + 2 * NT])
        turns = sb("turns", [P, B + 2 * NT])
        cos_in = sb("cos_in", [P, B + 2 * NT])
        sin_t = sb("sin_t", [P, B + 2 * NT])
        cos_t = sb("cos_t", [P, B + 2 * NT])
        emb = sb("emb", [P, KD, B])
        ada = sb("ada", [P, 2 * KD, B])
        bq4 = sb("bq4", [P, KD])
        bkp = sb("bkp", [P, 2])

        x_f = sb("x_f", [P, KD, CT])
        x_t = sb("x_t", [P, TT, D])
        w_sel = sb("w_sel", [A, CB, A])
        w_id = sb("w_id", [A, CB, A])
        hid = sb("hid", [A, CT])
        hid2 = sb("hid2", [A + 1, CT])
        y = sb("y", [P, TT, D])
        xn1 = y
        x1 = sb("x1", [P, KD, CT])
        q_f = sb("q_f", [P, KD, CT])
        k_f = sb("k_f", [P, KD, 2, CT])
        v_bd = sb("v_bd", [P, CB, H // 2, 2, HD])
        bias = [sb(f"bias{u}", [P, 4, 2, 4, S]) for u in range(2)]
        sc_both = sb("sc_both", [P, 2 * 2048])
        sc = [sc_both[:, 2048 * u:2048 * u + 2048].rearrange("p (r a h k) -> p r a h k", r=4, a=2, h=4)
              for u in range(2)]
        sc_max = [sb(f"sc_max{u}", [P, 32]) for u in range(2)]
        sc_sum = [sb(f"sc_sum{u}", [P, 32]) for u in range(2)]
        sc_inv = [sb(f"sc_inv{u}", [P, 32]) for u in range(2)]
        p_f = [sb(f"p_f{u}", [P, 4, 2, 2, P]) for u in range(2)]
        ctx_f = sb("ctx_f", [P, KD, CT])
        ada_t = ctx_f
        x2 = sb("x2", [P, TT, D])
        x2b = k_f[:, 0].rearrange("p s (i d) -> p (s i) d", d=D)
        xn2 = y
        h_f = q_f
        ff = sc_both[:].rearrange("p (f n) -> p f n", f=KF)
        x3 = x2
        rot = [p_f[1][:, i].rearrange("p a h (x e) -> p (a h) x e", e=2) for i in range(4)]
        x4 = q_f[:].rearrange("p k (i d) -> p (k i) d", d=D)
        xn3 = y
        h0 = ctx_f
        h3 = sb("h3", [P, KD, CT])
        stats = sb("stats", [P, 16, 6])
        mv = sb("mv", [P, 16, 2])
        var = sb("var", [P, 16])
        rstd = sb("rstd", [P, 16])
        newton = sb("newton", [P, 16])
        newton2 = sb("newton2", [P, 16])
        in_a = sb("in_a", [P, 16])
        in_b = sb("in_b", [P, 16])
        logit = sb("logit", [P, TT, E])
        logit2 = sb("logit2", [P, TT, E])
        cand = sb("cand", [P, TT, E])
        hot1 = sb("hot1", [P, TT, E])
        hot2 = sb("hot2", [P, TT, E])
        top1 = sb("top1", [P, TT])
        top2 = sb("top2", [P, TT])
        first = sb("first", [P, TT])
        gap = sb("gap", [P, TT])
        gap_e = sb("gap_e", [P, TT])
        gate_d = sb("gate_d", [P, TT])
        gate1 = sb("gate1", [P, TT])
        gate2 = sb("gate2", [P, TT])
        gate = sb("gate", [P, TT, E])
        gate_f = sb("gate_f", [E, CT])

        gate_all = sb("gate_all", [P, NT, E])
        acc = sb("acc", [P, NT, D])
        h3_all = sb("h3_all", [P, KD, N])
        flat = [v_bd[:].rearrange("p b j s d -> p (b j s d)"), p_f[0][:].rearrange("p r a h q -> p (r a h q)"),
                bias[0][:].rearrange("p r a h k -> p (r a h k)"), bias[1][:].rearrange("p r a h k -> p (r a h k)")]
        moe_w1 = [flat[0].rearrange("p (k f) -> p k f", k=KD), flat[2].rearrange("p (k f) -> p k f", k=KD)]
        moe_w2 = [flat[1].rearrange("p (k d) -> p k d", k=KF), flat[3].rearrange("p (k d) -> p k d", k=KF)]
        moe_h = ff

        early_in, cond_in, main_in = sem("early_in"), sem("cond_in"), sem("main_in")
        setup = sem("setup")
        setup_pe, setup_act = sem("setup_pe"), sem("setup_act")
        zeroed = sem("zeroed")
        dom_ready, w_in = sem("dom_ready"), sem("w_in")
        cond_ready = sem("cond_ready")
        mask_ready = sem("mask_ready")

        x_f_in, x_t_in = count("x_f_in", 16), count("x_t_in", 16)
        bias_in = [count(f"bias_in{u}", 16) for u in range(2)]
        w_sel_ready = count("w_sel_ready", 1)
        w_step = count("w_step", 2)
        down_done, hid_ready = free("down_done", 1), count("hid_ready", 1)
        expert_done, hid2_ready = free("expert_done", 1), count("hid2_ready", 1)
        up_done, y_ready = count("up_done", 2), free("y_ready", 2)
        xn1_ready, turn1_done = count("xn1_ready", 1), count("turn1_done", 2)
        ada_scaled, x1_ready = count("ada_scaled", 2), count("x1_ready", 2)
        q_done, q_ready = count("q_done", 2), count("q_ready", 2)
        k_done, k0_ready, k1_ready = count("k_done", 2), count("k0_ready", 1), count("k1_ready", 1)
        v_done, v0_ready, v1_ready = count("v_done", 2), count("v0_ready", 2), count("v1_ready", 2)
        bias_masked = [count(f"bias_masked{u}", 4) for u in range(2)]
        score_done = [count(f"score_done{u}", 4) for u in range(2)]
        biased = [free(f"biased{u}", 4) for u in range(2)]
        max_ready = [count(f"max_ready{u}", 1) for u in range(2)]
        shifted = [count(f"shifted{u}", 1) for u in range(2)]
        exp_ready = [count(f"exp_ready{u}", 1) for u in range(2)]
        inv_ready = [count(f"inv_ready{u}", 1) for u in range(2)]
        prob_ready = [count(f"prob_ready{u}", 1) for u in range(2)]
        prob_turned = [count(f"prob_turned{u}", 4) for u in range(2)]
        p_f_ready = [count(f"p_f_ready{u}", 4) for u in range(2)]
        ctx_done = [count(f"ctx_done{u}", 1) for u in range(2)]
        ctx_ready = [count(f"ctx_ready{u}", 2) for u in range(2)]
        wo_done, x2_ready = free("wo_done", 2), count("x2_ready", 2)
        x2b_ready = count("x2b_ready", 1)
        xn2_ready, turn2_done, h_ready = count("xn2_ready", 1), count("turn2_done", 2), count("h_ready", 2)
        ff1_done, ff_ready = count("ff1_done", KF), free("ff_ready", KF)
        ff2_done, x3_ready = count("ff2_done", 2), free("x3_ready", 2)
        rot_step, odd_ready = count("rot_step", 2), count("odd_ready", 1)
        xn3_ready, turn3_done, h0_ready = count("xn3_ready", 1), count("turn3_done", 2), free("h0_ready", 2)
        h3_ready, h3_kept = count("h3_ready", 1), free("h3_kept", 1)
        logit_done, gap_ready, gap_exp = count("logit_done", 1), count("gap_ready", 1), count("gap_exp", 1)
        gate_ready, gate_turned, gate_f_ready = count("gate_ready", 1), count("gate_turned", 1), count("gate_f_ready", 1)
        b2_done, acc_ready = count("b2_done", 2), free("acc_ready", 2)
        VEC_STEPS = 91
        vec_step = count("vec_step", VEC_STEPS)

        moe_in = [sem(f"moe_in{j}") for j in range(2)]
        m1_done, mh_ready = count("m1_done", 2 * NCH * KF), free("mh_ready", 2 * NCH * KF)
        m2_done, m_acc = free("m2_done", 2 * NCH * 2), free("m_acc", 2 * NCH * 2)
        out_done = sem("out_done")

        early = [
            (ident, t["ident"]), (iota_p, t["iota_p"]), (down_w, t["down_w"].rearrange("(k p) a -> p k a", p=P)),
            (down_b, t["down_b"]), (up_w, t["up_w"]), (dom_emb, t["dom_emb"]), (exp_b, t["exp_b"]),
            (gamma0, t["gamma0"].broadcast_to([P, D])), (beta0, t["beta0"].broadcast_to([P, D])),
            (dom_i, t["dom_i"].broadcast_to([P, B])),
        ]
        cond = [
            (freqs, t["freqs"]), (time_i, t["time_i"].broadcast_to([P, B])), (sub_i, t["sub_i"].broadcast_to([P, B])),
            (angle, t["angles"]),
            (w_ada, t["w_ada"].rearrange("(k p) n -> p k n", p=P)), (b_ada, t["b_ada"]),
            (subj_emb, t["subj_emb"]), (hyp_w1, t["hyp_w1"]), (hyp_b1, t["hyp_b1"]), (hyp_w2, t["hyp_w2"]),
            (hyp_b2, t["hyp_b2"]), (sty_w1, t["sty_w1"]), (sty_b1, t["sty_b1"]), (sty_w2, t["sty_w2"]),
            (sty_b2, t["sty_b2"]), (bq, t["bq"]), (bk, t["bk"]), (bv, t["bv"]), (parity, t["parity"]),
            (iota_e, t["iota_e"].broadcast_to([P, E])), (mask_u8, t["mask"]),
        ]
        main = [
            (wq, t["wq"].rearrange("(k p) n -> p k n", p=P)), (wk, t["wk"].rearrange("(k p) n -> p k n", p=P)),
            (wv, t["wv"].rearrange("(k p) n -> p k n", p=P)), (wo, t["wo"].rearrange("(k p) n -> p k n", p=P)),
            (bo, t["bo"].broadcast_to([P, D])), (w1, t["w1"].rearrange("(k p) n -> p k n", p=P)), (b1, t["b1"]),
            (w2, t["w2"].rearrange("(k p) n -> p k n", p=P)), (b2, t["b2"].broadcast_to([P, D])),
            (g2, t["g2"]), (beta2, t["beta2"]), (ln_g, t["ln_g"]), (ln_b, t["ln_b"]),
            (router, t["router"].rearrange("(k p) n -> p k n", p=P)), (moe_b1, t["moe_b1"]), (moe_b2, t["moe_b2"]),
        ]
        N_EARLY, N_COND, N_MAIN = 16 * len(early), 16 * len(cond), 16 * len(main)

        block = ctx.enter_context(nc.Block())

        @block.sync
        def _(sp):
            for dst, src in early:
                sp.dma_start(dst[:], src).then_inc(early_in, 16)
            for dst, src in cond:
                sp.dma_start(dst[:], src).then_inc(cond_in, 16)
            sp.wait_ge(dom_ready, 1)
            with sp.Fori(0, B) as b:
                e = sp.value_load(dom_at[0:1, bass.ds(b, 1)], min_val=0, max_val=NDOM - 1)
                sp.dma_start(w_all[:, bass.ds(b, 1), :], t["exp_w"][bass.ds(e, 1), :, :]
                             .rearrange("e a o -> a e o")).then_inc(w_in, 16)
            with sp.Fori(0, NCH) as c:
                sp.wait_ge(down_done.sem, down_done.of(c, 0))
                sp.dma_start(x_f[:], t["x_f"].rearrange("(k p) n -> p k n", p=P)[:, :, bass.ds(c * CT, CT)]
                             ).then_inc(x_f_in.sem, 16)
                sp.wait_ge(y_ready.sem, y_ready.of(c, 0))
                sp.dma_start(x_t[:], t["x_t"].rearrange("(n p) d -> p n d", p=P)[:, bass.ds(c * TT, TT), :]
                             ).then_inc(x_t_in.sem, 16)
                for u in range(2):
                    sp.wait_ge(biased[u].sem, biased[u].of(c, 0))
                    sp.dma_start(bias[u][:].rearrange("p r a h k -> p (r a h k)"),
                                 t["bias"][bass.ds(c * 2 + u, 1), :, :].rearrange("s p n -> (s p) n")
                                 ).then_inc(bias_in[u].sem, 16)
            with sp.Fori(0, E // 2) as i:
                for j in range(2):
                    sp.wait_ge(m2_done.sem, m2_done.of(i, 0))
                    sp.wait_ge(ctx_done[1].sem, ctx_done[1].of(NCH, 0))
                    sp.wait_ge(biased[j].sem, biased[j].of(NCH, 0))
                    sp.dma_start(moe_w1[j][:], t["moe_w1"][bass.ds(i * 2 + j, 1), :, :]
                                 .rearrange("e (k p) f -> p (e k) f", p=P)).then_inc(moe_in[j], 16)
                    sp.dma_start(moe_w2[j][:], t["moe_w2"][bass.ds(i * 2 + j, 1), :, :]
                                 .rearrange("e (k p) d -> p (e k) d", p=P)).then_inc(moe_in[j], 16)
            sp.wait_ge(m_acc.sem, m_acc.of(E // 2, 0))
            sp.dma_start(out.rearrange("(n p) d -> p n d", p=P), acc[:]).then_inc(out_done, 16)
            sp.wait_ge(out_done, 16)

        @block.gpsimd
        def _(pool):
            for free_at_first in (h3_kept,):
                pool.sem_inc(free_at_first.sem, 1)
            for dst, src in main:
                pool.dma_start(dst[:], src).then_inc(main_in, 16)
            pool.wait_ge(cond_in, N_COND)
            pool.tensor_scalar(mask_add[:], mask_u8[:], MASKED, None, ALU.mult).then_inc(mask_ready, 1)
            pool.wait_ge(w_in, 16 * B)
            pool.wait_ge(mask_ready, 1)
            pool.wait_ge(setup, SETUP_DOM)
            pool.wait_ge(cond_ready, 1)
            pool.wait_ge(main_in, N_MAIN)
            with pool.Fori(0, NCH) as c:
                pool.wait_ge(expert_done.sem, expert_done.of(c, 0))
                pool.tensor_tensor(w_sel[:], w_all[:, bass.ds(c * CB, CB), :],
                                   valid[0:A, bass.ds(c * CB, CB)].unsqueeze(2).broadcast_to([A, CB, A]),
                                   ALU.mult).then_inc(w_step.sem, 1)
                pool.tensor_tensor(w_id[:], ident[0:A, 0:A].unsqueeze(1).broadcast_to([A, CB, A]),
                                   invalid[0:A, bass.ds(c * CB, CB)].unsqueeze(2).broadcast_to([A, CB, A]),
                                   ALU.mult).then_inc(w_step.sem, 1)
                pool.wait_ge(w_step.sem, w_step.of(c, 2))
                pool.tensor_tensor(w_sel[:], w_sel[:], w_id[:], ALU.add).then_inc(w_sel_ready.sem, 1)
                for u in range(2):
                    pool.wait_ge(bias_in[u].sem, bias_in[u].of(c, 16))
                    for r in range(4):
                        pool.tensor_tensor(
                            bias[u][:, r], bias[u][:, r],
                            mask_add[:, bass.ds(c * TT + 2 * u, 2), :].unsqueeze(2).broadcast_to([P, 2, 4, S]),
                            ALU.add).then_inc(bias_masked[u].sem, 1)
                for k in range(KD):
                    pool.wait_ge(ada_scaled.sem, ada_scaled.of(c, k + 1))
                    if k == 0:
                        pool.wait_ge(wo_done.sem, wo_done.of(c, 0))
                    pool.tensor_tensor(
                        x1[:, k, :].rearrange("p (b s) -> p b s", s=S),
                        ada_t[:, k, :].rearrange("p (b s) -> p b s", s=S),
                        ada[:, KD + k, bass.ds(c * CB, CB)].unsqueeze(2).broadcast_to([P, CB, S]),
                        ALU.add).then_inc(x1_ready.sem, 1)
                for u in range(2):
                    pool.wait_ge(max_ready[u].sem, max_ready[u].of(c, 1))
                    v = sc[u][:].rearrange("p r a h k -> p (r a h) k")
                    pool.tensor_tensor(v, v, sc_max[u][:].unsqueeze(2).broadcast_to([P, 32, S]),
                                       ALU.subtract).then_inc(shifted[u].sem, 1)
                for u in range(2):
                    pool.wait_ge(inv_ready[u].sem, inv_ready[u].of(c, 1))
                    v = sc[u][:].rearrange("p r a h k -> p (r a h) k")
                    pool.tensor_tensor(v, v, sc_inv[u][:].unsqueeze(2).broadcast_to([P, 32, S]),
                                       ALU.mult).then_inc(prob_ready[u].sem, 1)
                pool.wait_ge(x2_ready.sem, x2_ready.of(c, 2))
                pool.wait_ge(x3_ready.sem, x3_ready.of(c, 0))
                pool.tensor_tensor(x2b[:], x2[:], b2[:].unsqueeze(1).broadcast_to([P, TT, D]),
                                   ALU.add).then_inc(x2b_ready.sem, 1)
                pool.wait_ge(x3_ready.sem, x3_ready.of(c, 2))
                pool.wait_ge(acc_ready.sem, acc_ready.of(c, 0))
                v3 = x3[:].rearrange("p n (i a e) -> p n i a e", a=2, e=2)
                v4 = x4[:].rearrange("p n (i a e) -> p n i a e", a=2, e=2)
                cs = cos_t[:, bass.ds(B + c * TT * 2, TT * 2)].rearrange("p (n a) -> p n a", a=2)
                sn = sin_t[:, bass.ds(B + c * TT * 2, TT * 2)].rearrange("p (n a) -> p n a", a=2)
                cs = cs.unsqueeze(2).broadcast_to([P, TT, S, 2])
                sn = sn.unsqueeze(2).broadcast_to([P, TT, S, 2])
                pool.tensor_tensor(rot[2][:], v3[:, :, :, :, 1], cs, ALU.mult).then_inc(rot_step.sem, 1)
                pool.tensor_tensor(rot[3][:], v3[:, :, :, :, 0], sn, ALU.mult).then_inc(rot_step.sem, 1)
                pool.wait_ge(rot_step.sem, rot_step.of(c, 2))
                pool.tensor_tensor(v4[:, :, :, :, 1], rot[2][:], rot[3][:], ALU.subtract).then_inc(odd_ready.sem, 1)
                pool.wait_ge(h3_ready.sem, h3_ready.of(c, 1))
                pool.tensor_copy(h3_all[:, :, bass.ds(c * CT, CT)], h3[:]).then_inc(h3_kept.sem, 1)

        @block.scalar
        def _(act):
            for free_at_first in (h0_ready, ff_ready, mh_ready):
                act.sem_inc(free_at_first.sem, 1)
            act.wait_ge(setup, SETUP_ANGLES)
            act.activation(sin_t[:], angle[:], ACT.Sin).then_inc(setup_act, 1)
            act.activation(cos_t[:], cos_in[:], ACT.Sin).then_inc(setup_act, 1)
            act.wait_ge(setup_act, 2)
            act.activation(emb[:, 0, :], sin_t[:, 0:B], ACT.Silu).then_inc(setup_act, 1)
            act.activation(emb[:, 1, :], cos_t[:, 0:B], ACT.Silu).then_inc(setup_act, 1)
            act.wait_ge(setup, SETUP_ABS)
            act.activation(soft[:, 1], soft[:, 0], ACT.Exp).then_inc(setup_act, 1)
            act.wait_ge(setup, SETUP_ABS + 1)
            act.activation(soft[:, 3], soft[:, 2], ACT.Ln).then_inc(setup_act, 1)
            act.wait_ge(main_in, N_MAIN)
            act.wait_ge(cond_ready, 1)
            with act.Fori(0, NCH) as c:
                act.wait_ge(down_done.sem, down_done.of(c, 1))
                act.activation(hid[:], bank[4][0:A, :], ACT.Gelu, bias=down_b[:, 0:1]).then_inc(hid_ready.sem, 1)
                for m in range(KD):
                    act.wait_ge(q_done.sem, q_done.of(c, m + 1))
                    act.activation(q_f[:, m, :], bank[m][:], ACT.Identity, bias=bq4[:, m:m + 1],
                                   scale=0.25).then_inc(q_ready.sem, 1)
                act.wait_ge(k_done.sem, k_done.of(c, 1))
                act.activation(k_f[:, 0, 0, :], bank[2][:], ACT.Identity, bias=bkp[:, 0:1], scale=parity[:, 0:1])
                act.activation(k_f[:, 0, 1, :], bank[2][:], ACT.Identity, bias=bkp[:, 1:2],
                               scale=parity[:, 1:2]).then_inc(k0_ready.sem, 1)
                act.wait_ge(v_done.sem, v_done.of(c, 1))
                for s in range(2):
                    act.activation(v_bd[64 * s:64 * s + 64, 0:4, :, s, :].rearrange("p b j d -> p (b j) d"),
                                   bank[6][64 * s:64 * s + 64, :].rearrange("p (j d) -> p j d", d=HD),
                                   ACT.Copy).then_inc(v0_ready.sem, 1)
                for u in range(2):
                    act.wait_ge(shifted[u].sem, shifted[u].of(c, 1))
                    act.activation(sc[u][:], sc[u][:], ACT.Exp).then_inc(exp_ready[u].sem, 1)
                for u in range(2):
                    for r in range(4):
                        act.wait_ge(prob_turned[u].sem, prob_turned[u].of(c, r + 1))
                        act.activation(p_f[u][:, r].rearrange("p a h q -> p (a h q)"), bank[4 + r % 2][:],
                                       ACT.Copy).then_inc(p_f_ready[u].sem, 1)
                    act.wait_ge(ctx_done[u].sem, ctx_done[u].of(c, 1))
                    for k in range(KD):
                        act.activation(ctx_f[:, k, 256 * u:256 * u + 256], bank[6 + u][:, 256 * k:256 * k + 256],
                                       ACT.Identity, bias=bv[:, k:k + 1]).then_inc(ctx_ready[u].sem, 1)
                for k in range(KD):
                    act.wait_ge(turn2_done.sem, turn2_done.of(c, k + 1))
                    act.activation(h_f[:, k, :], bank[4 + k][:], ACT.Identity, bias=beta2[:, k:k + 1],
                                   scale=g2[:, k:k + 1]).then_inc(h_ready.sem, 1)
                for f in range(KF):
                    act.wait_ge(ff1_done.sem, ff1_done.of(c, f + 1))
                    act.activation(ff[:, f, :], bank[f % 4][:], ACT.Gelu_apprx_sigmoid,
                                   bias=b1[:, f:f + 1]).then_inc(ff_ready.sem, 1)
                for k in range(KD):
                    act.wait_ge(turn3_done.sem, turn3_done.of(c, k + 1))
                    act.activation(h0[:, k, :], bank[4 + k][:], ACT.Identity, bias=ln_b[:, k:k + 1],
                                   scale=ln_g[:, k:k + 1]).then_inc(h0_ready.sem, 1)
                act.wait_ge(gap_ready.sem, gap_ready.of(c, 1))
                act.activation(gap_e[:], gap[:], ACT.Exp).then_inc(gap_exp.sem, 1)
            with act.Fori(0, E // 2) as i:
                for j in range(2):
                    for n in range(NCH):
                        for f in range(KF):
                            at = (j * NCH + n) * KF + f + 1
                            act.wait_ge(m1_done.sem, m1_done.of(i, at))
                            act.nop(nofuse=True)
                            act.activation(moe_h[:, f, :], bank[f % 4][:], ACT.Relu,
                                           bias=moe_b1[:, bass.ds(i * 2 + j, 1), f]).then_inc(mh_ready.sem, 1)

        @block.vector
        def _(dve):
            for free_at_first in (y_ready, x3_ready, acc_ready, m_acc, biased[0], biased[1]):
                dve.sem_inc(free_at_first.sem, 1)
            done = [0]

            def step(ins):
                done[0] += 1
                ins.then_inc(setup, 1)
                dve.wait_ge(setup, done[0])

            dve.memset(v_bd[:], 0.0).then_inc(zeroed, 1)
            dve.memset(hid2[A:A + 1, :], 1.0).then_inc(zeroed, 1)
            dve.wait_ge(early_in, N_EARLY)
            step(dve.tensor_copy(dom_f[:], dom_i[:]))
            step(dve.tensor_scalar(dom_c[:], dom_f[:], 0.0, float(NDOM - 1), ALU.max, ALU.min))
            dve.tensor_copy(dom_at[:], dom_c[0:1, :]).then_inc(dom_ready, 1)
            step(dve.tensor_tensor(valid[:], dom_f[:], dom_c[:], ALU.is_equal))
            step(dve.tensor_scalar(hot_dom[:], dom_c[0:NDOM, :], iota_p[0:NDOM, 0:1], None, ALU.is_equal))
            step(dve.tensor_tensor(hot_val[:], hot_dom[:], valid[0:NDOM, :], ALU.mult))
            step(dve.tensor_scalar(invalid[:], valid[:], -1.0, 1.0, ALU.mult, ALU.add))
            assert done[0] == SETUP_DOM
            dve.wait_ge(cond_in, N_COND)
            step(dve.tensor_copy(time_f[:], time_i[:]))
            step(dve.tensor_scalar(quot[:], time_f[:], 0.01, None, ALU.mult))
            step(dve.tensor_scalar(q_hi[:], quot[:], 4097.0, None, ALU.mult))
            step(dve.tensor_tensor(q_lo[:], q_hi[:], quot[:], ALU.subtract))
            step(dve.tensor_tensor(q_hi[:], q_hi[:], q_lo[:], ALU.subtract))
            step(dve.tensor_tensor(q_lo[:], quot[:], q_hi[:], ALU.subtract))
            step(dve.scalar_tensor_tensor(time_f[:], q_hi[:], -100.0, time_f[:], ALU.mult, ALU.add))
            step(dve.scalar_tensor_tensor(time_f[:], q_lo[:], -100.0, time_f[:], ALU.mult, ALU.add))
            step(dve.scalar_tensor_tensor(time_f[:], time_f[:], 0.01, quot[:], ALU.mult, ALU.add))
            step(dve.tensor_scalar(angle[:, 0:B], time_f[:], 4000.0, freqs[:, 0:1], ALU.mult, ALU.mult))
            step(dve.tensor_scalar(turns[:], angle[:], INV_2PI, ROUND, ALU.mult, ALU.add))
            step(dve.tensor_scalar(turns[:], turns[:], ROUND, None, ALU.subtract))
            for part in TWO_PI_PARTS:
                step(dve.scalar_tensor_tensor(angle[:], turns[:], -part, angle[:], ALU.mult, ALU.add))
            step(dve.tensor_scalar(angle[:], angle[:], float(np.float32(3.1415925)), -float(np.float32(3.1415925)),
                                   ALU.min, ALU.max))
            step(dve.scalar_tensor_tensor(cos_in[:], angle[:], -1.0, angle[:], ALU.mult, ALU.max))
            step(dve.tensor_scalar(cos_in[:], cos_in[:], -1.0, HALF_PI, ALU.mult, ALU.add))
            assert done[0] == SETUP_ANGLES
            step(dve.tensor_copy(sub_f[:], sub_i[:]))
            step(dve.tensor_scalar(sub_f[:], sub_f[:], 0.0, float(NSUB - 1), ALU.max, ALU.min))
            step(dve.tensor_scalar(hot_sub[:], sub_f[0:NSUB, :], iota_p[0:NSUB, 0:1], None, ALU.is_equal))
            assert done[0] == SETUP_SUB
            step(dve.tensor_scalar(bq4[:], bq[:], 0.25, None, ALU.mult))
            step(dve.tensor_scalar(bkp[:], parity[:], bk[:, 0:1], None, ALU.mult))
            dve.wait_ge(setup_pe, 1)
            step(dve.tensor_copy(add_o[:], bank[0][0:A, 0:B]))
            dve.wait_ge(setup_pe, 2)
            step(dve.tensor_copy(se[:], bank[1][0:SE, 0:B]))
            assert done[0] == SETUP_SE
            dve.wait_ge(setup_pe, 3)
            step(dve.tensor_scalar(hyp1[:], bank[2][0:SH, 0:B], hyp_b1[:, 0:1], 0.0, ALU.add, ALU.max))
            dve.wait_ge(setup_pe, 4)
            step(dve.tensor_scalar(hyp2[:], bank[3][0:SH, 0:B], hyp_b2[:, 0:1], None, ALU.add))
            dve.wait_ge(setup_pe, 5)
            step(dve.tensor_scalar(sty1[:], bank[4][0:SH // 2, 0:B], sty_b1[:, 0:1], 0.0, ALU.add, ALU.max))
            dve.wait_ge(setup_pe, 6)
            for m in range(2 * KD):
                step(dve.tensor_scalar(sty[:, m, :], bank[5][:, B * m:B * m + B], sty_b2[:, m:m + 1], None, ALU.add))
            step(dve.scalar_tensor_tensor(soft[:, 0], sty[:, 0:KD, :], -1.0, sty[:, 0:KD, :], ALU.mult, ALU.min))
            assert done[0] == SETUP_ABS
            dve.wait_ge(setup_act, 5)
            step(dve.tensor_scalar(soft[:, 2], soft[:, 1], 1.0, None, ALU.add))
            step(dve.tensor_scalar(gamma3[:], soft[:, 2], -1.0, None, ALU.add))
            step(dve.tensor_tensor(gamma3[:], soft[:, 1], gamma3[:], ALU.subtract))
            step(dve.scalar_tensor_tensor(gamma3[:], sty[:, 0:KD, :], 0.0, gamma3[:], ALU.max, ALU.add))
            dve.wait_ge(setup_act, 6)
            step(dve.tensor_tensor(gamma3[:], gamma3[:], soft[:, 3], ALU.add))
            step(dve.tensor_scalar(gamma3[:], gamma3[:], 1e-8, None, ALU.add))
            dve.wait_ge(setup_pe, 7)
            for m in range(2 * KD):
                step(dve.tensor_scalar(ada[:, m, :], bank[6][:, B * m:B * m + B], b_ada[:, m:m + 1],
                                       1.0 if m < KD else 0.0, ALU.add, ALU.add))
            dve.drain().then_inc(cond_ready, 1)
            dve.wait_ge(main_in, N_MAIN)
            dve.wait_ge(setup_act, 6)
            dve.wait_ge(zeroed, 2)

            with dve.Fori(0, NCH) as c:
                n = [0]

                def vec(ins):
                    n[0] += 1
                    ins.then_inc(vec_step.sem, 1)
                    dve.wait_ge(vec_step.sem, vec_step.of(c, n[0]))

                def rsqrt(w, eps):
                    v, r, a, b = var[:, 0:w], rstd[:, 0:w], newton[:, 0:w], newton2[:, 0:w]
                    vec(dve.tensor_scalar(v, mv[:, 0:w, 1], eps, None, ALU.add))
                    vec(dve.tensor_scalar(r.bitcast(I32), v.bitcast(I32), -0.5, RSQRT_SEED, ALU.mult, ALU.add))
                    for _ in range(3):
                        vec(dve.scalar_tensor_tensor(a, r, -0.5, r, ALU.mult, ALU.mult))
                        vec(dve.tensor_tensor(b, a, v, ALU.mult))
                        vec(dve.scalar_tensor_tensor(r, b, 1.5, r, ALU.add, ALU.mult))

                def token_stats(z):
                    for i in range(TT):
                        ins = dve.bn_stats(stats[:, i, :], z[:, i, :])
                    vec(ins)
                    dve.nop(nofuse=True)
                    for i in range(TT):
                        ins = dve.bn_aggr(mv[:, i, :], stats[:, i, :])
                    vec(ins)
                    rsqrt(TT, 1e-5)

                def normalise(dst, z):
                    for i in range(TT):
                        ins = dve.tensor_scalar(dst[:, i, :], z[:, i, :], mv[:, i, 0:1], rstd[:, i:i + 1],
                                                ALU.subtract, ALU.mult)
                    return ins

                dve.wait_ge(expert_done.sem, expert_done.of(c, 1))
                dve.tensor_tensor(hid2[0:A, :].rearrange("p (b s) -> p b s", s=S),
                                  bank[5][0:A, :].rearrange("p (b s) -> p b s", s=S),
                                  add_o[:, bass.ds(c * CB, CB)].unsqueeze(2).broadcast_to([A, CB, S]),
                                  ALU.add).then_inc(hid2_ready.sem, 1)
                dve.wait_ge(x_t_in.sem, x_t_in.of(c, 16))
                for g in range(2):
                    dve.wait_ge(up_done.sem, up_done.of(c, g + 1))
                    dve.tensor_tensor(y[:, 2 * g:2 * g + 2, :], bank[6 + g][:].rearrange("p (n d) -> p n d", d=D),
                                      x_t[:, 2 * g:2 * g + 2, :], ALU.add).then_inc(y_ready.sem, 1)
                dve.wait_ge(y_ready.sem, y_ready.of(c, 2))
                token_stats(y)
                for i in range(TT):
                    ins = dve.scalar_tensor_tensor(y[:, i, :], y[:, i, :], mv[:, i, 0:1], gamma0[:],
                                                   ALU.subtract, ALU.mult)
                vec(ins)
                for i in range(TT):
                    ins = dve.scalar_tensor_tensor(y[:, i, :], y[:, i, :], rstd[:, i:i + 1], beta0[:],
                                                   ALU.mult, ALU.add)
                vec(ins)
                token_stats(y)
                normalise(xn1, y).then_inc(xn1_ready.sem, 1)
                for k in range(KD):
                    dve.wait_ge(turn1_done.sem, turn1_done.of(c, k + 1))
                    dve.tensor_tensor(ada_t[:, k, :].rearrange("p (b s) -> p b s", s=S),
                                      bank[4 + k][:].rearrange("p (b s) -> p b s", s=S),
                                      ada[:, k, bass.ds(c * CB, CB)].unsqueeze(2).broadcast_to([P, CB, S]),
                                      ALU.mult).then_inc(ada_scaled.sem, 1)
                dve.wait_ge(k_done.sem, k_done.of(c, 2))
                dve.tensor_scalar(k_f[:, 1, 0, :], bank[3][:], bk[:, 1:2], parity[:, 0:1], ALU.add, ALU.mult)
                dve.tensor_scalar(k_f[:, 1, 1, :], bank[3][:], bk[:, 1:2], parity[:, 1:2], ALU.add,
                                  ALU.mult).then_inc(k1_ready.sem, 1)
                dve.wait_ge(v_done.sem, v_done.of(c, 2))
                for s in range(2):
                    dve.tensor_copy(v_bd[64 * s:64 * s + 64, 4:8, :, s, :].rearrange("p b j d -> p (b j) d"),
                                    bank[7][64 * s:64 * s + 64, :].rearrange("p (j d) -> p j d", d=HD)
                                    ).then_inc(v1_ready.sem, 1)
                for u in range(2):
                    for r in range(4):
                        dve.wait_ge(score_done[u].sem, score_done[u].of(c, r + 1))
                        dve.wait_ge(bias_masked[u].sem, bias_masked[u].of(c, r + 1))
                        dve.tensor_tensor(sc[u][:, r].rearrange("p a h k -> p (a h k)"), bank[r][:],
                                          bias[u][:, r].rearrange("p a h k -> p (a h k)"),
                                          ALU.add).then_inc(biased[u].sem, 1)
                    dve.wait_ge(biased[u].sem, biased[u].of(c, 4))
                    dve.tensor_reduce(sc_max[u][:], sc[u][:].rearrange("p r a h k -> p (r a h) k"), AX.X,
                                      ALU.max).then_inc(max_ready[u].sem, 1)
                for u in range(2):
                    dve.wait_ge(exp_ready[u].sem, exp_ready[u].of(c, 1))
                    vec(dve.tensor_reduce(sc_sum[u][:], sc[u][:].rearrange("p r a h k -> p (r a h) k"), AX.X, ALU.add))
                    dve.reciprocal(sc_inv[u][:], sc_sum[u][:]).then_inc(inv_ready[u].sem, 1)
                for g in range(2):
                    dve.wait_ge(wo_done.sem, wo_done.of(c, g + 1))
                    dve.tensor_tensor(x2[:, 2 * g:2 * g + 2, :], bank[6 + g][:].rearrange("p (n d) -> p n d", d=D),
                                      bo[:].unsqueeze(1).broadcast_to([P, 2, D]), ALU.add).then_inc(x2_ready.sem, 1)
                dve.wait_ge(x2_ready.sem, x2_ready.of(c, 2))
                token_stats(x2)
                normalise(xn2, x2).then_inc(xn2_ready.sem, 1)
                for g in range(2):
                    dve.wait_ge(ff2_done.sem, ff2_done.of(c, g + 1))
                    dve.wait_ge(x2b_ready.sem, x2b_ready.of(c, 1))
                    dve.tensor_tensor(x3[:, 2 * g:2 * g + 2, :], bank[6 + g][:].rearrange("p (n d) -> p n d", d=D),
                                      x2b[:, 2 * g:2 * g + 2, :], ALU.add).then_inc(x3_ready.sem, 1)
                v3 = x3[:].rearrange("p n (i a e) -> p n i a e", a=2, e=2)
                v4 = x4[:].rearrange("p n (i a e) -> p n i a e", a=2, e=2)
                cs = cos_t[:, bass.ds(B + c * TT * 2, TT * 2)].rearrange("p (n a) -> p n a", a=2)
                sn = sin_t[:, bass.ds(B + c * TT * 2, TT * 2)].rearrange("p (n a) -> p n a", a=2)
                cs = cs.unsqueeze(2).broadcast_to([P, TT, S, 2])
                sn = sn.unsqueeze(2).broadcast_to([P, TT, S, 2])
                dve.wait_ge(x3_ready.sem, x3_ready.of(c, 2))
                dve.tensor_tensor(rot[0][:], v3[:, :, :, :, 0], cs, ALU.mult)
                vec(dve.tensor_tensor(rot[1][:], v3[:, :, :, :, 1], sn, ALU.mult))
                vec(dve.tensor_tensor(v4[:, :, :, :, 0], rot[0][:], rot[1][:], ALU.add))
                dve.wait_ge(odd_ready.sem, odd_ready.of(c, 1))
                token_stats(x4)
                normalise(xn3, x4).then_inc(xn3_ready.sem, 1)
                dve.wait_ge(h0_ready.sem, h0_ready.of(c, 2))
                for k in range(KD):
                    for b in range(CB):
                        ins = dve.bn_stats(stats[:, k * CB + b, :], h0[:, k, S * b:S * b + S])
                vec(ins)
                dve.nop(nofuse=True)
                for i in range(KD * CB):
                    ins = dve.bn_aggr(mv[:, i, :], stats[:, i, :])
                vec(ins)
                rsqrt(KD * CB, 1e-8)
                vec(dve.tensor_tensor(in_a[:].rearrange("p (k b) -> p k b", k=KD),
                                      rstd[:].rearrange("p (k b) -> p k b", k=KD),
                                      gamma3[:, :, bass.ds(c * CB, CB)], ALU.mult))
                vec(dve.tensor_tensor(in_b[:], in_a[:], mv[:, :, 0], ALU.mult))
                vec(dve.tensor_tensor(in_b[:].rearrange("p (k b) -> p k b", k=KD),
                                      sty[:, KD:2 * KD, bass.ds(c * CB, CB)],
                                      in_b[:].rearrange("p (k b) -> p k b", k=KD), ALU.subtract))
                dve.wait_ge(h3_kept.sem, h3_kept.of(c, 0))
                for k in range(KD):
                    for b in range(CB):
                        i = k * CB + b
                        ins = dve.tensor_scalar(h3[:, k, S * b:S * b + S], h0[:, k, S * b:S * b + S],
                                                in_a[:, i:i + 1], in_b[:, i:i + 1], ALU.mult, ALU.add)
                ins.then_inc(h3_ready.sem, 1)
                ie = iota_e[:].unsqueeze(1).broadcast_to([P, TT, E])

                def wide(x):
                    return x[:].unsqueeze(2).broadcast_to([P, TT, E])

                def largest(top, hot, values):
                    vec(dve.tensor_reduce(top[:], values[:], AX.X, ALU.max))
                    vec(dve.tensor_tensor(cand[:], values[:], wide(top), ALU.is_equal))
                    vec(dve.scalar_tensor_tensor(cand[:], cand[:], -100.0, ie, ALU.mult, ALU.add))
                    vec(dve.tensor_reduce(first[:], cand[:], AX.X, ALU.min))
                    vec(dve.tensor_tensor(hot[:], cand[:], wide(first), ALU.is_equal))

                dve.wait_ge(logit_done.sem, logit_done.of(c, 1))
                vec(dve.tensor_copy(logit[:], bank[6][:, 0:TT * E].rearrange("p (n e) -> p n e", e=E)))
                largest(top1, hot1, logit)
                vec(dve.scalar_tensor_tensor(logit2[:], hot1[:], MASKED, logit[:], ALU.mult, ALU.add))
                largest(top2, hot2, logit2)
                dve.tensor_tensor(gap[:], top2[:], top1[:], ALU.subtract).then_inc(gap_ready.sem, 1)
                dve.wait_ge(gap_exp.sem, gap_exp.of(c, 1))
                vec(dve.tensor_scalar(gate_d[:], gap_e[:], 1.0, None, ALU.add))
                vec(dve.reciprocal(gate1[:], gate_d[:]))
                vec(dve.tensor_tensor(gate2[:], gap_e[:], gate1[:], ALU.mult))
                dve.tensor_tensor(hot1[:], hot1[:], wide(gate1), ALU.mult)
                vec(dve.tensor_tensor(hot2[:], hot2[:], wide(gate2), ALU.mult))
                vec(dve.tensor_tensor(gate[:], hot1[:], hot2[:], ALU.add))
                dve.tensor_copy(gate_all[:, bass.ds(c * TT, TT), :], gate[:]).then_inc(gate_ready.sem, 1)
                dve.wait_ge(gate_turned.sem, gate_turned.of(c, 1))
                dve.tensor_copy(gate_f[:], bank[7][0:E, :]).then_inc(gate_f_ready.sem, 1)
                for g in range(2):
                    dve.wait_ge(b2_done.sem, b2_done.of(c, g + 1))
                    dve.tensor_tensor(acc[:, bass.ds(c * TT + 2 * g, 2), :],
                                      bank[6 + g][:].rearrange("p (n d) -> p n d", d=D),
                                      x4[:, 2 * g:2 * g + 2, :], ALU.add).then_inc(acc_ready.sem, 1)
                assert n[0] == VEC_STEPS, n[0]
            dve.wait_ge(acc_ready.sem, acc_ready.of(NCH, 0))
            with dve.Fori(0, E // 2) as i:
                for j in range(2):
                    for n4 in range(NCH):
                        for g in range(2):
                            at = (j * NCH + n4) * 2 + g + 1
                            dve.wait_ge(m2_done.sem, m2_done.of(i, at))
                            for h in range(2):
                                tile = n4 * TT + 2 * g + h
                                ins = dve.scalar_tensor_tensor(
                                    acc[:, tile, :], bank[4 + g][:, 256 * h:256 * h + 256],
                                    gate_all[:, tile, bass.ds(i * 2 + j, 1)], acc[:, tile, :], ALU.mult, ALU.add)
                            ins.then_inc(m_acc.sem, 1)

        @block.tensor
        def _(pe):
            for free_at_first in (down_done, expert_done, wo_done, m2_done):
                pe.sem_inc(free_at_first.sem, 1)
            pe.wait_ge(early_in, N_EARLY)
            pe.wait_ge(setup, SETUP_DOM)
            pe.matmul(bank[0][0:A, 0:B], dom_emb[:], hot_dom[:], start=True, stop=False)
            pe.matmul(bank[0][0:A, 0:B], exp_b[:], hot_val[:], start=False, stop=True).then_inc(setup_pe, 1)
            pe.wait_ge(cond_in, N_COND)
            pe.wait_ge(setup, SETUP_SUB)
            pe.matmul(bank[1][0:SE, 0:B], subj_emb[:], hot_sub[:], start=True, stop=True).then_inc(setup_pe, 1)
            pe.wait_ge(setup, SETUP_SE)
            pe.matmul(bank[2][0:SH, 0:B], hyp_w1[:], se[:], start=True, stop=True).then_inc(setup_pe, 1)
            pe.wait_ge(setup, SETUP_SE + 1)
            pe.matmul(bank[3][0:SH, 0:B], hyp_w2[:], hyp1[:], start=True, stop=True).then_inc(setup_pe, 1)
            pe.wait_ge(setup, SETUP_SE + 2)
            pe.matmul(bank[4][0:SH // 2, 0:B], sty_w1[:], hyp2[:], start=True, stop=True).then_inc(setup_pe, 1)
            pe.wait_ge(setup, SETUP_SE + 3)
            for m in range(2 * KD):
                mm = pe.matmul(bank[5][:, B * m:B * m + B], sty_w2[:, P * m:P * m + P], sty1[:], start=True, stop=True)
            mm.then_inc(setup_pe, 1)
            pe.wait_ge(setup_act, 4)
            for m in range(2 * KD):
                for k in range(KD):
                    mm = pe.matmul(bank[6][:, B * m:B * m + B], w_ada[:, k, P * m:P * m + P], emb[:, k, :],
                                   start=(k == 0), stop=(k == KD - 1))
            mm.then_inc(setup_pe, 1)
            pe.wait_ge(main_in, N_MAIN)
            pe.wait_ge(cond_ready, 1)
            pe.wait_ge(zeroed, 2)

            with pe.Fori(0, NCH) as c:
                def turn(z, k, done):
                    for i in range(TT):
                        mm = pe.transpose(bank[4 + k][:, P * i:P * i + P], z[:, i, P * k:P * k + P], ident[:])
                    mm.then_inc(done.sem, 1)

                pe.wait_ge(x_f_in.sem, x_f_in.of(c, 16))
                pe.wait_ge(h0_ready.sem, h0_ready.of(c, 0))
                for k in range(KD):
                    mm = pe.matmul(bank[4][0:A, :], down_w[:, k, :], x_f[:, k, :], start=(k == 0), stop=(k == KD - 1))
                mm.then_inc(down_done.sem, 1)
                pe.wait_ge(hid_ready.sem, hid_ready.of(c, 1))
                pe.wait_ge(w_sel_ready.sem, w_sel_ready.of(c, 1))
                pe.nop(nofuse=True)
                for b in range(CB):
                    mm = pe.matmul(bank[5][0:A, S * b:S * b + S], w_sel[:, b, :], hid[:, S * b:S * b + S],
                                   start=True, stop=True)
                mm.then_inc(expert_done.sem, 1)
                pe.wait_ge(hid2_ready.sem, hid2_ready.of(c, 1))
                pe.wait_ge(acc_ready.sem, acc_ready.of(c, 0))
                for i in range(TT):
                    mm = pe.matmul(bank[6 + i // 2][:, D * (i % 2):D * (i % 2) + D], hid2[:, P * i:P * i + P], up_w[:],
                                   start=True, stop=True)
                    if i % 2:
                        mm.then_inc(up_done.sem, 1)
                pe.wait_ge(xn1_ready.sem, xn1_ready.of(c, 1))
                for k in range(KD):
                    turn(xn1, k, turn1_done)
                pe.wait_ge(x1_ready.sem, x1_ready.of(c, 2))
                pe.wait_ge(ff_ready.sem, ff_ready.of(c, 0))
                for base, w, done in ((0, wq, q_done), (2, wk, k_done)):
                    for m in range(KD):
                        for k in range(KD):
                            mm = pe.matmul(bank[base + m][:], w[:, k, P * m:P * m + P], x1[:, k, :],
                                           start=(k == 0), stop=(k == KD - 1))
                        mm.then_inc(done.sem, 1)
                pe.wait_ge(y_ready.sem, y_ready.of(c, 2))
                for b in range(CB):
                    for s in range(2):
                        for k in range(KD):
                            mm = pe.matmul(bank[6 + b // 4][64 * s:64 * s + 64, P * (b % 4):P * (b % 4) + P],
                                           x1[:, k, S * b:S * b + S], wv[:, k, P * s:P * s + P],
                                           start=(k == 0), stop=(k == KD - 1))
                    if b % 4 == 3:
                        mm.then_inc(v_done.sem, 1)
                pe.wait_ge(q_ready.sem, q_ready.of(c, 2))
                pe.wait_ge(k0_ready.sem, k0_ready.of(c, 1))
                pe.wait_ge(k1_ready.sem, k1_ready.of(c, 1))
                for u in range(2):
                    for r in range(4):
                        if u == 1:
                            pe.wait_ge(biased[0].sem, biased[0].of(c, r + 1))
                        for a in range(2):
                            for b2 in range(2):
                                b = 4 * u + 2 * a + b2
                                for h in range(2):
                                    at = a * 256 + h * P
                                    mm = pe.matmul(
                                        bank[r][64 * b2:64 * b2 + 64, at:at + P].rearrange("q (s k) -> q s k", s=2),
                                        q_f[32 * r:32 * r + 32, h, S * b:S * b + S],
                                        k_f[32 * r:32 * r + 32, h, :, S * b:S * b + S], start=True, stop=True)
                        mm.then_inc(score_done[u].sem, 1)
                for u in range(2):
                    pe.wait_ge(prob_ready[u].sem, prob_ready[u].of(c, 1))
                    for r in range(4):
                        if r >= 2:
                            pe.wait_ge(p_f_ready[u].sem, p_f_ready[u].of(c, r - 1))
                        elif u == 1:
                            pe.wait_ge(p_f_ready[0].sem, p_f_ready[0].of(c, 3 + r))
                        else:
                            pe.wait_ge(ada_scaled.sem, ada_scaled.of(c, 2))
                        for i in range(4):
                            a, h = i // 2, i % 2
                            mm = pe.transpose(bank[4 + r % 2][:, P * i:P * i + P],
                                              sc[u][:, r, a, 2 * h:2 * h + 2, :].rearrange("p s k -> p (s k)"), ident[:])
                        mm.then_inc(prob_turned[u].sem, 1)
                    if u == 0:
                        pe.wait_ge(v0_ready.sem, v0_ready.of(c, 2))
                        pe.wait_ge(v1_ready.sem, v1_ready.of(c, 2))
                    for r in range(4):
                        pe.wait_ge(p_f_ready[u].sem, p_f_ready[u].of(c, r + 1))
                        for a in range(2):
                            for b2 in range(2):
                                for h in range(2):
                                    at = h * 256 + a * P + b2 * S
                                    mm = pe.matmul(bank[6 + u][32 * r:32 * r + 32, at:at + S],
                                                   v_bd[:, 4 * u + 2 * a + b2, 4 * h + r].rearrange("p s d -> p (s d)"),
                                                   p_f[u][:, r, a, h, S * b2:S * b2 + S], start=True, stop=True)
                    mm.then_inc(ctx_done[u].sem, 1)
                for g in range(2):
                    pe.wait_ge(ctx_ready[g].sem, ctx_ready[g].of(c, 2))
                    if g == 0:
                        pe.wait_ge(ctx_ready[1].sem, ctx_ready[1].of(c, 2))
                    for i in range(2):
                        at = P * (2 * g + i)
                        for k in range(KD):
                            pe.matmul(bank[6 + g][:, D * i:D * i + D], ctx_f[:, k, at:at + P], wo[:, k, :],
                                      start=(k == 0), stop=False, skip_group_check=True)
                        for k in range(KD):
                            mm = pe.matmul(bank[6 + g][:, D * i + P * k:D * i + P * k + P], x1[:, k, at:at + P], ident[:],
                                           start=False, stop=True, skip_group_check=True)
                    mm.then_inc(wo_done.sem, 1)
                pe.wait_ge(xn2_ready.sem, xn2_ready.of(c, 1))
                pe.wait_ge(p_f_ready[1].sem, p_f_ready[1].of(c, 4))
                for k in range(KD):
                    turn(xn2, k, turn2_done)
                pe.wait_ge(h_ready.sem, h_ready.of(c, 2))
                for f in range(KF):
                    if f < 4:
                        pe.wait_ge(biased[1].sem, biased[1].of(c, f + 1))
                    else:
                        pe.wait_ge(ff_ready.sem, ff_ready.of(c, f - 3))
                    for k in range(KD):
                        mm = pe.matmul(bank[f % 4][:], w1[:, k, P * f:P * f + P], h_f[:, k, :],
                                       start=(k == 0), stop=(k == KD - 1))
                    mm.then_inc(ff1_done.sem, 1)
                pe.wait_ge(x2_ready.sem, x2_ready.of(c, 2))
                for i in range(TT):
                    for f in range(KF):
                        if i == 0:
                            pe.wait_ge(ff_ready.sem, ff_ready.of(c, f + 1))
                        mm = pe.matmul(bank[6 + i // 2][:, D * (i % 2):D * (i % 2) + D], ff[:, f, P * i:P * i + P],
                                       w2[:, f, :], start=(f == 0), stop=(f == KF - 1))
                    if i % 2:
                        mm.then_inc(ff2_done.sem, 1)
                pe.wait_ge(xn3_ready.sem, xn3_ready.of(c, 1))
                pe.wait_ge(h_ready.sem, h_ready.of(c, 2))
                for k in range(KD):
                    turn(xn3, k, turn3_done)
                pe.wait_ge(h3_ready.sem, h3_ready.of(c, 1))
                pe.wait_ge(x3_ready.sem, x3_ready.of(c, 2))
                for i in range(TT):
                    for k in range(KD):
                        mm = pe.matmul(bank[6][:, E * i:E * i + E], h3[:, k, P * i:P * i + P], router[:, k, :],
                                       start=(k == 0), stop=(k == KD - 1))
                mm.then_inc(logit_done.sem, 1)
                pe.wait_ge(gate_ready.sem, gate_ready.of(c, 1))
                for i in range(TT):
                    mm = pe.transpose(bank[7][0:E, P * i:P * i + P], gate[:, i, :], ident[:])
                mm.then_inc(gate_turned.sem, 1)
                pe.wait_ge(gate_f_ready.sem, gate_f_ready.of(c, 1))
                for i in range(TT):
                    mm = pe.matmul(bank[6 + i // 2][:, D * (i % 2):D * (i % 2) + D], gate_f[:, P * i:P * i + P], moe_b2[:],
                                   start=True, stop=True)
                    if i % 2:
                        mm.then_inc(b2_done.sem, 1)
            pe.wait_ge(h3_kept.sem, h3_kept.of(NCH, 0))
            pe.wait_ge(ff_ready.sem, ff_ready.of(NCH, 0))
            pe.wait_ge(h0_ready.sem, h0_ready.of(NCH, 0))
            with pe.Fori(0, E // 2) as i:
                for j in range(2):
                    pe.wait_ge(moe_in[j], i * 32 + 32)
                    for n4 in range(NCH):
                        for f in range(KF):
                            at = (j * NCH + n4) * KF + f
                            if at >= 4:
                                pe.wait_ge(mh_ready.sem, mh_ready.of(i, at - 3))
                            else:
                                pe.wait_ge(mh_ready.sem, mh_ready.of(i, 0))
                            for k in range(KD):
                                mm = pe.matmul(bank[f % 4][:], moe_w1[j][:, k, P * f:P * f + P],
                                               h3_all[:, k, CT * n4:CT * n4 + CT], start=(k == 0), stop=(k == KD - 1))
                            mm.then_inc(m1_done.sem, 1)
                        for g in range(2):
                            at = (j * NCH + n4) * 2 + g
                            if at >= 2:
                                pe.wait_ge(m_acc.sem, m_acc.of(i, at - 1))
                            else:
                                pe.wait_ge(m_acc.sem, m_acc.of(i, 0))
                            for h in range(2):
                                for f in range(KF):
                                    if g == 0 and h == 0:
                                        pe.wait_ge(mh_ready.sem, mh_ready.of(i, (j * NCH + n4) * KF + f + 1))
                                    tok = P * (2 * g + h)
                                    mm = pe.matmul(bank[4 + g][:, D * h:D * h + D], moe_h[:, f, tok:tok + P],
                                                   moe_w2[j][:, f, :], start=(f == 0), stop=(f == KF - 1))
                            mm.then_inc(m2_done.sem, 1)


SETUP_DOM = 6
SETUP_ANGLES = SETUP_DOM + 18
SETUP_SUB = SETUP_ANGLES + 3
SETUP_SE = SETUP_SUB + 4
SETUP_ABS = SETUP_SE + 8


def kernel(**inputs):
    import concourse.bacc as bacc
    from concourse.bass_utils import run_bass_kernel_spmd as run

    a = {k: np.ascontiguousarray(v) for k, v in inputs.items()}
    c_ = np.ascontiguousarray

    def cols(v):
        return c_(v.reshape(-1, P).T)

    def row(v):
        return v.reshape(1, -1)

    x = a["x"].reshape(N, D)
    bias = a["fside_Bx16xSxS_0"].reshape(B // 4, 2, 2, 2, 4, 2, S, S)
    bias = bias.transpose(0, 2, 6, 4, 1, 3, 5, 7).reshape(B // 4, P, 2048)
    mask = a["mask_Bx1xSxS_bk0"].reshape(NT, 2, S, S).transpose(1, 2, 0, 3).reshape(P, NT, S)
    wv = a["L1_cond_Wv"].reshape(D, H // 2, 2, HD).transpose(0, 2, 1, 3).reshape(D, D)
    th = np.stack([a["condB_theta"], a["condB_phi"]], -1).reshape(NT, 2, 2).transpose(1, 0, 2).reshape(2, 1, 2 * NT)
    angles = np.concatenate([np.zeros((P, B), np.float32), np.broadcast_to(th, (2, S, 2 * NT)).reshape(P, 2 * NT)], 1)
    half = D // 2
    freqs = np.exp(np.arange(half, dtype=np.float32) * np.float32(-np.log(10000.0) / (half - 1)))
    lane = np.arange(P)
    laid = {
        "x_f": x.T, "x_t": x, "bias": bias, "mask": mask, "angles": angles,
        "ident": np.eye(P, dtype=np.float32), "iota_p": lane.astype(np.float32).reshape(P, 1),
        "iota_e": np.arange(E, dtype=np.float32).reshape(1, E),
        "parity": ((lane[:, None] // HD) % 2 == np.arange(2)[None, :]).astype(np.float32),
        "freqs": freqs.astype(np.float32).reshape(P, 1),
        "dom_i": row(a["itok_B_0_15"]), "time_i": row(a["itok_B_34_63"]), "sub_i": row(a["itok_B_6_14"]),
        "down_w": a["L0_cond_down_W"].T, "down_b": a["L0_cond_down_b"].reshape(A, 1),
        "up_w": np.concatenate([a["L0_cond_up_W"].T, row(a["L0_cond_up_b"])], 0),
        "exp_w": a["L0_cond_expert_W"].transpose(0, 2, 1), "exp_b": a["L0_cond_expert_b"],
        "dom_emb": a["L0_cond_domain_emb"], "gamma0": row(a["L0_cond_ln_gamma"]), "beta0": row(a["L0_cond_ln_beta"]),
        "w_ada": a["L1_cond_W_ada"], "b_ada": cols(a["L1_cond_b_ada"]),
        "wq": a["L1_cond_Wq"], "wk": a["L1_cond_Wk"], "wv": wv, "wo": a["L1_cond_Wo"],
        "bq": cols(a["L1_cond_bq"]), "bk": cols(a["L1_cond_bk"]), "bv": cols(a["L1_cond_bv"]), "bo": row(a["L1_cond_bo"]),
        "w1": a["L1_cond_W1"], "b1": cols(a["L1_cond_b1"]), "w2": a["L1_cond_W2"], "b2": row(a["L1_cond_b2"]),
        "g2": cols(a["L1_cond_g2"]), "beta2": cols(a["L1_cond_beta2"]),
        "ln_g": cols(a["L3_cond_ln_g"]), "ln_b": cols(a["L3_cond_ln_b"]), "subj_emb": a["L3_cond_subj_emb"],
        "hyp_w1": a["L3_cond_hyp_w1"], "hyp_b1": a["L3_cond_hyp_b1"].reshape(-1, 1),
        "hyp_w2": a["L3_cond_hyp_w2"], "hyp_b2": a["L3_cond_hyp_b2"].reshape(-1, 1),
        "sty_w1": a["L3_cond_sty_w1"], "sty_b1": a["L3_cond_sty_b1"].reshape(-1, 1),
        "sty_w2": a["L3_cond_sty_w2"], "sty_b2": cols(a["L3_cond_sty_b2"]), "router": a["L3_cond_router_w"],
        "moe_w1": a["L3_cond_exp_w1"], "moe_w2": a["L3_cond_exp_w2"],
        "moe_b1": a["L3_cond_exp_b1"].reshape(E, KF, P).transpose(2, 0, 1), "moe_b2": a["L3_cond_exp_b2"],
    }
    nc = bacc.Bacc("TRN2", target_bir_lowering=False, num_devices=1)
    arrays, tensors = {}, {}
    for name, v in laid.items():
        arrays[f"in_{name}"] = c_(v)
        tensors[name] = nc.dram_tensor(f"in_{name}", v.shape, mybir.dt.from_np(v.dtype), kind="ExternalInput").ap()
    out = nc.dram_tensor("out_x", (N, D), F32, kind="ExternalOutput").ap()
    build(nc, tensors, out)
    r = run(nc, [arrays], core_ids=[0])
    return r.results[0]["out_x"].reshape(B, S, D)
```

```python
from contextlib import ExitStack

import numpy as np

import concourse.bass as bass
import concourse.mybir as mybir

F32 = mybir.dt.float32
I32 = mybir.dt.int32
U8 = mybir.dt.uint8
U32 = mybir.dt.uint32
F16 = mybir.dt.float16
ALU = mybir.AluOpType
ACT = mybir.ActivationFunctionType
AX = mybir.AxisListType

P = 128
B, S, D = 32, 64, 256
N = B * S
A = 64
NDOM = 16
H, HD = 16, 16
FF = 1024
E = 8
NSUB, SE, SH = 32, 64, 128
CT = 512
NCH = N // CT
CB = CT // S
TT = CT // P
NT = N // P
KD = D // P
KF = FF // P
HALF_PI = float(np.pi / 2)
INV_2PI = float(1.0 / (2 * np.pi))
ROUND = 12582912.0
TWO_PI_PARTS = (6.28125, 0.0019350051879882812, 3.0199159819460083e-07)
MASKED = -1.0e30
W_SCALE = 256.0
CAP = N + P
ROW = D + 4
TILES = (2 * N + E * (P - 1)) // P
NO_TOKEN = 1 << 24
WE = 8192
RSQRT_SEED = 1597463007.0


class Count:

    def __init__(self, sem, per, start):
        self.sem, self.per, self.start = sem, per, start

    def of(self, c, n):
        return c * self.per + n + self.start


def build(nc, t, out):
    with ExitStack() as ctx:
        def sb(name, shape, dt=F32):
            return ctx.enter_context(nc.sbuf_tensor(name, shape, dt))

        def sem(name):
            return ctx.enter_context(nc.semaphore(name))

        def count(name, per):
            return Count(sem(name), per, 0)

        def free(name, per):
            return Count(sem(name), per, 1)

        bank = [ctx.enter_context(nc.psum_tensor(f"bank{i}", [P, 512], F32)) for i in range(8)]

        w_moe = sb("w_moe", [P, E * WE], F16)
        arena = w_moe[:].bitcast(F32)
        used = [0]

        def carve(*shape):
            n = int(np.prod(shape[1:]))
            ap = arena[0:shape[0], used[0]:used[0] + n]
            used[0] += n
            assert used[0] <= E * WE // 2, used
            names = "abcdef"[:len(shape) - 1]
            sizes = dict(zip(names, shape[1:]))
            return ap.rearrange(f"p ({' '.join(names)}) -> p {' '.join(names)}", **sizes)

        w_all = carve(A, B, A)
        w1 = carve(P, KD, FF)
        assert used[0] == WE // 2

        ident = sb("ident", [P, P])
        iota_p = sb("iota_p", [P, 1])
        iota_e = sb("iota_e", [P, E])
        parity = sb("parity", [P, 2])
        freqs = sb("freqs", [P, 1])
        down_w = sb("down_w", [P, KD, A])
        down_b = sb("down_b", [A, 1])
        up_w = carve(A + 1, D)
        dom_emb = sb("dom_emb", [NDOM, A])
        exp_b = sb("exp_b", [NDOM, A])
        gamma0 = carve(P, D)
        beta0 = carve(P, D)
        w_ada = sb("w_ada", [P, KD, 2 * D])
        b_ada = sb("b_ada", [P, 2 * KD])
        wq = carve(P, KD, D)
        wk = carve(P, KD, D)
        wv = carve(P, KD, D)
        wo = carve(P, KD, D)
        bq = sb("bq", [P, KD])
        bk = sb("bk", [P, KD])
        bv = sb("bv", [P, KD])
        bo = carve(P, D)
        b1 = sb("b1", [P, KF])
        w2 = sb("w2", [P, KF, D])
        b2 = sb("b2", [P, D])
        g2 = sb("g2", [P, KD])
        beta2 = sb("beta2", [P, KD])
        ln_g = sb("ln_g", [P, KD])
        ln_b = sb("ln_b", [P, KD])
        subj_emb = sb("subj_emb", [NSUB, SE])
        hyp_w1 = sb("hyp_w1", [SE, SH])
        hyp_b1 = sb("hyp_b1", [SH, 1])
        hyp_w2 = sb("hyp_w2", [SH, SH])
        hyp_b2 = sb("hyp_b2", [SH, 1])
        sty_w1 = sb("sty_w1", [SH, SH // 2])
        sty_b1 = sb("sty_b1", [SH // 2, 1])
        sty_w2 = sb("sty_w2", [SH // 2, 2 * D])
        sty_b2 = sb("sty_b2", [P, 2 * KD])
        router = sb("router", [P, KD, E])
        moe_b1 = sb("moe_b1", [P, E, KF])
        moe_b2 = sb("moe_b2", [E, D])
        mask_u8 = sb("mask_u8", [P, NT, S], U8)
        mask_add = sb("mask_add", [P, NT, S])

        dom_i = sb("dom_i", [P, B], I32)
        dom_f = sb("dom_f", [P, B])
        dom_c = sb("dom_c", [P, B])
        dom_at = sb("dom_at", [1, B], I32)
        valid = sb("valid", [P, B])
        invalid = sb("invalid", [P, B])
        hot_dom = sb("hot_dom", [NDOM, B])
        hot_val = sb("hot_val", [NDOM, B])
        add_o = sb("add_o", [A, B])
        sub_i = sb("sub_i", [P, B], I32)
        sub_f = sb("sub_f", [P, B])
        hot_sub = sb("hot_sub", [NSUB, B])
        se = sb("se", [SE, B])
        hyp1 = sb("hyp1", [SH, B])
        hyp2 = sb("hyp2", [SH, B])
        sty1 = sb("sty1", [SH // 2, B])
        sty = sb("sty", [P, 2 * KD, B])
        soft = sb("soft", [P, 4, KD, B])
        gamma3 = sb("gamma3", [P, KD, B])
        time_i = sb("time_i", [P, B], I32)
        time_f = sb("time_f", [P, B])
        quot, q_hi, q_lo = sb("quot", [P, B]), sb("q_hi", [P, B]), sb("q_lo", [P, B])
        angle = sb("angle", [P, B + 2 * NT])
        turns = sb("turns", [P, B + 2 * NT])
        cos_in = sb("cos_in", [P, B + 2 * NT])
        sin_t = sb("sin_t", [P, B + 2 * NT])
        cos_t = sb("cos_t", [P, B + 2 * NT])
        emb = sb("emb", [P, KD, B])
        ada = sb("ada", [P, 2 * KD, B])
        bq4 = sb("bq4", [P, KD])
        bkp = sb("bkp", [P, 2])

        x_f = carve(P, KD, CT)
        x_t = carve(P, TT, D)
        w_sel = carve(A, CB, A)
        w_id = carve(A, CB, A)
        hid = carve(A, CT)
        hid2 = carve(A + 1, CT)
        y = carve(P, TT, D)
        xn1 = y
        x1 = carve(P, KD, CT)
        q_f = carve(P, KD, CT)
        k_f = carve(P, KD, 2, CT)
        v_bd = carve(P, CB, H // 2, 2, HD)
        bias = [carve(P, 4, 2, 4, S) for u in range(2)]
        sc_both = carve(P, 2 * 2048)
        sc = [sc_both[:, 2048 * u:2048 * u + 2048].rearrange("p (r a h k) -> p r a h k", r=4, a=2, h=4)
              for u in range(2)]
        sc_max = [sb(f"sc_max{u}", [P, 32]) for u in range(2)]
        sc_sum = [sb(f"sc_sum{u}", [P, 32]) for u in range(2)]
        sc_inv = [sb(f"sc_inv{u}", [P, 32]) for u in range(2)]
        p_f = [carve(P, 4, 2, 2, P) for u in range(2)]
        ctx_f = carve(P, KD, CT)
        ada_t = ctx_f
        x2 = carve(P, TT, D)
        x2b = k_f[:, 0].rearrange("p s (i d) -> p (s i) d", d=D)
        xn2 = y
        h_f = q_f
        ff = sc_both[:].rearrange("p (f n) -> p f n", f=KF)
        x3 = x2
        rot = [p_f[1][:, i].rearrange("p a h (x e) -> p (a h) x e", e=2) for i in range(4)]
        x4 = q_f[:].rearrange("p k (i d) -> p (k i) d", d=D)
        xn3 = y
        h0 = ctx_f
        h3 = sb("h3", [P, KD, CT])
        stats = sb("stats", [P, 16, 6])
        mv = sb("mv", [P, 16, 2])
        var = sb("var", [P, 16])
        rstd = sb("rstd", [P, 16])
        newton = sb("newton", [P, 16])
        newton2 = sb("newton2", [P, 16])
        in_a = sb("in_a", [P, 16])
        in_b = sb("in_b", [P, 16])
        logit = sb("logit", [P, TT, E])
        logit2 = sb("logit2", [P, TT, E])
        cand = sb("cand", [P, TT, E])
        hot1 = sb("hot1", [P, TT, E])
        hot2 = sb("hot2", [P, TT, E])
        top1 = sb("top1", [P, TT])
        top2 = sb("top2", [P, TT])
        first = sb("first", [P, TT])
        gap = sb("gap", [P, TT])
        gap_e = sb("gap_e", [P, TT])
        gate_d = sb("gate_d", [P, TT])
        gate1 = sb("gate1", [P, TT])
        gate2 = sb("gate2", [P, TT])
        gate = sb("gate", [P, TT, E])
        gate_f = sb("gate_f", [E, CT])
        x4b = x2

        lower = sb("lower", [P, P])
        ones = sb("ones", [P, P])
        iota_t = sb("iota_t", [P, TILES + 2])
        tile_m = sb("tile_m", [P, NT])
        region = sb("region", [P, E])
        tok_id = sb("tok_id", [P, NT], I32)
        first1 = first
        first2 = sb("first2", [P, TT])
        picks = sb("picks", [P, TT, E])
        total = sb("total", [P, TT, E])
        before = sb("before", [P, TT + 1, E])
        seen = sb("seen", [P, E])
        place = sb("place", [P, TT, E])
        picked = sb("picked", [P, 2, TT, E])
        slot_f = sb("slot_f", [P, 2, TT])
        slot = sb("slot", [P, 2, TT], U32)
        disp = sb("disp", [P, TT, ROW])
        empty = sb("empty", [P, ROW])
        stage = sb("stage", [P, WE // 4])
        split = sb("split", [P, 2, WE // 4], F16)
        over = sb("over", [P, E, NT])
        n_tiles = sb("n_tiles", [P, E])
        ends = sb("ends", [P, E])
        past = sb("past", [P, TILES + 2, E])
        past_n = sb("past_n", [P, TILES + 2, E])
        tile_e = sb("tile_e", [P, TILES + 2])
        tile_s = sb("tile_s", [P, TILES + 2])
        tile_l = sb("tile_l", [P, TILES + 2])
        tile_r = sb("tile_r", [P, TILES + 2])
        tile_ei = sb("tile_ei", [1, TILES + 2], I32)
        tile_ri = sb("tile_ri", [1, TILES + 2], I32)
        rest_i = sb("rest_i", [1, E], I32)
        xs = [sb(f"xs{j}", [P, ROW]) for j in range(2)]
        xs_f = [sb(f"xs_f{j}", [P, 4, P], F16) for j in range(2)]
        ident16 = sb("ident16", [P, P], F16)
        meta = sb("meta", [P, TILES + 2, 4])
        gates = sb("gates", [P, TILES + 2])
        h32 = [stage[:, j * KF * P:(j + 1) * KF * P].rearrange("p (f n) -> p f n", f=KF) for j in range(2)]
        h_hi = [split[:, 0, j * KF * P:(j + 1) * KF * P].rearrange("p (f n) -> p f n", f=KF) for j in range(2)]
        h_lo = [split[:, 1, j * KF * P:(j + 1) * KF * P].rearrange("p (f n) -> p f n", f=KF) for j in range(2)]
        ys = [sb(f"ys{j}", [P, D]) for j in range(2)]
        ids = [sb(f"ids{j}", [P, 1], U32) for j in range(2)]
        xs_dram = nc.dram_tensor("dispatched", (E * CAP + P, ROW), F32).ap()
        w_dram = nc.dram_tensor("w_split", (E, P, WE), F16).ap()

        early_in, cond_in, main_in = sem("early_in"), sem("cond_in"), sem("main_in")
        setup = sem("setup")
        setup_pe, setup_act = sem("setup_pe"), sem("setup_act")
        zeroed = sem("zeroed")
        dom_ready, w_in = sem("dom_ready"), sem("w_in")
        cond_ready = sem("cond_ready")
        mask_ready = sem("mask_ready")

        x_f_in, x_t_in = count("x_f_in", 16), count("x_t_in", 16)
        bias_in = [count(f"bias_in{u}", 16) for u in range(2)]
        w_sel_ready = count("w_sel_ready", 1)
        w_step = count("w_step", 2)
        down_done, hid_ready = free("down_done", 1), count("hid_ready", 1)
        expert_done, hid2_ready = free("expert_done", 1), count("hid2_ready", 1)
        up_done, y_ready = count("up_done", 2), free("y_ready", 2)
        xn1_ready, turn1_done = count("xn1_ready", 1), count("turn1_done", 2)
        ada_scaled, x1_ready = count("ada_scaled", 2), count("x1_ready", 2)
        q_done, q_ready = count("q_done", 2), count("q_ready", 2)
        k_done, k0_ready, k1_ready = count("k_done", 2), count("k0_ready", 1), count("k1_ready", 1)
        v_done, v0_ready, v1_ready = count("v_done", 2), count("v0_ready", 2), count("v1_ready", 2)
        bias_masked = [count(f"bias_masked{u}", 4) for u in range(2)]
        score_done = [count(f"score_done{u}", 4) for u in range(2)]
        biased = [free(f"biased{u}", 4) for u in range(2)]
        max_ready = [count(f"max_ready{u}", 1) for u in range(2)]
        shifted = [count(f"shifted{u}", 1) for u in range(2)]
        exp_ready = [count(f"exp_ready{u}", 1) for u in range(2)]
        inv_ready = [count(f"inv_ready{u}", 1) for u in range(2)]
        prob_ready = [count(f"prob_ready{u}", 1) for u in range(2)]
        prob_turned = [count(f"prob_turned{u}", 4) for u in range(2)]
        p_f_ready = [count(f"p_f_ready{u}", 4) for u in range(2)]
        ctx_done = [count(f"ctx_done{u}", 1) for u in range(2)]
        ctx_ready = [count(f"ctx_ready{u}", 2) for u in range(2)]
        wo_done, x2_ready = free("wo_done", 2), count("x2_ready", 2)
        x2b_ready = count("x2b_ready", 1)
        xn2_ready, turn2_done, h_ready = count("xn2_ready", 1), count("turn2_done", 2), count("h_ready", 2)
        ff1_done, ff_ready = count("ff1_done", KF), free("ff_ready", KF)
        ff2_done, x3_ready = count("ff2_done", 2), free("x3_ready", 2)
        rot_step, odd_ready = count("rot_step", 2), count("odd_ready", 1)
        xn3_ready, turn3_done, h0_ready = count("xn3_ready", 1), count("turn3_done", 2), free("h0_ready", 2)
        h3_ready = count("h3_ready", 1)
        logit_done, gap_ready, gap_exp = count("logit_done", 1), count("gap_ready", 1), count("gap_exp", 1)
        gate_ready, gate_turned, gate_f_ready = count("gate_ready", 1), count("gate_turned", 1), count("gate_f_ready", 1)
        b2_done, acc_ready = count("b2_done", 2), free("acc_ready", 2)
        VEC_STEPS = 102
        vec_step = count("vec_step", VEC_STEPS)

        picks_ready, rank_done = count("picks_ready", 1), count("rank_done", 1)
        slot_ready = count("slot_ready", 1)
        rows_done, rows_hi, rows_ready = count("rows_done", 2), count("rows_hi", 2), free("rows_ready", 2)
        disp_ready, xs_out = count("disp_ready", 1), count("xs_out", 16 * 2 * TT)
        x_out, rows_sent, x_stored = count("x_out", 16), free("rows_sent", 1), free("x_stored", 1)
        stage_in, split_hi, split_lo = count("stage_in", 64), count("split_hi", 4), free("split_lo", 4)
        w_out = free("w_out", 64)
        plan, plan_ready, rest_out = sem("plan"), sem("plan_ready"), sem("rest_out")
        weights_in = sem("weights_in")
        xs_in = [sem(f"xs_in{j}") for j in range(2)]
        turned, xs_f_ready = sem("turned"), sem("xs_f_ready")
        gate_step, gates_ready = sem("gate_step"), sem("gates_ready")
        m1_done, h32_ready, hi_ready, lo_ready = sem("m1_done"), sem("h32_ready"), sem("hi_ready"), sem("lo_ready")
        m2_done, ys_ready, ids_ready = sem("m2_done"), sem("ys_ready"), sem("ids_ready")
        rows_out, added = sem("rows_out"), sem("added")

        early = [
            (ident, t["ident"]), (iota_p, t["iota_p"]), (down_w, t["down_w"].rearrange("(k p) a -> p k a", p=P)),
            (down_b, t["down_b"]), (up_w, t["up_w"]), (dom_emb, t["dom_emb"]), (exp_b, t["exp_b"]),
            (gamma0, t["gamma0"].broadcast_to([P, D])), (beta0, t["beta0"].broadcast_to([P, D])),
            (dom_i, t["dom_i"].broadcast_to([P, B])),
        ]
        cond = [
            (freqs, t["freqs"]), (time_i, t["time_i"].broadcast_to([P, B])), (sub_i, t["sub_i"].broadcast_to([P, B])),
            (angle, t["angles"]),
            (w_ada, t["w_ada"].rearrange("(k p) n -> p k n", p=P)), (b_ada, t["b_ada"]),
            (subj_emb, t["subj_emb"]), (hyp_w1, t["hyp_w1"]), (hyp_b1, t["hyp_b1"]), (hyp_w2, t["hyp_w2"]),
            (hyp_b2, t["hyp_b2"]), (sty_w1, t["sty_w1"]), (sty_b1, t["sty_b1"]), (sty_w2, t["sty_w2"]),
            (sty_b2, t["sty_b2"]), (bq, t["bq"]), (bk, t["bk"]), (bv, t["bv"]), (parity, t["parity"]),
            (iota_e, t["iota_e"].broadcast_to([P, E])), (mask_u8, t["mask"]),
            (lower, t["lower"]), (iota_t, t["iota_t"].broadcast_to([P, TILES + 2])),
            (tile_m, t["tile_m"].broadcast_to([P, NT])), (region, t["region"].broadcast_to([P, E])),
            (tok_id, t["tok_id"]),
        ]
        main = [
            (wq, t["wq"].rearrange("(k p) n -> p k n", p=P)), (wk, t["wk"].rearrange("(k p) n -> p k n", p=P)),
            (wv, t["wv"].rearrange("(k p) n -> p k n", p=P)), (wo, t["wo"].rearrange("(k p) n -> p k n", p=P)),
            (bo, t["bo"].broadcast_to([P, D])), (w1, t["w1"].rearrange("(k p) n -> p k n", p=P)), (b1, t["b1"]),
            (w2, t["w2"].rearrange("(k p) n -> p k n", p=P)), (b2, t["b2"].broadcast_to([P, D])),
            (g2, t["g2"]), (beta2, t["beta2"]), (ln_g, t["ln_g"]), (ln_b, t["ln_b"]),
            (router, t["router"].rearrange("(k p) n -> p k n", p=P)), (moe_b1, t["moe_b1"]), (moe_b2, t["moe_b2"]),
        ]
        N_EARLY, N_COND, N_MAIN = 16 * len(early), 16 * len(cond), 16 * len(main)

        block = ctx.enter_context(nc.Block())

        @block.sync
        def _(sp):
            sp.sem_inc(w_out.sem, 1)
            for dst, src in early:
                sp.dma_start(dst[:], src).then_inc(early_in, 16)
            for dst, src in cond:
                sp.dma_start(dst[:], src).then_inc(cond_in, 16)
            sp.wait_ge(dom_ready, 1)
            with sp.Fori(0, B) as b:
                e = sp.value_load(dom_at[0:1, bass.ds(b, 1)], min_val=0, max_val=NDOM - 1)
                sp.dma_start(w_all[:, bass.ds(b, 1), :], t["exp_w"][bass.ds(e, 1), :, :]
                             .rearrange("e a o -> a e o")).then_inc(w_in, 16)
            with sp.Fori(0, NCH) as c:
                sp.wait_ge(down_done.sem, down_done.of(c, 0))
                sp.dma_start(x_f[:], t["x_f"].rearrange("(k p) n -> p k n", p=P)[:, :, bass.ds(c * CT, CT)]
                             ).then_inc(x_f_in.sem, 16)
                sp.wait_ge(y_ready.sem, y_ready.of(c, 0))
                sp.dma_start(x_t[:], t["x_t"].rearrange("(n p) d -> p n d", p=P)[:, bass.ds(c * TT, TT), :]
                             ).then_inc(x_t_in.sem, 16)
                for u in range(2):
                    sp.wait_ge(biased[u].sem, biased[u].of(c, 0))
                    sp.dma_start(bias[u][:].rearrange("p r a h k -> p (r a h k)"),
                                 t["bias"][bass.ds(c * 2 + u, 1), :, :].rearrange("s p n -> (s p) n")
                                 ).then_inc(bias_in[u].sem, 16)
                for q in range(4):
                    sp.wait_ge(split_lo.sem, split_lo.of(c, q))
                    w_part = t["moe_w1"] if q % 2 == 0 else t["moe_w2"]
                    sp.dma_start(stage[:].rearrange("p (k n) -> p k n", k=KD if q % 2 == 0 else KF),
                                 w_part[bass.ds(c * 2 + q // 2, 1), :, :].rearrange("e (k p) n -> p (e k) n", p=P)
                                 ).then_inc(stage_in.sem, 16)
                    sp.wait_ge(split_lo.sem, split_lo.of(c, q + 1))
                    sp.dma_start(w_dram[bass.ds(c * 2 + q // 2, 1), :, q % 2 * (WE // 2):(q % 2 + 1) * (WE // 2)]
                                 .rearrange("e p n -> p (e n)"), split[:].rearrange("p h n -> p (h n)")
                                 ).then_inc(w_out.sem, 16)
            sp.wait_ge(w_out.sem, w_out.of(NCH, 0))
            sp.dma_start(w_moe[:, 0:WE], w_dram[0]).then_inc(weights_in, 16)
            sp.wait_ge(plan_ready, 1)
            with sp.Fori(0, E) as e:
                r = sp.value_load(rest_i[0:1, bass.ds(e, 1)], min_val=0, max_val=E * CAP - P)
                sp.dma_start(xs_dram[bass.ds(r, P), :], empty[:]).then_inc(rest_out, 16)
            sp.dma_start(xs_dram[E * CAP:E * CAP + P, :], empty[:]).then_inc(rest_out, 16)
            sp.wait_ge(x_stored.sem, x_stored.of(NCH, 0))
            with sp.Fori(1, E) as e:
                sp.wait_ge(weights_in, e * 16)
                sp.dma_start(w_moe[:, bass.ds(e * WE, WE)], w_dram[bass.ds(e, 1), :, :].rearrange("e p n -> p (e n)")
                             ).then_inc(weights_in, 16)
            sp.wait_ge(weights_in, 16 * E)

        @block.gpsimd
        def _(pool):
            for free_at_first in (rows_sent, x_stored):
                pool.sem_inc(free_at_first.sem, 1)
            for dst, src in main:
                pool.dma_start(dst[:], src).then_inc(main_in, 16)
            pool.wait_ge(cond_in, N_COND)
            pool.tensor_scalar(mask_add[:], mask_u8[:], MASKED, None, ALU.mult).then_inc(mask_ready, 1)
            pool.wait_ge(w_in, 16 * B)
            pool.wait_ge(mask_ready, 1)
            pool.wait_ge(setup, SETUP_DOM)
            pool.wait_ge(cond_ready, 1)
            pool.wait_ge(main_in, N_MAIN)
            with pool.Fori(0, NCH) as c:
                pool.wait_ge(expert_done.sem, expert_done.of(c, 0))
                pool.tensor_tensor(w_sel[:], w_all[:, bass.ds(c * CB, CB), :],
                                   valid[0:A, bass.ds(c * CB, CB)].unsqueeze(2).broadcast_to([A, CB, A]),
                                   ALU.mult).then_inc(w_step.sem, 1)
                pool.tensor_tensor(w_id[:], ident[0:A, 0:A].unsqueeze(1).broadcast_to([A, CB, A]),
                                   invalid[0:A, bass.ds(c * CB, CB)].unsqueeze(2).broadcast_to([A, CB, A]),
                                   ALU.mult).then_inc(w_step.sem, 1)
                pool.wait_ge(w_step.sem, w_step.of(c, 2))
                pool.tensor_tensor(w_sel[:], w_sel[:], w_id[:], ALU.add).then_inc(w_sel_ready.sem, 1)
                for u in range(2):
                    pool.wait_ge(bias_in[u].sem, bias_in[u].of(c, 16))
                    for r in range(4):
                        pool.tensor_tensor(
                            bias[u][:, r], bias[u][:, r],
                            mask_add[:, bass.ds(c * TT + 2 * u, 2), :].unsqueeze(2).broadcast_to([P, 2, 4, S]),
                            ALU.add).then_inc(bias_masked[u].sem, 1)
                for k in range(KD):
                    pool.wait_ge(ada_scaled.sem, ada_scaled.of(c, k + 1))
                    if k == 0:
                        pool.wait_ge(wo_done.sem, wo_done.of(c, 0))
                    pool.tensor_tensor(
                        x1[:, k, :].rearrange("p (b s) -> p b s", s=S),
                        ada_t[:, k, :].rearrange("p (b s) -> p b s", s=S),
                        ada[:, KD + k, bass.ds(c * CB, CB)].unsqueeze(2).broadcast_to([P, CB, S]),
                        ALU.add).then_inc(x1_ready.sem, 1)
                for u in range(2):
                    pool.wait_ge(max_ready[u].sem, max_ready[u].of(c, 1))
                    v = sc[u][:].rearrange("p r a h k -> p (r a h) k")
                    pool.tensor_tensor(v, v, sc_max[u][:].unsqueeze(2).broadcast_to([P, 32, S]),
                                       ALU.subtract).then_inc(shifted[u].sem, 1)
                for u in range(2):
                    pool.wait_ge(inv_ready[u].sem, inv_ready[u].of(c, 1))
                    v = sc[u][:].rearrange("p r a h k -> p (r a h) k")
                    pool.tensor_tensor(v, v, sc_inv[u][:].unsqueeze(2).broadcast_to([P, 32, S]),
                                       ALU.mult).then_inc(prob_ready[u].sem, 1)
                pool.wait_ge(x2_ready.sem, x2_ready.of(c, 2))
                pool.wait_ge(x3_ready.sem, x3_ready.of(c, 0))
                pool.tensor_tensor(x2b[:], x2[:], b2[:].unsqueeze(1).broadcast_to([P, TT, D]),
                                   ALU.add).then_inc(x2b_ready.sem, 1)
                pool.wait_ge(x3_ready.sem, x3_ready.of(c, 2))
                pool.wait_ge(acc_ready.sem, acc_ready.of(c, 0))
                v3 = x3[:].rearrange("p n (i a e) -> p n i a e", a=2, e=2)
                v4 = x4[:].rearrange("p n (i a e) -> p n i a e", a=2, e=2)
                cs = cos_t[:, bass.ds(B + c * TT * 2, TT * 2)].rearrange("p (n a) -> p n a", a=2)
                sn = sin_t[:, bass.ds(B + c * TT * 2, TT * 2)].rearrange("p (n a) -> p n a", a=2)
                cs = cs.unsqueeze(2).broadcast_to([P, TT, S, 2])
                sn = sn.unsqueeze(2).broadcast_to([P, TT, S, 2])
                pool.tensor_tensor(rot[2][:], v3[:, :, :, :, 1], cs, ALU.mult).then_inc(rot_step.sem, 1)
                pool.tensor_tensor(rot[3][:], v3[:, :, :, :, 0], sn, ALU.mult).then_inc(rot_step.sem, 1)
                pool.wait_ge(rot_step.sem, rot_step.of(c, 2))
                pool.tensor_tensor(v4[:, :, :, :, 1], rot[2][:], rot[3][:], ALU.subtract).then_inc(odd_ready.sem, 1)
                pool.wait_ge(slot_ready.sem, slot_ready.of(c, 1))
                pool.wait_ge(disp_ready.sem, disp_ready.of(c, 1))
                pool.nop(nofuse=True)
                for i in range(TT):
                    for a in range(2):
                        pool.indirect_dma_start(
                            out=xs_dram[:, :], out_offset=bass.IndirectOffsetOnAxis(ap=slot[:, a, i:i + 1], axis=0),
                            in_=disp[:, i, :], in_offset=None).then_inc(xs_out.sem, 16)
                pool.wait_ge(acc_ready.sem, acc_ready.of(c, 2))
                pool.dma_start(out.rearrange("(n p) d -> p n d", p=P)[:, bass.ds(c * TT, TT), :], x4b[:]
                               ).then_inc(x_out.sem, 16)
                pool.wait_ge(xs_out.sem, xs_out.of(c, 16 * 2 * TT))
                pool.sem_inc(rows_sent.sem, 1)
                pool.wait_ge(x_out.sem, x_out.of(c, 16))
                pool.sem_inc(x_stored.sem, 1)

            def add_rows(n, j):
                pool.wait_ge(gates_ready, n + 1)
                pool.nop(nofuse=True)
                pool.tensor_copy(ids[j][:], meta[:, bass.ds(n, 1), 0].bitcast(U32)).then_inc(ids_ready, 1)
                pool.wait_ge(ids_ready, n + 1)
                pool.wait_ge(ys_ready, n + 3)
                pool.nop(nofuse=True)
                pool.indirect_dma_start(
                    out=out[:, :], out_offset=bass.IndirectOffsetOnAxis(ap=ids[j][:, 0:1], axis=0),
                    in_=ys[j][:], in_offset=None, bounds_check=N - 1, oob_is_err=False,
                    compute_op=ALU.add).then_inc(rows_out, 16)
                pool.wait_ge(rows_out, n * 16 + 16)
                pool.nop(nofuse=True)
                pool.sem_inc(added, 1)

            pool.sem_inc(added, 2)
            with pool.Fori(0, TILES // 2) as i:
                for j in range(2):
                    add_rows(i * 2 + j, j)
            if TILES % 2:
                add_rows(TILES - 1, 0)

        @block.scalar
        def _(act):
            for free_at_first in (h0_ready, ff_ready):
                act.sem_inc(free_at_first.sem, 1)
            act.wait_ge(setup, SETUP_ANGLES)
            act.activation(sin_t[:], angle[:], ACT.Sin).then_inc(setup_act, 1)
            act.activation(cos_t[:], cos_in[:], ACT.Sin).then_inc(setup_act, 1)
            act.wait_ge(setup_act, 2)
            act.activation(emb[:, 0, :], sin_t[:, 0:B], ACT.Silu).then_inc(setup_act, 1)
            act.activation(emb[:, 1, :], cos_t[:, 0:B], ACT.Silu).then_inc(setup_act, 1)
            act.wait_ge(setup, SETUP_ABS)
            act.activation(soft[:, 1], soft[:, 0], ACT.Exp).then_inc(setup_act, 1)
            act.wait_ge(setup, SETUP_ABS + 1)
            act.activation(soft[:, 3], soft[:, 2], ACT.Ln).then_inc(setup_act, 1)
            act.wait_ge(main_in, N_MAIN)
            act.wait_ge(cond_ready, 1)
            def split_high(c, q):
                act.wait_ge(stage_in.sem, stage_in.of(c, 16 * (q + 1)))
                act.wait_ge(w_out.sem, w_out.of(c, 16 * q))
                act.activation(split[:, 0, :], stage[:], ACT.Copy, scale=W_SCALE).then_inc(split_hi.sem, 1)

            with act.Fori(0, NCH) as c:
                act.wait_ge(down_done.sem, down_done.of(c, 1))
                act.activation(hid[:], bank[4][0:A, :], ACT.Gelu, bias=down_b[:, 0:1]).then_inc(hid_ready.sem, 1)
                split_high(c, 0)
                for m in range(KD):
                    act.wait_ge(q_done.sem, q_done.of(c, m + 1))
                    act.activation(q_f[:, m, :], bank[m][:], ACT.Identity, bias=bq4[:, m:m + 1],
                                   scale=0.25).then_inc(q_ready.sem, 1)
                act.wait_ge(k_done.sem, k_done.of(c, 1))
                act.activation(k_f[:, 0, 0, :], bank[2][:], ACT.Identity, bias=bkp[:, 0:1], scale=parity[:, 0:1])
                act.activation(k_f[:, 0, 1, :], bank[2][:], ACT.Identity, bias=bkp[:, 1:2],
                               scale=parity[:, 1:2]).then_inc(k0_ready.sem, 1)
                act.wait_ge(v_done.sem, v_done.of(c, 1))
                for s in range(2):
                    act.activation(v_bd[64 * s:64 * s + 64, 0:4, :, s, :].rearrange("p b j d -> p (b j) d"),
                                   bank[6][64 * s:64 * s + 64, :].rearrange("p (j d) -> p j d", d=HD),
                                   ACT.Copy).then_inc(v0_ready.sem, 1)
                split_high(c, 1)
                for u in range(2):
                    act.wait_ge(shifted[u].sem, shifted[u].of(c, 1))
                    act.activation(sc[u][:], sc[u][:], ACT.Exp).then_inc(exp_ready[u].sem, 1)
                for u in range(2):
                    for r in range(4):
                        act.wait_ge(prob_turned[u].sem, prob_turned[u].of(c, r + 1))
                        act.activation(p_f[u][:, r].rearrange("p a h q -> p (a h q)"), bank[4 + r % 2][:],
                                       ACT.Copy).then_inc(p_f_ready[u].sem, 1)
                    act.wait_ge(ctx_done[u].sem, ctx_done[u].of(c, 1))
                    for k in range(KD):
                        act.activation(ctx_f[:, k, 256 * u:256 * u + 256], bank[6 + u][:, 256 * k:256 * k + 256],
                                       ACT.Identity, bias=bv[:, k:k + 1]).then_inc(ctx_ready[u].sem, 1)
                split_high(c, 2)
                for k in range(KD):
                    act.wait_ge(turn2_done.sem, turn2_done.of(c, k + 1))
                    act.activation(h_f[:, k, :], bank[4 + k][:], ACT.Identity, bias=beta2[:, k:k + 1],
                                   scale=g2[:, k:k + 1]).then_inc(h_ready.sem, 1)
                for f in range(KF):
                    act.wait_ge(ff1_done.sem, ff1_done.of(c, f + 1))
                    act.activation(ff[:, f, :], bank[f % 4][:], ACT.Gelu_apprx_sigmoid,
                                   bias=b1[:, f:f + 1]).then_inc(ff_ready.sem, 1)
                split_high(c, 3)
                for k in range(KD):
                    act.wait_ge(turn3_done.sem, turn3_done.of(c, k + 1))
                    act.activation(h0[:, k, :], bank[4 + k][:], ACT.Identity, bias=ln_b[:, k:k + 1],
                                   scale=ln_g[:, k:k + 1]).then_inc(h0_ready.sem, 1)
                act.wait_ge(gap_ready.sem, gap_ready.of(c, 1))
                act.activation(gap_e[:], gap[:], ACT.Exp).then_inc(gap_exp.sem, 1)
                act.wait_ge(rows_sent.sem, rows_sent.of(c, 0))
                for g in range(2):
                    act.wait_ge(rows_done.sem, rows_done.of(c, g + 1))
                    act.activation(disp[:, 2 * g:2 * g + 2, 0:P].bitcast(F16),
                                   bank[4 + g][:].rearrange("p (i d) -> p i d", d=D), ACT.Copy).then_inc(rows_hi.sem, 1)

            def load_rows(n, j):
                r = act.value_load(tile_ri[0:1, bass.ds(n, 1)], min_val=0, max_val=E * CAP)
                act.dma_start(xs[j][:], xs_dram[bass.ds(r, P), :]).then_inc(xs_in[j], 16)

            def hidden(n, j):
                e = act.value_load(tile_ei[0:1, bass.ds(n, 1)], min_val=0, max_val=E - 1)
                for f in range(KF):
                    if f % 4 == 0:
                        act.wait_ge(m1_done, n * 2 + f // 4 + 1)
                        act.nop(nofuse=True)
                    ins = act.activation(h32[j][:, f, :], bank[2 * j + f // 4][:, P * (f % 4):P * (f % 4) + P], ACT.Relu,
                                         bias=moe_b1[:, bass.ds(e, 1), f], scale=1.0 / W_SCALE)
                    if f % 4 == 3:
                        ins.then_inc(h32_ready, 1)

            def scaled(n, j):
                act.wait_ge(m2_done, n + 1)
                act.wait_ge(gates_ready, n + 1)
                act.wait_ge(added, n + 1)
                act.nop(nofuse=True)
                act.activation(ys[j][:], bank[4 + j][:, 0:D], ACT.Copy, scale=gates[:, bass.ds(n, 1)]
                               ).then_inc(ys_ready, 1)

            act.sem_inc(ys_ready, 2)
            act.wait_ge(plan_ready, 1)
            act.wait_ge(rest_out, 16 * (E + 1))
            act.wait_ge(rows_sent.sem, rows_sent.of(NCH, 0))
            load_rows(0, 0)
            load_rows(1, 1)
            act.wait_ge(xs_f_ready, 1)
            act.wait_ge(gates_ready, 1)
            load_rows(2, 0)
            hidden(0, 0)
            with act.Fori(0, TILES // 2) as i:
                for j in range(2):
                    n = i * 2 + j + 1
                    act.wait_ge(xs_f_ready, n + 1)
                    act.wait_ge(gates_ready, n + 1)
                    load_rows(n + 2, 1 - j)
                    hidden(n, 1 - j)
                    scaled(n - 1, j)
            scaled(TILES - 1, (TILES - 1) % 2)
            act.wait_ge(xs_in[0], 16 * (TILES // 2 + 2))

        @block.vector
        def _(dve):
            for free_at_first in (y_ready, x3_ready, acc_ready, rows_ready, split_lo, biased[0], biased[1]):
                dve.sem_inc(free_at_first.sem, 1)
            done = [0]

            def step(ins):
                done[0] += 1
                ins.then_inc(setup, 1)
                dve.wait_ge(setup, done[0])

            dve.memset(v_bd[:], 0.0).then_inc(zeroed, 1)
            dve.memset(hid2[A:A + 1, :], 1.0).then_inc(zeroed, 1)
            dve.memset(ones[:], 1.0).then_inc(zeroed, 1)
            dve.memset(seen[:], 0.0).then_inc(zeroed, 1)
            dve.memset(empty[:].bitcast(U32), 0).then_inc(zeroed, 1)
            dve.wait_ge(zeroed, 5)
            dve.memset(empty[:, D:D + 1].bitcast(U32), NO_TOKEN).then_inc(zeroed, 1)
            dve.wait_ge(early_in, N_EARLY)
            dve.tensor_copy(ident16[:], ident[:]).then_inc(zeroed, 1)
            step(dve.tensor_copy(dom_f[:], dom_i[:]))
            step(dve.tensor_scalar(dom_c[:], dom_f[:], 0.0, float(NDOM - 1), ALU.max, ALU.min))
            dve.tensor_copy(dom_at[:], dom_c[0:1, :]).then_inc(dom_ready, 1)
            step(dve.tensor_tensor(valid[:], dom_f[:], dom_c[:], ALU.is_equal))
            step(dve.tensor_scalar(hot_dom[:], dom_c[0:NDOM, :], iota_p[0:NDOM, 0:1], None, ALU.is_equal))
            step(dve.tensor_tensor(hot_val[:], hot_dom[:], valid[0:NDOM, :], ALU.mult))
            step(dve.tensor_scalar(invalid[:], valid[:], -1.0, 1.0, ALU.mult, ALU.add))
            assert done[0] == SETUP_DOM
            dve.wait_ge(cond_in, N_COND)
            step(dve.tensor_copy(time_f[:], time_i[:]))
            step(dve.tensor_scalar(quot[:], time_f[:], 0.01, None, ALU.mult))
            step(dve.tensor_scalar(q_hi[:], quot[:], 4097.0, None, ALU.mult))
            step(dve.tensor_tensor(q_lo[:], q_hi[:], quot[:], ALU.subtract))
            step(dve.tensor_tensor(q_hi[:], q_hi[:], q_lo[:], ALU.subtract))
            step(dve.tensor_tensor(q_lo[:], quot[:], q_hi[:], ALU.subtract))
            step(dve.scalar_tensor_tensor(time_f[:], q_hi[:], -100.0, time_f[:], ALU.mult, ALU.add))
            step(dve.scalar_tensor_tensor(time_f[:], q_lo[:], -100.0, time_f[:], ALU.mult, ALU.add))
            step(dve.scalar_tensor_tensor(time_f[:], time_f[:], 0.01, quot[:], ALU.mult, ALU.add))
            step(dve.tensor_scalar(angle[:, 0:B], time_f[:], 4000.0, freqs[:, 0:1], ALU.mult, ALU.mult))
            step(dve.tensor_scalar(turns[:], angle[:], INV_2PI, ROUND, ALU.mult, ALU.add))
            step(dve.tensor_scalar(turns[:], turns[:], ROUND, None, ALU.subtract))
            for part in TWO_PI_PARTS:
                step(dve.scalar_tensor_tensor(angle[:], turns[:], -part, angle[:], ALU.mult, ALU.add))
            step(dve.tensor_scalar(angle[:], angle[:], float(np.float32(3.1415925)), -float(np.float32(3.1415925)),
                                   ALU.min, ALU.max))
            step(dve.scalar_tensor_tensor(cos_in[:], angle[:], -1.0, angle[:], ALU.mult, ALU.max))
            step(dve.tensor_scalar(cos_in[:], cos_in[:], -1.0, HALF_PI, ALU.mult, ALU.add))
            assert done[0] == SETUP_ANGLES
            step(dve.tensor_copy(sub_f[:], sub_i[:]))
            step(dve.tensor_scalar(sub_f[:], sub_f[:], 0.0, float(NSUB - 1), ALU.max, ALU.min))
            step(dve.tensor_scalar(hot_sub[:], sub_f[0:NSUB, :], iota_p[0:NSUB, 0:1], None, ALU.is_equal))
            assert done[0] == SETUP_SUB
            step(dve.tensor_scalar(bq4[:], bq[:], 0.25, None, ALU.mult))
            step(dve.tensor_scalar(bkp[:], parity[:], bk[:, 0:1], None, ALU.mult))
            dve.wait_ge(setup_pe, 1)
            step(dve.tensor_copy(add_o[:], bank[0][0:A, 0:B]))
            dve.wait_ge(setup_pe, 2)
            step(dve.tensor_copy(se[:], bank[1][0:SE, 0:B]))
            assert done[0] == SETUP_SE
            dve.wait_ge(setup_pe, 3)
            step(dve.tensor_scalar(hyp1[:], bank[2][0:SH, 0:B], hyp_b1[:, 0:1], 0.0, ALU.add, ALU.max))
            dve.wait_ge(setup_pe, 4)
            step(dve.tensor_scalar(hyp2[:], bank[3][0:SH, 0:B], hyp_b2[:, 0:1], None, ALU.add))
            dve.wait_ge(setup_pe, 5)
            step(dve.tensor_scalar(sty1[:], bank[4][0:SH // 2, 0:B], sty_b1[:, 0:1], 0.0, ALU.add, ALU.max))
            dve.wait_ge(setup_pe, 6)
            for m in range(2 * KD):
                step(dve.tensor_scalar(sty[:, m, :], bank[5][:, B * m:B * m + B], sty_b2[:, m:m + 1], None, ALU.add))
            step(dve.scalar_tensor_tensor(soft[:, 0], sty[:, 0:KD, :], -1.0, sty[:, 0:KD, :], ALU.mult, ALU.min))
            assert done[0] == SETUP_ABS
            dve.wait_ge(setup_act, 5)
            step(dve.tensor_scalar(soft[:, 2], soft[:, 1], 1.0, None, ALU.add))
            step(dve.tensor_scalar(gamma3[:], soft[:, 2], -1.0, None, ALU.add))
            step(dve.tensor_tensor(gamma3[:], soft[:, 1], gamma3[:], ALU.subtract))
            step(dve.scalar_tensor_tensor(gamma3[:], sty[:, 0:KD, :], 0.0, gamma3[:], ALU.max, ALU.add))
            dve.wait_ge(setup_act, 6)
            step(dve.tensor_tensor(gamma3[:], gamma3[:], soft[:, 3], ALU.add))
            step(dve.tensor_scalar(gamma3[:], gamma3[:], 1e-8, None, ALU.add))
            dve.wait_ge(setup_pe, 7)
            for m in range(2 * KD):
                step(dve.tensor_scalar(ada[:, m, :], bank[6][:, B * m:B * m + B], b_ada[:, m:m + 1],
                                       1.0 if m < KD else 0.0, ALU.add, ALU.add))
            dve.drain().then_inc(cond_ready, 1)
            dve.wait_ge(main_in, N_MAIN)
            dve.wait_ge(setup_act, 6)
            dve.wait_ge(zeroed, 7)

            def split_low(c, q):
                dve.wait_ge(split_hi.sem, split_hi.of(c, q + 1))
                dve.scalar_tensor_tensor(split[:, 1, :], stage[:], W_SCALE, split[:, 0, :], ALU.mult,
                                         ALU.subtract).then_inc(split_lo.sem, 1)

            with dve.Fori(0, NCH) as c:
                n = [0]

                def vec(ins):
                    n[0] += 1
                    ins.then_inc(vec_step.sem, 1)
                    dve.wait_ge(vec_step.sem, vec_step.of(c, n[0]))

                def rsqrt(w, eps):
                    v, r, a, b = var[:, 0:w], rstd[:, 0:w], newton[:, 0:w], newton2[:, 0:w]
                    vec(dve.tensor_scalar(v, mv[:, 0:w, 1], eps, None, ALU.add))
                    vec(dve.tensor_scalar(r.bitcast(I32), v.bitcast(I32), -0.5, RSQRT_SEED, ALU.mult, ALU.add))
                    for _ in range(3):
                        vec(dve.scalar_tensor_tensor(a, r, -0.5, r, ALU.mult, ALU.mult))
                        vec(dve.tensor_tensor(b, a, v, ALU.mult))
                        vec(dve.scalar_tensor_tensor(r, b, 1.5, r, ALU.add, ALU.mult))

                def token_stats(z):
                    for i in range(TT):
                        ins = dve.bn_stats(stats[:, i, :], z[:, i, :])
                    vec(ins)
                    dve.nop(nofuse=True)
                    for i in range(TT):
                        ins = dve.bn_aggr(mv[:, i, :], stats[:, i, :])
                    vec(ins)
                    rsqrt(TT, 1e-5)

                def normalise(dst, z):
                    for i in range(TT):
                        ins = dve.tensor_scalar(dst[:, i, :], z[:, i, :], mv[:, i, 0:1], rstd[:, i:i + 1],
                                                ALU.subtract, ALU.mult)
                    return ins

                dve.wait_ge(expert_done.sem, expert_done.of(c, 1))
                dve.tensor_tensor(hid2[0:A, :].rearrange("p (b s) -> p b s", s=S),
                                  bank[5][0:A, :].rearrange("p (b s) -> p b s", s=S),
                                  add_o[:, bass.ds(c * CB, CB)].unsqueeze(2).broadcast_to([A, CB, S]),
                                  ALU.add).then_inc(hid2_ready.sem, 1)
                dve.wait_ge(x_t_in.sem, x_t_in.of(c, 16))
                for g in range(2):
                    dve.wait_ge(up_done.sem, up_done.of(c, g + 1))
                    dve.tensor_tensor(y[:, 2 * g:2 * g + 2, :], bank[6 + g][:].rearrange("p (n d) -> p n d", d=D),
                                      x_t[:, 2 * g:2 * g + 2, :], ALU.add).then_inc(y_ready.sem, 1)
                dve.wait_ge(y_ready.sem, y_ready.of(c, 2))
                token_stats(y)
                split_low(c, 0)
                for i in range(TT):
                    ins = dve.scalar_tensor_tensor(y[:, i, :], y[:, i, :], mv[:, i, 0:1], gamma0[:],
                                                   ALU.subtract, ALU.mult)
                vec(ins)
                for i in range(TT):
                    ins = dve.scalar_tensor_tensor(y[:, i, :], y[:, i, :], rstd[:, i:i + 1], beta0[:],
                                                   ALU.mult, ALU.add)
                vec(ins)
                token_stats(y)
                normalise(xn1, y).then_inc(xn1_ready.sem, 1)
                for k in range(KD):
                    dve.wait_ge(turn1_done.sem, turn1_done.of(c, k + 1))
                    dve.tensor_tensor(ada_t[:, k, :].rearrange("p (b s) -> p b s", s=S),
                                      bank[4 + k][:].rearrange("p (b s) -> p b s", s=S),
                                      ada[:, k, bass.ds(c * CB, CB)].unsqueeze(2).broadcast_to([P, CB, S]),
                                      ALU.mult).then_inc(ada_scaled.sem, 1)
                dve.wait_ge(k_done.sem, k_done.of(c, 2))
                dve.tensor_scalar(k_f[:, 1, 0, :], bank[3][:], bk[:, 1:2], parity[:, 0:1], ALU.add, ALU.mult)
                dve.tensor_scalar(k_f[:, 1, 1, :], bank[3][:], bk[:, 1:2], parity[:, 1:2], ALU.add,
                                  ALU.mult).then_inc(k1_ready.sem, 1)
                dve.wait_ge(v_done.sem, v_done.of(c, 2))
                for s in range(2):
                    dve.tensor_copy(v_bd[64 * s:64 * s + 64, 4:8, :, s, :].rearrange("p b j d -> p (b j) d"),
                                    bank[7][64 * s:64 * s + 64, :].rearrange("p (j d) -> p j d", d=HD)
                                    ).then_inc(v1_ready.sem, 1)
                for u in range(2):
                    for r in range(4):
                        dve.wait_ge(score_done[u].sem, score_done[u].of(c, r + 1))
                        dve.wait_ge(bias_masked[u].sem, bias_masked[u].of(c, r + 1))
                        dve.tensor_tensor(sc[u][:, r].rearrange("p a h k -> p (a h k)"), bank[r][:],
                                          bias[u][:, r].rearrange("p a h k -> p (a h k)"),
                                          ALU.add).then_inc(biased[u].sem, 1)
                    dve.wait_ge(biased[u].sem, biased[u].of(c, 4))
                    dve.tensor_reduce(sc_max[u][:], sc[u][:].rearrange("p r a h k -> p (r a h) k"), AX.X,
                                      ALU.max).then_inc(max_ready[u].sem, 1)
                split_low(c, 1)
                for u in range(2):
                    dve.wait_ge(exp_ready[u].sem, exp_ready[u].of(c, 1))
                    vec(dve.tensor_reduce(sc_sum[u][:], sc[u][:].rearrange("p r a h k -> p (r a h) k"), AX.X, ALU.add))
                    dve.reciprocal(sc_inv[u][:], sc_sum[u][:]).then_inc(inv_ready[u].sem, 1)
                dve.wait_ge(x_stored.sem, x_stored.of(c, 0))
                for g in range(2):
                    dve.wait_ge(wo_done.sem, wo_done.of(c, g + 1))
                    dve.tensor_tensor(x2[:, 2 * g:2 * g + 2, :], bank[6 + g][:].rearrange("p (n d) -> p n d", d=D),
                                      bo[:].unsqueeze(1).broadcast_to([P, 2, D]), ALU.add).then_inc(x2_ready.sem, 1)
                dve.wait_ge(x2_ready.sem, x2_ready.of(c, 2))
                token_stats(x2)
                normalise(xn2, x2).then_inc(xn2_ready.sem, 1)
                split_low(c, 2)
                for g in range(2):
                    dve.wait_ge(ff2_done.sem, ff2_done.of(c, g + 1))
                    dve.wait_ge(x2b_ready.sem, x2b_ready.of(c, 1))
                    dve.tensor_tensor(x3[:, 2 * g:2 * g + 2, :], bank[6 + g][:].rearrange("p (n d) -> p n d", d=D),
                                      x2b[:, 2 * g:2 * g + 2, :], ALU.add).then_inc(x3_ready.sem, 1)
                v3 = x3[:].rearrange("p n (i a e) -> p n i a e", a=2, e=2)
                v4 = x4[:].rearrange("p n (i a e) -> p n i a e", a=2, e=2)
                cs = cos_t[:, bass.ds(B + c * TT * 2, TT * 2)].rearrange("p (n a) -> p n a", a=2)
                sn = sin_t[:, bass.ds(B + c * TT * 2, TT * 2)].rearrange("p (n a) -> p n a", a=2)
                cs = cs.unsqueeze(2).broadcast_to([P, TT, S, 2])
                sn = sn.unsqueeze(2).broadcast_to([P, TT, S, 2])
                dve.wait_ge(x3_ready.sem, x3_ready.of(c, 2))
                dve.tensor_tensor(rot[0][:], v3[:, :, :, :, 0], cs, ALU.mult)
                vec(dve.tensor_tensor(rot[1][:], v3[:, :, :, :, 1], sn, ALU.mult))
                vec(dve.tensor_tensor(v4[:, :, :, :, 0], rot[0][:], rot[1][:], ALU.add))
                dve.wait_ge(odd_ready.sem, odd_ready.of(c, 1))
                token_stats(x4)
                normalise(xn3, x4).then_inc(xn3_ready.sem, 1)
                split_low(c, 3)
                dve.wait_ge(h0_ready.sem, h0_ready.of(c, 2))
                for k in range(KD):
                    for b in range(CB):
                        ins = dve.bn_stats(stats[:, k * CB + b, :], h0[:, k, S * b:S * b + S])
                vec(ins)
                dve.nop(nofuse=True)
                for i in range(KD * CB):
                    ins = dve.bn_aggr(mv[:, i, :], stats[:, i, :])
                vec(ins)
                rsqrt(KD * CB, 1e-8)
                vec(dve.tensor_tensor(in_a[:].rearrange("p (k b) -> p k b", k=KD),
                                      rstd[:].rearrange("p (k b) -> p k b", k=KD),
                                      gamma3[:, :, bass.ds(c * CB, CB)], ALU.mult))
                vec(dve.tensor_tensor(in_b[:], in_a[:], mv[:, :, 0], ALU.mult))
                vec(dve.tensor_tensor(in_b[:].rearrange("p (k b) -> p k b", k=KD),
                                      sty[:, KD:2 * KD, bass.ds(c * CB, CB)],
                                      in_b[:].rearrange("p (k b) -> p k b", k=KD), ALU.subtract))
                for k in range(KD):
                    for b in range(CB):
                        i = k * CB + b
                        ins = dve.tensor_scalar(h3[:, k, S * b:S * b + S], h0[:, k, S * b:S * b + S],
                                                in_a[:, i:i + 1], in_b[:, i:i + 1], ALU.mult, ALU.add)
                ins.then_inc(h3_ready.sem, 1)
                ie = iota_e[:].unsqueeze(1).broadcast_to([P, TT, E])

                def wide(x):
                    return x[:].unsqueeze(2).broadcast_to([P, TT, E])

                def largest(top, hot, values, first):
                    vec(dve.tensor_reduce(top[:], values[:], AX.X, ALU.max))
                    vec(dve.tensor_tensor(cand[:], values[:], wide(top), ALU.is_equal))
                    vec(dve.scalar_tensor_tensor(cand[:], cand[:], -100.0, ie, ALU.mult, ALU.add))
                    vec(dve.tensor_reduce(first[:], cand[:], AX.X, ALU.min))
                    vec(dve.tensor_tensor(hot[:], cand[:], wide(first), ALU.is_equal))

                dve.wait_ge(logit_done.sem, logit_done.of(c, 1))
                vec(dve.tensor_copy(logit[:], bank[6][:, 0:TT * E].rearrange("p (n e) -> p n e", e=E)))
                largest(top1, hot1, logit, first1)
                vec(dve.scalar_tensor_tensor(logit2[:], hot1[:], MASKED, logit[:], ALU.mult, ALU.add))
                largest(top2, hot2, logit2, first2)
                dve.tensor_tensor(gap[:], top2[:], top1[:], ALU.subtract).then_inc(gap_ready.sem, 1)
                dve.tensor_tensor(picks[:], hot1[:], hot2[:], ALU.add).then_inc(picks_ready.sem, 1)
                dve.wait_ge(rank_done.sem, rank_done.of(c, 1))
                vec(dve.tensor_copy(total[:].rearrange("p n e -> p (n e)"), bank[6][:, TT * E:2 * TT * E]))
                vec(dve.tensor_copy(before[:, 0, :], seen[:]))
                for i in range(TT):
                    vec(dve.tensor_tensor(before[:, i + 1, :], before[:, i, :], total[:, i, :], ALU.add))
                vec(dve.tensor_copy(seen[:], before[:, TT, :]))
                vec(dve.tensor_tensor(place[:], bank[6][:, 0:TT * E].rearrange("p (n e) -> p n e", e=E),
                                      before[:, 0:TT, :], ALU.add))
                vec(dve.tensor_tensor(place[:], place[:], region[:].unsqueeze(1).broadcast_to([P, TT, E]), ALU.add))
                dve.tensor_tensor(picked[:, 0], place[:], hot1[:], ALU.mult)
                vec(dve.tensor_tensor(picked[:, 1], place[:], hot2[:], ALU.mult))
                vec(dve.tensor_reduce(slot_f[:], picked[:], AX.X, ALU.add))
                dve.wait_ge(rows_sent.sem, rows_sent.of(c, 0))
                dve.tensor_copy(slot[:], slot_f[:]).then_inc(slot_ready.sem, 1)
                for g in range(2):
                    dve.wait_ge(rows_hi.sem, rows_hi.of(c, g + 1))
                    dve.tensor_tensor(disp[:, 2 * g:2 * g + 2, P:D].bitcast(F16),
                                      bank[4 + g][:].rearrange("p (i d) -> p i d", d=D),
                                      disp[:, 2 * g:2 * g + 2, 0:P].bitcast(F16), ALU.subtract).then_inc(rows_ready.sem, 1)
                dve.tensor_copy(disp[:, :, D].bitcast(I32), tok_id[:, bass.ds(c * TT, TT)])
                dve.tensor_scalar(disp[:, :, D + 1], first1[:], 100.0, None, ALU.add)
                dve.wait_ge(gap_exp.sem, gap_exp.of(c, 1))
                vec(dve.tensor_scalar(gate_d[:], gap_e[:], 1.0, None, ALU.add))
                vec(dve.reciprocal(gate1[:], gate_d[:]))
                vec(dve.tensor_tensor(gate2[:], gap_e[:], gate1[:], ALU.mult))
                vec(dve.tensor_scalar(disp[:, :, D + 2], gate2[:], 1.0 / W_SCALE, None, ALU.mult))
                dve.scalar_tensor_tensor(disp[:, :, D + 3], gate1[:], 1.0 / W_SCALE, disp[:, :, D + 2], ALU.mult,
                                         ALU.subtract).then_inc(disp_ready.sem, 1)
                dve.tensor_tensor(hot1[:], hot1[:], wide(gate1), ALU.mult)
                vec(dve.tensor_tensor(hot2[:], hot2[:], wide(gate2), ALU.mult))
                dve.tensor_tensor(gate[:], hot1[:], hot2[:], ALU.add).then_inc(gate_ready.sem, 1)
                dve.wait_ge(gate_turned.sem, gate_turned.of(c, 1))
                dve.tensor_copy(gate_f[:], bank[7][0:E, :]).then_inc(gate_f_ready.sem, 1)
                for g in range(2):
                    dve.wait_ge(b2_done.sem, b2_done.of(c, g + 1))
                    dve.tensor_tensor(x4b[:, 2 * g:2 * g + 2, :],
                                      bank[6 + g][:].rearrange("p (n d) -> p n d", d=D),
                                      x4[:, 2 * g:2 * g + 2, :], ALU.add).then_inc(acc_ready.sem, 1)
                assert n[0] == VEC_STEPS, n[0]
            planned = [0]

            def plan_step(ins):
                planned[0] += 1
                ins.then_inc(plan, 1)
                dve.wait_ge(plan, planned[0])

            T2 = TILES + 2
            dve.wait_ge(acc_ready.sem, acc_ready.of(NCH, 0))
            plan_step(dve.tensor_tensor(over[:], seen[:].unsqueeze(2).broadcast_to([P, E, NT]),
                                        tile_m[:].unsqueeze(1).broadcast_to([P, E, NT]), ALU.is_gt))
            plan_step(dve.tensor_reduce(n_tiles[:], over[:], AX.X, ALU.add))
            plan_step(dve.tensor_copy(ends[:], n_tiles[:]))
            for e in range(1, E):
                plan_step(dve.tensor_tensor(ends[:, e:e + 1], ends[:, e:e + 1], ends[:, e - 1:e], ALU.add))
            plan_step(dve.tensor_tensor(past[:], iota_t[:].unsqueeze(2).broadcast_to([P, T2, E]),
                                        ends[:].unsqueeze(1).broadcast_to([P, T2, E]), ALU.is_ge))
            plan_step(dve.tensor_reduce(tile_e[:], past[:], AX.X, ALU.add))
            plan_step(dve.tensor_tensor(past_n[:], past[:], n_tiles[:].unsqueeze(1).broadcast_to([P, T2, E]), ALU.mult))
            plan_step(dve.tensor_reduce(tile_s[:], past_n[:], AX.X, ALU.add))
            plan_step(dve.tensor_tensor(tile_s[:], iota_t[:], tile_s[:], ALU.subtract))
            plan_step(dve.tensor_scalar(tile_l[:], tile_e[:], E - 0.5, None, ALU.is_lt))
            plan_step(dve.tensor_tensor(tile_s[:], tile_s[:], tile_l[:], ALU.mult))
            plan_step(dve.tensor_scalar(tile_r[:], tile_e[:], float(CAP), None, ALU.mult))
            plan_step(dve.scalar_tensor_tensor(tile_r[:], tile_s[:], float(P), tile_r[:], ALU.mult, ALU.add))
            plan_step(dve.tensor_scalar(tile_e[:], tile_e[:], float(E - 1), None, ALU.min))
            plan_step(dve.tensor_copy(tile_ri[:], tile_r[0:1, :]))
            plan_step(dve.tensor_copy(tile_ei[:], tile_e[0:1, :]))
            dve.tensor_tensor(rest_i[:], seen[0:1, :], region[0:1, :], ALU.add).then_inc(plan_ready, 1)
            dve.wait_ge(w_out.sem, w_out.of(NCH, 0))

            def rows_in(n, j):
                dve.wait_ge(turned, n + 1)
                dve.tensor_copy(xs_f[j][:].rearrange("p k n -> p (k n)"), bank[6 + j][:, 0:D].bitcast(F16)
                                ).then_inc(xs_f_ready, 1)
                dve.tensor_copy(meta[:, bass.ds(n, 1), :].rearrange("p a w -> p (a w)").bitcast(U32),
                                xs[j][:, D:ROW].bitcast(U32)).then_inc(gate_step, 1)
                dve.tensor_scalar(gates[:, bass.ds(n, 1)], xs[j][:, D + 1:D + 2], tile_e[:, bass.ds(n, 1)],
                                  xs[j][:, D + 3:D + 4], ALU.is_equal, ALU.mult).then_inc(gate_step, 1)
                dve.wait_ge(gate_step, n * 2 + 2)
                dve.tensor_tensor(gates[:, bass.ds(n, 1)], gates[:, bass.ds(n, 1)], xs[j][:, D + 2:D + 3],
                                  ALU.add).then_inc(gates_ready, 1)

            def halves(n, j):
                for g in range(2):
                    dve.wait_ge(h32_ready, n * 2 + g + 1)
                    dve.tensor_copy(h_hi[j][:, 4 * g:4 * g + 4, :], h32[j][:, 4 * g:4 * g + 4, :]).then_inc(hi_ready, 1)
                    dve.wait_ge(hi_ready, n * 2 + g + 1)
                    dve.tensor_tensor(h_lo[j][:, 4 * g:4 * g + 4, :], h32[j][:, 4 * g:4 * g + 4, :],
                                      h_hi[j][:, 4 * g:4 * g + 4, :], ALU.subtract).then_inc(lo_ready, 1)

            rows_in(0, 0)
            rows_in(1, 1)
            halves(0, 0)
            with dve.Fori(0, TILES // 2) as i:
                for j in range(2):
                    n = i * 2 + j + 1
                    rows_in(n + 1, j)
                    halves(n, 1 - j)

        @block.tensor
        def _(pe):
            for free_at_first in (down_done, expert_done, wo_done):
                pe.sem_inc(free_at_first.sem, 1)
            pe.wait_ge(early_in, N_EARLY)
            pe.wait_ge(setup, SETUP_DOM)
            pe.matmul(bank[0][0:A, 0:B], dom_emb[:], hot_dom[:], start=True, stop=False)
            pe.matmul(bank[0][0:A, 0:B], exp_b[:], hot_val[:], start=False, stop=True).then_inc(setup_pe, 1)
            pe.wait_ge(cond_in, N_COND)
            pe.wait_ge(setup, SETUP_SUB)
            pe.matmul(bank[1][0:SE, 0:B], subj_emb[:], hot_sub[:], start=True, stop=True).then_inc(setup_pe, 1)
            pe.wait_ge(setup, SETUP_SE)
            pe.matmul(bank[2][0:SH, 0:B], hyp_w1[:], se[:], start=True, stop=True).then_inc(setup_pe, 1)
            pe.wait_ge(setup, SETUP_SE + 1)
            pe.matmul(bank[3][0:SH, 0:B], hyp_w2[:], hyp1[:], start=True, stop=True).then_inc(setup_pe, 1)
            pe.wait_ge(setup, SETUP_SE + 2)
            pe.matmul(bank[4][0:SH // 2, 0:B], sty_w1[:], hyp2[:], start=True, stop=True).then_inc(setup_pe, 1)
            pe.wait_ge(setup, SETUP_SE + 3)
            for m in range(2 * KD):
                mm = pe.matmul(bank[5][:, B * m:B * m + B], sty_w2[:, P * m:P * m + P], sty1[:], start=True, stop=True)
            mm.then_inc(setup_pe, 1)
            pe.wait_ge(setup_act, 4)
            for m in range(2 * KD):
                for k in range(KD):
                    mm = pe.matmul(bank[6][:, B * m:B * m + B], w_ada[:, k, P * m:P * m + P], emb[:, k, :],
                                   start=(k == 0), stop=(k == KD - 1))
            mm.then_inc(setup_pe, 1)
            pe.wait_ge(main_in, N_MAIN)
            pe.wait_ge(cond_ready, 1)
            pe.wait_ge(zeroed, 7)

            with pe.Fori(0, NCH) as c:
                def turn(z, k, done):
                    for i in range(TT):
                        mm = pe.transpose(bank[4 + k][:, P * i:P * i + P], z[:, i, P * k:P * k + P], ident[:])
                    mm.then_inc(done.sem, 1)

                pe.wait_ge(x_f_in.sem, x_f_in.of(c, 16))
                pe.wait_ge(rows_ready.sem, rows_ready.of(c, 0))
                for k in range(KD):
                    mm = pe.matmul(bank[4][0:A, :], down_w[:, k, :], x_f[:, k, :], start=(k == 0), stop=(k == KD - 1))
                mm.then_inc(down_done.sem, 1)
                pe.wait_ge(hid_ready.sem, hid_ready.of(c, 1))
                pe.wait_ge(w_sel_ready.sem, w_sel_ready.of(c, 1))
                pe.nop(nofuse=True)
                for b in range(CB):
                    mm = pe.matmul(bank[5][0:A, S * b:S * b + S], w_sel[:, b, :], hid[:, S * b:S * b + S],
                                   start=True, stop=True)
                mm.then_inc(expert_done.sem, 1)
                pe.wait_ge(hid2_ready.sem, hid2_ready.of(c, 1))
                pe.wait_ge(acc_ready.sem, acc_ready.of(c, 0))
                for i in range(TT):
                    mm = pe.matmul(bank[6 + i // 2][:, D * (i % 2):D * (i % 2) + D], hid2[:, P * i:P * i + P], up_w[:],
                                   start=True, stop=True)
                    if i % 2:
                        mm.then_inc(up_done.sem, 1)
                pe.wait_ge(xn1_ready.sem, xn1_ready.of(c, 1))
                for k in range(KD):
                    turn(xn1, k, turn1_done)
                pe.wait_ge(x1_ready.sem, x1_ready.of(c, 2))
                pe.wait_ge(ff_ready.sem, ff_ready.of(c, 0))
                for base, w, done in ((0, wq, q_done), (2, wk, k_done)):
                    for m in range(KD):
                        for k in range(KD):
                            mm = pe.matmul(bank[base + m][:], w[:, k, P * m:P * m + P], x1[:, k, :],
                                           start=(k == 0), stop=(k == KD - 1))
                        mm.then_inc(done.sem, 1)
                pe.wait_ge(y_ready.sem, y_ready.of(c, 2))
                for b in range(CB):
                    for s in range(2):
                        for k in range(KD):
                            mm = pe.matmul(bank[6 + b // 4][64 * s:64 * s + 64, P * (b % 4):P * (b % 4) + P],
                                           x1[:, k, S * b:S * b + S], wv[:, k, P * s:P * s + P],
                                           start=(k == 0), stop=(k == KD - 1))
                    if b % 4 == 3:
                        mm.then_inc(v_done.sem, 1)
                pe.wait_ge(q_ready.sem, q_ready.of(c, 2))
                pe.wait_ge(k0_ready.sem, k0_ready.of(c, 1))
                pe.wait_ge(k1_ready.sem, k1_ready.of(c, 1))
                for u in range(2):
                    for r in range(4):
                        if u == 1:
                            pe.wait_ge(biased[0].sem, biased[0].of(c, r + 1))
                        for a in range(2):
                            for b2 in range(2):
                                b = 4 * u + 2 * a + b2
                                for h in range(2):
                                    at = a * 256 + h * P
                                    mm = pe.matmul(
                                        bank[r][64 * b2:64 * b2 + 64, at:at + P].rearrange("q (s k) -> q s k", s=2),
                                        q_f[32 * r:32 * r + 32, h, S * b:S * b + S],
                                        k_f[32 * r:32 * r + 32, h, :, S * b:S * b + S], start=True, stop=True)
                        mm.then_inc(score_done[u].sem, 1)
                for u in range(2):
                    pe.wait_ge(prob_ready[u].sem, prob_ready[u].of(c, 1))
                    for r in range(4):
                        if r >= 2:
                            pe.wait_ge(p_f_ready[u].sem, p_f_ready[u].of(c, r - 1))
                        elif u == 1:
                            pe.wait_ge(p_f_ready[0].sem, p_f_ready[0].of(c, 3 + r))
                        else:
                            pe.wait_ge(ada_scaled.sem, ada_scaled.of(c, 2))
                        for i in range(4):
                            a, h = i // 2, i % 2
                            mm = pe.transpose(bank[4 + r % 2][:, P * i:P * i + P],
                                              sc[u][:, r, a, 2 * h:2 * h + 2, :].rearrange("p s k -> p (s k)"), ident[:])
                        mm.then_inc(prob_turned[u].sem, 1)
                    if u == 0:
                        pe.wait_ge(v0_ready.sem, v0_ready.of(c, 2))
                        pe.wait_ge(v1_ready.sem, v1_ready.of(c, 2))
                    for r in range(4):
                        pe.wait_ge(p_f_ready[u].sem, p_f_ready[u].of(c, r + 1))
                        for a in range(2):
                            for b2 in range(2):
                                for h in range(2):
                                    at = h * 256 + a * P + b2 * S
                                    mm = pe.matmul(bank[6 + u][32 * r:32 * r + 32, at:at + S],
                                                   v_bd[:, 4 * u + 2 * a + b2, 4 * h + r].rearrange("p s d -> p (s d)"),
                                                   p_f[u][:, r, a, h, S * b2:S * b2 + S], start=True, stop=True)
                    mm.then_inc(ctx_done[u].sem, 1)
                for g in range(2):
                    pe.wait_ge(ctx_ready[g].sem, ctx_ready[g].of(c, 2))
                    if g == 0:
                        pe.wait_ge(ctx_ready[1].sem, ctx_ready[1].of(c, 2))
                    for i in range(2):
                        at = P * (2 * g + i)
                        for k in range(KD):
                            pe.matmul(bank[6 + g][:, D * i:D * i + D], ctx_f[:, k, at:at + P], wo[:, k, :],
                                      start=(k == 0), stop=False, skip_group_check=True)
                        for k in range(KD):
                            mm = pe.matmul(bank[6 + g][:, D * i + P * k:D * i + P * k + P], x1[:, k, at:at + P], ident[:],
                                           start=False, stop=True, skip_group_check=True)
                    mm.then_inc(wo_done.sem, 1)
                pe.wait_ge(xn2_ready.sem, xn2_ready.of(c, 1))
                pe.wait_ge(p_f_ready[1].sem, p_f_ready[1].of(c, 4))
                for k in range(KD):
                    turn(xn2, k, turn2_done)
                pe.wait_ge(h_ready.sem, h_ready.of(c, 2))
                for f in range(KF):
                    if f < 4:
                        pe.wait_ge(biased[1].sem, biased[1].of(c, f + 1))
                    else:
                        pe.wait_ge(ff_ready.sem, ff_ready.of(c, f - 3))
                    for k in range(KD):
                        mm = pe.matmul(bank[f % 4][:], w1[:, k, P * f:P * f + P], h_f[:, k, :],
                                       start=(k == 0), stop=(k == KD - 1))
                    mm.then_inc(ff1_done.sem, 1)
                pe.wait_ge(x2_ready.sem, x2_ready.of(c, 2))
                for i in range(TT):
                    for f in range(KF):
                        if i == 0:
                            pe.wait_ge(ff_ready.sem, ff_ready.of(c, f + 1))
                        mm = pe.matmul(bank[6 + i // 2][:, D * (i % 2):D * (i % 2) + D], ff[:, f, P * i:P * i + P],
                                       w2[:, f, :], start=(f == 0), stop=(f == KF - 1))
                    if i % 2:
                        mm.then_inc(ff2_done.sem, 1)
                pe.wait_ge(xn3_ready.sem, xn3_ready.of(c, 1))
                pe.wait_ge(h_ready.sem, h_ready.of(c, 2))
                for k in range(KD):
                    turn(xn3, k, turn3_done)
                pe.wait_ge(h3_ready.sem, h3_ready.of(c, 1))
                pe.wait_ge(x3_ready.sem, x3_ready.of(c, 2))
                for i in range(TT):
                    for k in range(KD):
                        mm = pe.matmul(bank[6][:, E * i:E * i + E], h3[:, k, P * i:P * i + P], router[:, k, :],
                                       start=(k == 0), stop=(k == KD - 1))
                mm.then_inc(logit_done.sem, 1)
                for g in range(2):
                    for i in range(2):
                        for k in range(KD):
                            mm = pe.transpose(bank[4 + g][:, D * i + P * k:D * i + P * k + P],
                                              h3[:, k, P * (2 * g + i):P * (2 * g + i) + P], ident[:])
                    mm.then_inc(rows_done.sem, 1)
                pe.wait_ge(picks_ready.sem, picks_ready.of(c, 1))
                pe.matmul(bank[6][:, 0:TT * E], lower[:], picks[:].rearrange("p n e -> p (n e)"), start=True, stop=True)
                pe.matmul(bank[6][:, TT * E:2 * TT * E], ones[:], picks[:].rearrange("p n e -> p (n e)"),
                          start=True, stop=True).then_inc(rank_done.sem, 1)
                pe.wait_ge(gate_ready.sem, gate_ready.of(c, 1))
                for i in range(TT):
                    mm = pe.transpose(bank[7][0:E, P * i:P * i + P], gate[:, i, :], ident[:])
                mm.then_inc(gate_turned.sem, 1)
                pe.wait_ge(gate_f_ready.sem, gate_f_ready.of(c, 1))
                for i in range(TT):
                    mm = pe.matmul(bank[6 + i // 2][:, D * (i % 2):D * (i % 2) + D], gate_f[:, P * i:P * i + P], moe_b2[:],
                                   start=True, stop=True)
                    if i % 2:
                        mm.then_inc(b2_done.sem, 1)
            pe.wait_ge(acc_ready.sem, acc_ready.of(NCH, 0))
            pe.wait_ge(plan_ready, 1)

            def turn_rows(n, j, turn):
                pe.wait_ge(xs_in[j], turn * 16 + 16)
                for k in range(4):
                    mm = pe.transpose(bank[6 + j][:, 64 * k:64 * k + 64].bitcast(F16),
                                      xs[j][:, 64 * k:64 * k + 64].bitcast(F16), ident16[:])
                mm.then_inc(turned, 1)

            def up(n, j):
                e = pe.value_load(tile_ei[0:1, bass.ds(n, 1)], min_val=0, max_val=E - 1)
                pe.wait_ge(weights_in, e * 16 + 16)
                pe.wait_ge(xs_f_ready, n + 1)
                pe.nop(nofuse=True)
                for f in range(KF):
                    o = bank[2 * j + f // 4][:, P * (f % 4):P * (f % 4) + P]
                    for k in range(KD):
                        hi = w_moe[:, bass.ds(e * WE + (k * FF + f * P), P)]
                        lo = w_moe[:, bass.ds(e * WE + (WE // 4 + k * FF + f * P), P)]
                        pe.matmul(o, hi, xs_f[j][:, k, :], start=(k == 0), stop=False)
                        pe.matmul(o, hi, xs_f[j][:, KD + k, :], start=False, stop=False)
                        mm = pe.matmul(o, lo, xs_f[j][:, k, :], start=False, stop=(k == KD - 1))
                    if f % 4 == 3:
                        mm.then_inc(m1_done, 1)

            def down(n, j):
                e = pe.value_load(tile_ei[0:1, bass.ds(n, 1)], min_val=0, max_val=E - 1)
                o = bank[4 + j][:, 0:D]
                for f in range(KF):
                    if f % 4 == 0:
                        pe.wait_ge(lo_ready, n * 2 + f // 4 + 1)
                        pe.nop(nofuse=True)
                    hi = w_moe[:, bass.ds(e * WE + (WE // 2 + f * D), D)]
                    lo = w_moe[:, bass.ds(e * WE + (3 * WE // 4 + f * D), D)]
                    pe.matmul(o, h_hi[j][:, f, :], hi, start=(f == 0), stop=False)
                    pe.matmul(o, h_hi[j][:, f, :], lo, start=False, stop=False)
                    mm = pe.matmul(o, h_lo[j][:, f, :], hi, start=False, stop=(f == KF - 1))
                mm.then_inc(m2_done, 1)

            turn_rows(0, 0, 0)
            turn_rows(1, 1, 0)
            up(0, 0)
            with pe.Fori(0, TILES // 2) as i:
                for j in range(2):
                    n = i * 2 + j + 1
                    up(n, 1 - j)
                    turn_rows(n + 1, j, i + 1)
                    pe.wait_ge(ys_ready, n)
                    pe.nop(nofuse=True)
                    down(n - 1, j)
            pe.wait_ge(ys_ready, TILES)
            down(TILES - 1, (TILES - 1) % 2)


SETUP_DOM = 6
SETUP_ANGLES = SETUP_DOM + 18
SETUP_SUB = SETUP_ANGLES + 3
SETUP_SE = SETUP_SUB + 4
SETUP_ABS = SETUP_SE + 8


def kernel(**inputs):
    import concourse.bacc as bacc
    from concourse.bass_utils import run_bass_kernel_spmd as run

    a = {k: np.ascontiguousarray(v) for k, v in inputs.items()}
    c_ = np.ascontiguousarray

    def cols(v):
        return c_(v.reshape(-1, P).T)

    def row(v):
        return v.reshape(1, -1)

    x = a["x"].reshape(N, D)
    bias = a["fside_Bx16xSxS_0"].reshape(B // 4, 2, 2, 2, 4, 2, S, S)
    bias = bias.transpose(0, 2, 6, 4, 1, 3, 5, 7).reshape(B // 4, P, 2048)
    mask = a["mask_Bx1xSxS_bk0"].reshape(NT, 2, S, S).transpose(1, 2, 0, 3).reshape(P, NT, S)
    wv = a["L1_cond_Wv"].reshape(D, H // 2, 2, HD).transpose(0, 2, 1, 3).reshape(D, D)
    th = np.stack([a["condB_theta"], a["condB_phi"]], -1).reshape(NT, 2, 2).transpose(1, 0, 2).reshape(2, 1, 2 * NT)
    angles = np.concatenate([np.zeros((P, B), np.float32), np.broadcast_to(th, (2, S, 2 * NT)).reshape(P, 2 * NT)], 1)
    half = D // 2
    freqs = np.exp(np.arange(half, dtype=np.float32) * np.float32(-np.log(10000.0) / (half - 1)))
    lane = np.arange(P)
    laid = {
        "x_f": x.T, "x_t": x, "bias": bias, "mask": mask, "angles": angles,
        "ident": np.eye(P, dtype=np.float32), "iota_p": lane.astype(np.float32).reshape(P, 1),
        "iota_e": np.arange(E, dtype=np.float32).reshape(1, E),
        "parity": ((lane[:, None] // HD) % 2 == np.arange(2)[None, :]).astype(np.float32),
        "freqs": freqs.astype(np.float32).reshape(P, 1),
        "dom_i": row(a["itok_B_0_15"]), "time_i": row(a["itok_B_34_63"]), "sub_i": row(a["itok_B_6_14"]),
        "down_w": a["L0_cond_down_W"].T, "down_b": a["L0_cond_down_b"].reshape(A, 1),
        "up_w": np.concatenate([a["L0_cond_up_W"].T, row(a["L0_cond_up_b"])], 0),
        "exp_w": a["L0_cond_expert_W"].transpose(0, 2, 1), "exp_b": a["L0_cond_expert_b"],
        "dom_emb": a["L0_cond_domain_emb"], "gamma0": row(a["L0_cond_ln_gamma"]), "beta0": row(a["L0_cond_ln_beta"]),
        "w_ada": a["L1_cond_W_ada"], "b_ada": cols(a["L1_cond_b_ada"]),
        "wq": a["L1_cond_Wq"], "wk": a["L1_cond_Wk"], "wv": wv, "wo": a["L1_cond_Wo"],
        "bq": cols(a["L1_cond_bq"]), "bk": cols(a["L1_cond_bk"]), "bv": cols(a["L1_cond_bv"]), "bo": row(a["L1_cond_bo"]),
        "w1": a["L1_cond_W1"], "b1": cols(a["L1_cond_b1"]), "w2": a["L1_cond_W2"], "b2": row(a["L1_cond_b2"]),
        "g2": cols(a["L1_cond_g2"]), "beta2": cols(a["L1_cond_beta2"]),
        "ln_g": cols(a["L3_cond_ln_g"]), "ln_b": cols(a["L3_cond_ln_b"]), "subj_emb": a["L3_cond_subj_emb"],
        "hyp_w1": a["L3_cond_hyp_w1"], "hyp_b1": a["L3_cond_hyp_b1"].reshape(-1, 1),
        "hyp_w2": a["L3_cond_hyp_w2"], "hyp_b2": a["L3_cond_hyp_b2"].reshape(-1, 1),
        "sty_w1": a["L3_cond_sty_w1"], "sty_b1": a["L3_cond_sty_b1"].reshape(-1, 1),
        "sty_w2": a["L3_cond_sty_w2"], "sty_b2": cols(a["L3_cond_sty_b2"]), "router": a["L3_cond_router_w"],
        "lower": np.triu(np.ones((P, P), np.float32), 1), "iota_t": np.arange(TILES + 2, dtype=np.float32).reshape(1, -1),
        "tile_m": (np.arange(NT, dtype=np.float32) * P).reshape(1, -1),
        "region": (np.arange(E, dtype=np.float32) * CAP).reshape(1, -1),
        "tok_id": np.arange(N, dtype=np.int32).reshape(NT, P).T,
        "moe_w1": a["L3_cond_exp_w1"], "moe_w2": a["L3_cond_exp_w2"],
        "moe_b1": a["L3_cond_exp_b1"].reshape(E, KF, P).transpose(2, 0, 1), "moe_b2": a["L3_cond_exp_b2"],
    }
    nc = bacc.Bacc("TRN2", target_bir_lowering=False, num_devices=1)
    arrays, tensors = {}, {}
    for name, v in laid.items():
        arrays[f"in_{name}"] = c_(v)
        tensors[name] = nc.dram_tensor(f"in_{name}", v.shape, mybir.dt.from_np(v.dtype), kind="ExternalInput").ap()
    out = nc.dram_tensor("out_x", (N, D), F32, kind="ExternalOutput").ap()
    build(nc, tensors, out)
    r = run(nc, [arrays], core_ids=[0])
    return r.results[0]["out_x"].reshape(B, S, D)
```

```python
from contextlib import ExitStack

import numpy as np

import concourse.bass as bass
import concourse.mybir as mybir

F32 = mybir.dt.float32
I32 = mybir.dt.int32
U8 = mybir.dt.uint8
U32 = mybir.dt.uint32
F16 = mybir.dt.float16
ALU = mybir.AluOpType
ACT = mybir.ActivationFunctionType
AX = mybir.AxisListType

P = 128
B, S, D = 32, 64, 256
N = B * S
A = 64
NDOM = 16
H, HD = 16, 16
FF = 1024
E = 8
NSUB, SE, SH = 32, 64, 128
CT = 512
NCH = N // CT
CB = CT // S
TT = CT // P
NT = N // P
KD = D // P
KF = FF // P
HALF_PI = float(np.pi / 2)
INV_2PI = float(1.0 / (2 * np.pi))
ROUND = 12582912.0
TWO_PI_PARTS = (6.28125, 0.0019350051879882812, 3.0199159819460083e-07)
MASKED = -1.0e30
BANK_ORDER = (2, 3, 0, 1)
W_SCALE = 256.0
CAP = N + P
ROW = D + 4
TILES = (2 * N + E * (P - 1)) // P
NO_TOKEN = 1 << 24
STEPS = 6
TURNS = (TILES - 2) // STEPS
LEFT = 2 + TURNS * STEPS
ENTRIES = LEFT + STEPS
DIGIT = E
FIRST_HALF = 5
WE = 8192
RSQRT_SEED = 1597463007.0


COLS = (("iota_p", P, 1), ("parity", P, 2), ("freqs", P, 1), ("angles", P, B + 2 * NT), ("down_b", A, 1),
        ("b_ada", P, 2 * KD), ("bq", P, KD), ("bk", P, KD), ("bv", P, KD), ("b1", P, KF), ("g2", P, KD),
        ("beta2", P, KD), ("ln_g", P, KD), ("ln_b", P, KD), ("hyp_b1", SH, 1), ("hyp_b2", SH, 1),
        ("sty_b1", SH // 2, 1), ("sty_b2", P, 2 * KD), ("moe_b1", P, E * KF), ("iota_e", P, E),
        ("iota_t", P, ENTRIES), ("tile_m", P, NT), ("region", P, E))


class Count:

    def __init__(self, sem, per, start):
        self.sem, self.per, self.start = sem, per, start

    def of(self, c, n):
        return c * self.per + n + self.start


def build(nc, t, out):
    with ExitStack() as ctx:
        def sb(name, shape, dt=F32):
            return ctx.enter_context(nc.sbuf_tensor(name, shape, dt))

        def sem(name):
            return ctx.enter_context(nc.semaphore(name))

        def count(name, per):
            return Count(sem(name), per, 0)

        def free(name, per):
            return Count(sem(name), per, 1)

        bank = [ctx.enter_context(nc.psum_tensor(f"bank{i}", [P, 512], F32)) for i in range(8)]

        w_moe = sb("w_moe", [P, E * WE], F16)
        arena = w_moe[:].bitcast(F32)
        used = [0]

        def carve(*shape):
            n = int(np.prod(shape[1:]))
            ap = arena[0:shape[0], used[0]:used[0] + n]
            used[0] += n
            assert used[0] <= E * WE // 2, used
            names = "abcdef"[:len(shape) - 1]
            sizes = dict(zip(names, shape[1:]))
            return ap.rearrange(f"p ({' '.join(names)}) -> p {' '.join(names)}", **sizes)

        w_qkv = carve(P, KD, 3 * D)
        wq, wk, wv = (w_qkv[:, :, i * D:(i + 1) * D] for i in range(3))
        up_w = carve(A + 1, D)
        norm0 = carve(P, 2, D)
        gamma0, beta0 = norm0[:, 0], norm0[:, 1]
        x_f = carve(P, KD, CT)
        x_t = carve(P, TT, D)
        w_raw = carve(A, CB, A)
        w_sel = carve(A, CB, A)
        w_id = carve(A, CB, A)
        hid = carve(A, CT)
        hid2 = carve(A + 1, CT)
        y = carve(P, TT, D)
        xn1 = y
        q_f = carve(P, KD, CT)
        ada_t = q_f
        k_f = carve(P, KD, 2, CT)
        v_bd = carve(P, CB, H // 2, 2, HD)
        sc = [carve(P, 4, 2, 4, S) for u in range(2)]
        p_f = carve(P, 4, 2, 2, P)
        used[0] = FIRST_HALF * WE // 2
        wo = carve(P, KD, D)
        biases = carve(P, 2, D)
        bo, b2 = biases[:, 0], biases[:, 1]
        w1 = carve(P, KD, FF)
        x1 = carve(P, KD, CT)
        ctx_f = carve(P, KD, CT)
        x2 = carve(P, TT, D)
        x3 = x2
        xn2 = carve(P, TT, D)
        xn3 = xn2
        h_f = carve(P, KD, CT)
        x4 = h_f[:].rearrange("p k (i d) -> p (k i) d", d=D)
        ff = carve(P, KF, CT)
        rot = [ff[:, i].rearrange("p (n x e) -> p n x e", n=TT, e=2) for i in range(4)]
        h3 = sb("h3", [P, KD, CT])
        h0 = h3
        x4b = sb("x4b", [P, TT, D])
        x1_kept = sb("x1_kept", [P, KD, CT])

        cols = sb("cols", [P, sum(width for _, _, width in COLS)])
        col, at = {}, 0
        for name, rows_of_it, width in COLS:
            col[name] = cols[0:rows_of_it, at:at + width]
            at += width
        iota_p, parity, freqs, angle, down_b = (col[n] for n in ("iota_p", "parity", "freqs", "angles", "down_b"))
        b_ada, bq, bk, bv, b1 = (col[n] for n in ("b_ada", "bq", "bk", "bv", "b1"))
        g2, beta2, ln_g, ln_b = (col[n] for n in ("g2", "beta2", "ln_g", "ln_b"))
        hyp_b1, hyp_b2, sty_b1, sty_b2 = (col[n] for n in ("hyp_b1", "hyp_b2", "sty_b1", "sty_b2"))
        moe_b1 = col["moe_b1"].rearrange("p (e f) -> p e f", e=E)
        iota_e, iota_t, tile_m, region = (col[n] for n in ("iota_e", "iota_t", "tile_m", "region"))
        ints = sb("ints", [P, 3 * B + NT], I32)
        dom_i, time_i, sub_i, tok_id = (ints[:, 0:B], ints[:, B:2 * B], ints[:, 2 * B:3 * B], ints[:, 3 * B:])
        mats = sb("mats", [P, 3 * P + SH // 2])
        ident, lower, hyp_w2, sty_w1 = (mats[:, 0:P], mats[:, P:2 * P], mats[:, 2 * P:3 * P], mats[:, 3 * P:])
        domains = sb("domains", [NDOM, 2 * A])
        dom_emb, exp_b = domains[:, 0:A], domains[:, A:]
        down_w = sb("down_w", [P, KD, A])
        w_ada = sb("w_ada", [P, KD, 2 * D])
        w2 = sb("w2", [P, KF, D])
        subj_emb = sb("subj_emb", [NSUB, SE])
        hyp_w1 = sb("hyp_w1", [SE, SH])
        sty_w2 = sb("sty_w2", [SH // 2, 2 * D])
        router = sb("router", [P, KD, E])
        moe_b2 = sb("moe_b2", [E, D])
        mask_u8 = sb("mask_u8", [P, NT, S], U8)
        mask_add = sb("mask_add", [P, NT, S])

        dom_f = sb("dom_f", [P, B])
        dom_c = sb("dom_c", [P, B])
        dom_at = sb("dom_at", [1, B], I32)
        valid = sb("valid", [P, B])
        invalid = sb("invalid", [P, B])
        hot_dom = sb("hot_dom", [NDOM, B])
        hot_val = sb("hot_val", [NDOM, B])
        add_o = sb("add_o", [A, B])
        sub_f = sb("sub_f", [P, B])
        hot_sub = sb("hot_sub", [NSUB, B])
        se = sb("se", [SE, B])
        hyp1 = sb("hyp1", [SH, B])
        hyp2 = sb("hyp2", [SH, B])
        sty1 = sb("sty1", [SH // 2, B])
        sty = sb("sty", [P, 2 * KD, B])
        soft = sb("soft", [P, 4, KD, B])
        gamma3 = sb("gamma3", [P, KD, B])
        time_f = sb("time_f", [P, B])
        quot, q_hi, q_lo = sb("quot", [P, B]), sb("q_hi", [P, B]), sb("q_lo", [P, B])
        turns = sb("turns", [P, B + 2 * NT])
        cos_in = sb("cos_in", [P, B + 2 * NT])
        sin_t = sb("sin_t", [P, B + 2 * NT])
        cos_t = sb("cos_t", [P, B + 2 * NT])
        emb = sb("emb", [P, KD, B])
        ada = sb("ada", [P, 2 * KD, B])
        bq4 = sb("bq4", [P, KD])
        bkp = sb("bkp", [P, KD, 2])

        sc_max = [sb(f"sc_max{u}", [P, 32]) for u in range(2)]
        sc_sum = [sb(f"sc_sum{u}", [P, 32]) for u in range(2)]
        sc_inv = [sb(f"sc_inv{u}", [P, 32]) for u in range(2)]
        stats = sb("stats", [P, 16, 6])
        mv = sb("mv", [P, 16, 2])
        var = sb("var", [P, 16])
        rstd = sb("rstd", [P, 16])
        newton = sb("newton", [P, 16])
        newton2 = sb("newton2", [P, 16])
        in_a = sb("in_a", [P, 16])
        in_b = sb("in_b", [P, 16])
        logit = sb("logit", [P, TT, E])
        logit2 = sb("logit2", [P, TT, E])
        cand = sb("cand", [P, TT, E])
        hot1 = sb("hot1", [P, TT, E])
        hot2 = sb("hot2", [P, TT, E])
        top1 = sb("top1", [P, TT])
        top2 = sb("top2", [P, TT])
        first = sb("first", [P, TT])
        gap = sb("gap", [P, TT])
        gap_e = sb("gap_e", [P, TT])
        gate_d = sb("gate_d", [P, TT])
        gate1 = sb("gate1", [P, TT])
        gate2 = sb("gate2", [P, TT])
        gated1, gated2 = cand, logit2
        gate = sb("gate", [P, TT, E])
        gate_f = sb("gate_f", [E, CT])
        ones = sb("ones", [P, P])
        first1 = first
        first2 = sb("first2", [P, TT])
        picks = sb("picks", [P, TT + 1, E])
        seen = sb("seen", [P, E])
        next_row = sb("next_row", [P, E])
        place = sb("place", [P, TT, E])
        picked = sb("picked", [P, 2, TT, E])
        slot_f = sb("slot_f", [P, 2, TT])
        slot = sb("slot", [P, 2, TT], U32)
        disp = sb("disp", [P, TT, ROW])
        empty = sb("empty", [P, ROW])
        stage = sb("stage", [P, WE // 4])
        split = sb("split", [P, 2, WE // 4], F16)

        def split_of(q):
            if q % 2 == 0:
                return stage[:], split[:, 0, :], split[:, 1, :]
            rows_of = split[:].rearrange("p h n -> p (h n)").rearrange("p (f h d) -> p f h d", h=2, d=D)
            return stage[:].rearrange("p (f d) -> p f d", d=D), rows_of[:, :, 0, :], rows_of[:, :, 1, :]

        over = sb("over", [P, E, NT])
        n_tiles = sb("n_tiles", [P, E])
        ends = sb("ends", [P, E])
        past = sb("past", [P, ENTRIES, E])
        past_n = sb("past_n", [P, ENTRIES, E])
        tile_e = sb("tile_e", [P, ENTRIES])
        tile_s = sb("tile_s", [P, ENTRIES])
        tile_l = sb("tile_l", [P, ENTRIES])
        tile_r = sb("tile_r", [P, ENTRIES])
        tile_ei = sb("tile_ei", [1, ENTRIES], I32)
        digits = sb("digits", [P, TURNS + 1])
        turn_ei = sb("turn_ei", [1, TURNS + 1], I32)
        tile_ri = sb("tile_ri", [1, ENTRIES], I32)
        rest_i = sb("rest_i", [1, E], I32)
        xs = [sb(f"xs{j}", [P, ROW]) for j in range(2)]
        xs_f = [sb(f"xs_f{j}", [P, 4, P], F16) for j in range(2)]
        ident16 = sb("ident16", [P, P], F16)
        meta = sb("meta", [P, ENTRIES, 4])
        gates = sb("gates", [P, ENTRIES])
        h32 = [stage[:, j * KF * P:(j + 1) * KF * P].rearrange("p (f n) -> p f n", f=KF) for j in range(2)]
        halves_of = [split[:, :, 0:KF * P], split[:, :, KF * P:],
                     mask_add[:].bitcast(F16).rearrange("p n s -> p (n s)").rearrange("p (h n) -> p h n", h=2)]
        h_hi = [both[:, 0].rearrange("p (f n) -> p f n", f=KF) for both in halves_of]
        h_lo = [both[:, 1].rearrange("p (f n) -> p f n", f=KF) for both in halves_of]
        ys = [x1_kept[:, j, 0:D] for j in range(2)]
        ys_low = [x1_kept[:, j, D:2 * D] for j in range(2)]
        ids = [sb(f"ids{j}", [P, 1], U32) for j in range(2)]
        xs_dram = nc.dram_tensor("dispatched", (E * CAP + P, ROW), F32).ap()
        w_dram = nc.dram_tensor("w_split", (E, P, WE), F16).ap()

        early_in, cond_in, main_in = sem("early_in"), sem("cond_in"), sem("main_in")
        setup = sem("setup")
        setup_pe, setup_act = sem("setup_pe"), sem("setup_act")
        zeroed = sem("zeroed")
        dom_ready = sem("dom_ready")
        cond_ready = sem("cond_ready")
        mask_ready = sem("mask_ready")

        x_f_in, x_t_in = count("x_f_in", 16), count("x_t_in", 16)
        bias_in = [count(f"bias_in{u}", 16) for u in range(2)]
        w_sel_ready = count("w_sel_ready", 1)
        w_raw_in, w_step = count("w_raw_in", 16 * CB), free("w_step", 2)
        down_done, hid_ready = free("down_done", 1), count("hid_ready", 1)
        expert_done, hid2_ready = free("expert_done", 1), count("hid2_ready", 1)
        up_done, y_ready = count("up_done", 2), free("y_ready", 2)
        xn1_ready, turn1_done = count("xn1_ready", 1), count("turn1_done", 2)
        ada_scaled, x1_ready = count("ada_scaled", 2), count("x1_ready", 2)
        q_done, q_ready = count("q_done", 2), count("q_ready", 2)
        k_done, k_ready = count("k_done", 2), count("k_ready", 2)
        kept_ready = free("kept_ready", 1)
        v_done, v0_ready, v1_ready = free("v_done", 2), count("v0_ready", 2), count("v1_ready", 2)
        bias_masked = [count(f"bias_masked{u}", 4) for u in range(2)]
        score_done = [count(f"score_done{u}", 4) for u in range(2)]
        biased = [free(f"biased{u}", 4) for u in range(2)]
        max_ready = [count(f"max_ready{u}", 1) for u in range(2)]
        shifted = [count(f"shifted{u}", 1) for u in range(2)]
        exp_ready = [count(f"exp_ready{u}", 1) for u in range(2)]
        inv_ready = [count(f"inv_ready{u}", 1) for u in range(2)]
        prob_ready = [count(f"prob_ready{u}", 1) for u in range(2)]
        prob_turned = [free(f"prob_turned{u}", 4) for u in range(2)]
        p_f_ready = [count(f"p_f_ready{u}", 4) for u in range(2)]
        ctx_done = [count(f"ctx_done{u}", 1) for u in range(2)]
        ctx_ready = [count(f"ctx_ready{u}", 2) for u in range(2)]
        wo_done, x2_ready = free("wo_done", 2), count("x2_ready", 2)
        x2b_ready = count("x2b_ready", 1)
        xn2_ready, turn2_done, h_ready = count("xn2_ready", 1), count("turn2_done", 2), count("h_ready", 2)
        ff1_done, ff_ready = count("ff1_done", KF), count("ff_ready", KF)
        ff2_done, x3_ready = count("ff2_done", 2), count("x3_ready", 2)
        rot_step, odd_ready = count("rot_step", 2), count("odd_ready", 1)
        xn3_ready, turn3_done, h0_ready = count("xn3_ready", 1), count("turn3_done", 2), count("h0_ready", 2)
        h3_ready = count("h3_ready", 1)
        logit_done, gap_ready, gap_exp = count("logit_done", 1), count("gap_ready", 1), count("gap_exp", 1)
        gate_ready, gate_turned, gate_f_ready = count("gate_ready", 1), count("gate_turned", 1), count("gate_f_ready", 1)
        b2_done, acc_ready = count("b2_done", 2), free("acc_ready", 2)
        adapter_step, attention_step = count("adapter_step", 24), count("attention_step", 2)
        second_step = count("second_step", 58)

        picks_ready, rank_done = count("picks_ready", 1), count("rank_done", 1)
        slot_ready = free("slot_ready", 1)
        rows_done, rows_hi, rows_ready = count("rows_done", 2), count("rows_hi", 2), free("rows_ready", 2)
        disp_ready = count("disp_ready", 1)
        xs_out = Count(sem("xs_out"), 16 * 2 * TT, 16)
        x_stored, rows_sent = free("x_stored", 16), free("rows_sent", 1)
        stage_in, split_hi, split_lo = count("stage_in", 64), count("split_hi", 4), free("split_lo", 4)
        w_out = free("w_out", 64)
        plan, plan_ready, rest_ready, rest_out = sem("plan"), sem("plan_ready"), sem("rest_ready"), sem("rest_out")
        weights_in = sem("weights_in")
        xs_in = [sem(f"xs_in{j}") for j in range(2)]
        turned, xs_f_ready = sem("turned"), sem("xs_f_ready")
        gate_step, gates_ready = sem("gate_step"), sem("gates_ready")
        m1_done, h32_ready, hi_ready, lo_ready = sem("m1_done"), sem("h32_ready"), sem("hi_ready"), sem("lo_ready")
        m2_done, ys_low_ready, ys_ready, ids_ready = sem("m2_done"), sem("ys_low_ready"), sem("ys_ready"), sem("ids_ready")
        rows_out, added = sem("rows_out"), sem("added")

        early = [
            (ints, t["ints"]), (cols, t["cols"]), (domains, t["domains"]), (mats, t["mats"]),
            (down_w, t["down_w"].rearrange("(k p) a -> p k a", p=P)),
        ]
        cond = [
            (up_w, t["up_w"]), (norm0, t["norm0"].broadcast_to([P, 2, D])), (subj_emb, t["subj_emb"]),
            (hyp_w1, t["hyp_w1"]), (sty_w2, t["sty_w2"]), (w_ada, t["w_ada"].rearrange("(k p) n -> p k n", p=P)),
        ]
        main = [
            (w_qkv, t["w_qkv"].rearrange("(k p) n -> p k n", p=P)), (wo, t["wo"].rearrange("(k p) n -> p k n", p=P)),
            (biases, t["biases"].broadcast_to([P, 2, D])), (w1, t["w1"].rearrange("(k p) n -> p k n", p=P)),
            (w2, t["w2"].rearrange("(k p) n -> p k n", p=P)),
            (router, t["router"].rearrange("(k p) n -> p k n", p=P)), (moe_b2, t["moe_b2"]),
        ]
        N_EARLY, N_COND, N_MAIN = 16 * len(early), 16 * len(cond), 16 * len(main)

        block = ctx.enter_context(nc.Block())

        @block.sync
        def _(sp):
            sp.sem_inc(w_out.sem, 1)
            for dst, src in early:
                sp.dma_start(dst[:], src).then_inc(early_in, 16)
            def load_x(c):
                sp.wait_ge(down_done.sem, down_done.of(c, 0))
                sp.dma_start(x_f[:], t["x_f"].rearrange("(k p) n -> p k n", p=P)[:, :, bass.ds(c * CT, CT)]
                             ).then_inc(x_f_in.sem, 16)
                sp.wait_ge(dom_ready, 1)
                sp.wait_ge(w_step.sem, w_step.of(c, 0))
                _, chosen = nc.values_load_multi_w_load_instructions(
                    dom_at[0:1, bass.ds(c * CB, CB)], engines=[mybir.EngineType.SP], min_val=0, max_val=NDOM - 1)
                for b in range(CB):
                    sp.dma_start(w_raw[:, b, :], t["exp_w"][bass.ds(chosen[b], 1), :, :].rearrange("e a o -> a (e o)")
                                 ).then_inc(w_raw_in.sem, 16)
                sp.wait_ge(y_ready.sem, y_ready.of(c, 0))
                sp.dma_start(x_t[:], t["x_t"].rearrange("(n p) d -> p n d", p=P)[:, bass.ds(c * TT, TT), :]
                             ).then_inc(x_t_in.sem, 16)

            def load_bias(c):
                for u in range(2):
                    sp.wait_ge(prob_turned[u].sem, prob_turned[u].of(c, 0))
                    sp.dma_start(sc[u][:].rearrange("p r a h k -> p (r a h k)"),
                                 t["bias"][bass.ds(c * 2 + u, 1), :, :].rearrange("s p n -> (s p) n")
                                 ).then_inc(bias_in[u].sem, 16)

            def load_part(c, q):
                sp.wait_ge(split_lo.sem, split_lo.of(c, q))
                w_part = t["moe_w1"] if q % 2 == 0 else t["moe_w2"]
                sp.dma_start(stage[:].rearrange("p (k n) -> p k n", k=KD if q % 2 == 0 else KF),
                             w_part[bass.ds(c * 2 + q // 2, 1), :, :].rearrange("e (k p) n -> p (e k) n", p=P)
                             ).then_inc(stage_in.sem, 16)

            def store_part(c, q):
                sp.wait_ge(split_lo.sem, split_lo.of(c, q + 1))
                sp.dma_start(w_dram[bass.ds(c * 2 + q // 2, 1), :, q % 2 * (WE // 2):(q % 2 + 1) * (WE // 2)]
                             .rearrange("e p n -> p (e n)"), split[:].rearrange("p h n -> p (h n)")
                             ).then_inc(w_out.sem, 16)

            def pass_parts(c):
                for q in range(3):
                    load_part(c, q)
                    store_part(c, q)
                load_part(c, 3)

            load_x(0)
            load_bias(0)
            load_x(1)
            pass_parts(0)
            with sp.Fori(0, NCH - 2) as c:
                load_x(c + 2)
                load_bias(c + 1)
                store_part(c, 3)
                pass_parts(c + 1)
            load_bias(NCH - 1)
            store_part(NCH - 2, 3)
            pass_parts(NCH - 1)
            store_part(NCH - 1, 3)

            def load_weights(first, last):
                with sp.Fori(first, last) as e:
                    sp.wait_ge(weights_in, e * 16)
                    sp.dma_start(w_moe[:, bass.ds(e * WE, WE)], w_dram[bass.ds(e, 1), :, :].rearrange("e p n -> p (e n)")
                                 ).then_inc(weights_in, 16)

            sp.wait_ge(w_out.sem, w_out.of(NCH, 0))
            sp.wait_ge(ctx_ready[1].sem, ctx_ready[1].of(NCH, 0))
            sp.dma_start(w_moe[:, 0:WE], w_dram[0]).then_inc(weights_in, 16)
            load_weights(1, FIRST_HALF)
            sp.dma_start(xs_dram[E * CAP:E * CAP + P, :], empty[:]).then_inc(rest_out, 16)
            sp.wait_ge(rest_ready, 1)
            _, rests = nc.values_load_multi_w_load_instructions(
                rest_i[0:1, :], engines=[mybir.EngineType.SP], min_val=0, max_val=E * CAP - P)
            for rest in rests:
                sp.dma_start(xs_dram[bass.ds(rest, P), :], empty[:]).then_inc(rest_out, 16)
            sp.wait_ge(x_stored.sem, x_stored.of(NCH, 0))
            load_weights(FIRST_HALF, E)
            sp.wait_ge(weights_in, 16 * E)

        @block.gpsimd
        def _(pool):
            pool.dma_start(mask_u8[:], t["mask"]).then_inc(xs_out.sem, 16)
            pool.sem_inc(w_step.sem, 1)
            def select(c):
                pool.wait_ge(expert_done.sem, expert_done.of(c, 0))
                pool.wait_ge(w_raw_in.sem, w_raw_in.of(c, 16 * CB))
                pool.tensor_tensor(w_sel[:], w_raw[:],
                                   valid[0:A, bass.ds(c * CB, CB)].unsqueeze(2).broadcast_to([A, CB, A]),
                                   ALU.mult).then_inc(w_step.sem, 1)
                pool.tensor_tensor(w_id[:], ident[0:A, 0:A].unsqueeze(1).broadcast_to([A, CB, A]),
                                   invalid[0:A, bass.ds(c * CB, CB)].unsqueeze(2).broadcast_to([A, CB, A]),
                                   ALU.mult).then_inc(w_step.sem, 1)
                pool.wait_ge(w_step.sem, w_step.of(c, 2))
                pool.tensor_tensor(w_sel[:], w_sel[:], w_id[:], ALU.add).then_inc(w_sel_ready.sem, 1)

            def mask(c):
                for u in range(2):
                    pool.wait_ge(bias_in[u].sem, bias_in[u].of(c, 16))
                    for r in BANK_ORDER:
                        pool.tensor_tensor(
                            sc[u][:, r], sc[u][:, r],
                            mask_add[:, bass.ds(c * TT + 2 * u, 2), :].unsqueeze(2).broadcast_to([P, 2, 4, S]),
                            ALU.add).then_inc(bias_masked[u].sem, 1)

            def shift_norm(c):
                for k in range(KD):
                    pool.wait_ge(ada_scaled.sem, ada_scaled.of(c, k + 1))
                    if k == 0:
                        pool.wait_ge(v_done.sem, v_done.of(c, 0))
                        pool.wait_ge(kept_ready.sem, kept_ready.of(c, 0))
                    pool.tensor_tensor(
                        x1[:, k, :].rearrange("p (b s) -> p b s", s=S),
                        ada_t[:, k, :].rearrange("p (b s) -> p b s", s=S),
                        ada[:, KD + k, bass.ds(c * CB, CB)].unsqueeze(2).broadcast_to([P, CB, S]),
                        ALU.add).then_inc(x1_ready.sem, 1)

            def less_maximum(c, u):
                pool.wait_ge(max_ready[u].sem, max_ready[u].of(c, 1))
                v = sc[u][:].rearrange("p r a h k -> p (r a h) k")
                pool.tensor_tensor(v, v, sc_max[u][:].unsqueeze(2).broadcast_to([P, 32, S]),
                                   ALU.subtract).then_inc(shifted[u].sem, 1)

            def probabilities(c, u):
                pool.wait_ge(inv_ready[u].sem, inv_ready[u].of(c, 1))
                v = sc[u][:].rearrange("p r a h k -> p (r a h) k")
                pool.tensor_tensor(v, v, sc_inv[u][:].unsqueeze(2).broadcast_to([P, 32, S]),
                                   ALU.mult).then_inc(prob_ready[u].sem, 1)

            def residual(c):
                pool.wait_ge(xn2_ready.sem, xn2_ready.of(c, 1))
                pool.tensor_tensor(x2[:], x2[:], b2[:].unsqueeze(1).broadcast_to([P, TT, D]),
                                   ALU.add).then_inc(x2b_ready.sem, 1)

            def rotate_odd(c):
                pool.wait_ge(x3_ready.sem, x3_ready.of(c, 2))
                v3 = x3[:].rearrange("p n (i a e) -> p n i a e", a=2, e=2)
                v4 = x4[:].rearrange("p n (i a e) -> p n i a e", a=2, e=2)
                cs = cos_t[:, bass.ds(B + c * TT * 2, TT * 2)].rearrange("p (n a) -> p n a", a=2)
                sn = sin_t[:, bass.ds(B + c * TT * 2, TT * 2)].rearrange("p (n a) -> p n a", a=2)
                cs = cs.unsqueeze(2).broadcast_to([P, TT, S, 2])
                sn = sn.unsqueeze(2).broadcast_to([P, TT, S, 2])
                pool.tensor_tensor(rot[2], v3[:, :, :, :, 1], cs, ALU.mult).then_inc(rot_step.sem, 1)
                pool.tensor_tensor(rot[3], v3[:, :, :, :, 0], sn, ALU.mult).then_inc(rot_step.sem, 1)
                pool.wait_ge(rot_step.sem, rot_step.of(c, 2))
                pool.tensor_tensor(v4[:, :, :, :, 1], rot[2], rot[3], ALU.subtract).then_inc(odd_ready.sem, 1)

            def dispatch(c):
                pool.wait_ge(slot_ready.sem, slot_ready.of(c, 1))
                pool.wait_ge(disp_ready.sem, disp_ready.of(c, 1))
                pool.wait_ge(rows_ready.sem, rows_ready.of(c, 2))
                pool.nop(nofuse=True)
                for i in range(TT):
                    for a in range(2):
                        pool.indirect_dma_start(
                            out=xs_dram[:, :], out_offset=bass.IndirectOffsetOnAxis(ap=slot[:, a, i:i + 1], axis=0),
                            in_=disp[:, i, :], in_offset=None).then_inc(xs_out.sem, 16)

            def confirm(c):
                pool.wait_ge(xs_out.sem, xs_out.of(c, 0))
                pool.sem_inc(rows_sent.sem, 1)

            pool.wait_ge(setup, SETUP_DOM)
            select(0)
            pool.wait_ge(xs_out.sem, xs_out.of(0, 0))
            pool.tensor_scalar(mask_add[:], mask_u8[:], MASKED, None, ALU.mult).then_inc(mask_ready, 1)
            pool.wait_ge(mask_ready, 1)
            mask(0)
            pool.wait_ge(cond_ready, 1)
            shift_norm(0)
            select(1)
            less_maximum(0, 0)
            less_maximum(0, 1)
            probabilities(0, 0)
            probabilities(0, 1)
            shift_norm(1)
            pool.wait_ge(main_in, N_MAIN)
            def beside(c, adapter):
                if adapter:
                    select(c + 2)
                residual(c)
                mask(c + 1)
                confirm(c)
                less_maximum(c + 1, 0)
                less_maximum(c + 1, 1)
                rotate_odd(c)
                if adapter:
                    shift_norm(c + 2)
                probabilities(c + 1, 0)
                probabilities(c + 1, 1)
                dispatch(c)

            with pool.Fori(0, NCH - 2) as c:
                beside(c, True)
            beside(NCH - 2, False)
            residual(NCH - 1)
            confirm(NCH - 1)
            rotate_odd(NCH - 1)
            dispatch(NCH - 1)
            confirm(NCH)

            pool.wait_ge(x_stored.sem, x_stored.of(NCH, 0))

            def add_rows(n, j):
                pool.wait_ge(gates_ready, n + 1)
                pool.nop(nofuse=True)
                pool.tensor_copy(ids[j][:], meta[:, bass.ds(n, 1), 0].bitcast(U32)).then_inc(ids_ready, 1)
                pool.wait_ge(ids_ready, n + 1)
                pool.wait_ge(ys_ready, n + 3)
                pool.nop(nofuse=True)
                pool.indirect_dma_start(
                    out=out[:, :], out_offset=bass.IndirectOffsetOnAxis(ap=ids[j][:, 0:1], axis=0),
                    in_=ys[j], in_offset=None, bounds_check=N - 1, oob_is_err=False,
                    compute_op=ALU.add).then_inc(rows_out, 16)
                pool.wait_ge(rows_out, n * 16 + 16)
                pool.nop(nofuse=True)
                pool.sem_inc(added, 1)

            pool.sem_inc(added, 2)
            with pool.Fori(0, TILES // 2) as i:
                for j in range(2):
                    add_rows(i * 2 + j, j)
            if TILES % 2:
                add_rows(TILES - 1, 0)

        @block.scalar
        def _(act):
            def hidden(c):
                act.wait_ge(down_done.sem, down_done.of(c, 1))
                act.activation(hid[:], bank[2][0:A, :], ACT.Gelu, bias=down_b[:, 0:1]).then_inc(hid_ready.sem, 1)

            def split_high(c, q):
                act.wait_ge(stage_in.sem, stage_in.of(c, 16 * (q + 1)))
                act.wait_ge(w_out.sem, w_out.of(c, 16 * q))
                part, high, _ = split_of(q)
                act.activation(high, part, ACT.Copy, scale=W_SCALE).then_inc(split_hi.sem, 1)

            def queries(c):
                for m in range(KD):
                    act.wait_ge(q_done.sem, q_done.of(c, m + 1))
                    act.activation(q_f[:, m, :], bank[m][:], ACT.Identity, bias=bq4[:, m:m + 1],
                                   scale=0.25).then_inc(q_ready.sem, 1)

            def keys(c):
                for m in range(KD):
                    act.wait_ge(k_done.sem, k_done.of(c, m + 1))
                    for a in range(2):
                        ins = act.activation(k_f[:, m, a, :], bank[2 + m][:], ACT.Identity, bias=bkp[:, m, a:a + 1],
                                             scale=parity[:, a:a + 1])
                    ins.then_inc(k_ready.sem, 1)

            def values(c):
                act.wait_ge(v_done.sem, v_done.of(c, 1))
                for s in range(2):
                    act.activation(v_bd[64 * s:64 * s + 64, 0:4, :, s, :].rearrange("p b j d -> p (b j) d"),
                                   bank[0][64 * s:64 * s + 64, :].rearrange("p (j d) -> p j d", d=HD),
                                   ACT.Copy).then_inc(v0_ready.sem, 1)

            def keep(c):
                act.wait_ge(x1_ready.sem, x1_ready.of(c, 2))
                act.wait_ge(wo_done.sem, wo_done.of(c, 0))
                act.activation(x1_kept[:], x1[:], ACT.Copy).then_inc(kept_ready.sem, 1)

            def exponentials(c, u):
                act.wait_ge(shifted[u].sem, shifted[u].of(c, 1))
                act.activation(sc[u][:], sc[u][:], ACT.Exp).then_inc(exp_ready[u].sem, 1)

            def context(c, u):
                for r in range(4):
                    act.wait_ge(prob_turned[u].sem, prob_turned[u].of(c, r + 1))
                    act.activation(p_f[:, r].rearrange("p a h q -> p (a h q)"), bank[r % 2][:],
                                   ACT.Copy).then_inc(p_f_ready[u].sem, 1)
                act.wait_ge(ctx_done[u].sem, ctx_done[u].of(c, 1))
                for k in range(KD):
                    act.activation(ctx_f[:, k, 256 * u:256 * u + 256], bank[2 + u][:, 256 * k:256 * k + 256],
                                   ACT.Identity, bias=bv[:, k:k + 1]).then_inc(ctx_ready[u].sem, 1)

            def feed_forward_in(c):
                for k in range(KD):
                    act.wait_ge(turn2_done.sem, turn2_done.of(c, k + 1))
                    act.activation(h_f[:, k, :], bank[4 + k][:], ACT.Identity, bias=beta2[:, k:k + 1],
                                   scale=g2[:, k:k + 1]).then_inc(h_ready.sem, 1)

            def feed_forward(c, some):
                for f in some:
                    act.wait_ge(ff1_done.sem, ff1_done.of(c, f + 1))
                    act.activation(ff[:, f, :], bank[4 + f % 2][:], ACT.Gelu_apprx_sigmoid,
                                   bias=b1[:, f:f + 1]).then_inc(ff_ready.sem, 1)

            def norm3(c):
                for k in range(KD):
                    act.wait_ge(turn3_done.sem, turn3_done.of(c, k + 1))
                    act.activation(h0[:, k, :], bank[4 + k][:], ACT.Identity, bias=ln_b[:, k:k + 1],
                                   scale=ln_g[:, k:k + 1]).then_inc(h0_ready.sem, 1)

            def token_gates(c):
                act.wait_ge(gap_ready.sem, gap_ready.of(c, 1))
                act.activation(gap_e[:], gap[:], ACT.Exp).then_inc(gap_exp.sem, 1)

            def rows(c):
                act.wait_ge(rows_sent.sem, rows_sent.of(c, 0))
                for g in range(2):
                    act.wait_ge(rows_done.sem, rows_done.of(c, g + 1))
                    act.activation(disp[:, 2 * g:2 * g + 2, 0:P].bitcast(F16),
                                   bank[4 + g][:].rearrange("p (i d) -> p i d", d=D), ACT.Copy).then_inc(rows_hi.sem, 1)

            act.sem_inc(x_stored.sem, 1)
            act.sem_inc(kept_ready.sem, 1)
            for dst, src in cond:
                act.dma_start(dst[:], src).then_inc(cond_in, 16)
            for dst, src in main:
                act.dma_start(dst[:], src).then_inc(main_in, 16)
            def store(c):
                act.wait_ge(acc_ready.sem, acc_ready.of(c, 2))
                act.dma_start(out.rearrange("(n p) d -> p n d", p=P)[:, bass.ds(c * TT, TT), :], x4b[:]
                              ).then_inc(x_stored.sem, 16)

            hidden(0)
            act.wait_ge(setup, SETUP_ANGLES)
            act.activation(sin_t[:], angle[:], ACT.Sin).then_inc(setup_act, 1)
            act.activation(cos_t[:], cos_in[:], ACT.Sin).then_inc(setup_act, 1)
            act.wait_ge(setup_act, 2)
            act.activation(emb[:, 0, :], sin_t[:, 0:B], ACT.Silu).then_inc(setup_act, 1)
            act.activation(emb[:, 1, :], cos_t[:, 0:B], ACT.Silu).then_inc(setup_act, 1)
            act.wait_ge(setup, SETUP_ABS)
            act.activation(soft[:, 1], soft[:, 0], ACT.Exp).then_inc(setup_act, 1)
            act.wait_ge(setup, SETUP_ABS + 1)
            act.activation(soft[:, 3], soft[:, 2], ACT.Ln).then_inc(setup_act, 1)
            act.wait_ge(main_in, N_MAIN)
            split_high(0, 0)
            queries(0)
            keys(0)
            values(0)
            keep(0)
            split_high(0, 1)
            exponentials(0, 0)
            hidden(1)
            exponentials(0, 1)
            split_high(0, 2)
            context(0, 0)
            context(0, 1)
            split_high(0, 3)
            queries(1)
            keys(1)
            keep(1)

            def beside(c, adapter):
                values(c + 1)
                feed_forward_in(c)
                if adapter:
                    hidden(c + 2)
                feed_forward(c, range(KF))
                split_high(c + 1, 0)
                exponentials(c + 1, 0)
                split_high(c + 1, 1)
                exponentials(c + 1, 1)
                split_high(c + 1, 2)
                if adapter:
                    queries(c + 2)
                norm3(c)
                if adapter:
                    keys(c + 2)
                context(c + 1, 0)
                context(c + 1, 1)
                token_gates(c)
                rows(c)
                split_high(c + 1, 3)
                if adapter:
                    keep(c + 2)
                store(c)

            with act.Fori(0, NCH - 2) as c:
                beside(c, True)
            beside(NCH - 2, False)
            feed_forward_in(NCH - 1)
            feed_forward(NCH - 1, range(KF))
            norm3(NCH - 1)
            token_gates(NCH - 1)
            rows(NCH - 1)
            store(NCH - 1)

            def values_of(table, n, count, most):
                _, values = nc.values_load_multi_w_load_instructions(
                    table[0:1, bass.ds(n, count)], engines=[mybir.EngineType.Activation], min_val=0, max_val=most)
                return values

            def load_rows(r, j, e):
                act.wait_ge(weights_in, e * 16 + 16)
                act.dma_start(xs[j][:], xs_dram[bass.ds(r, P), :]).then_inc(xs_in[j], 16)

            def hidden(n, j, e, g):
                act.wait_ge(m1_done, n * 2 + g + 1)
                act.nop(nofuse=True)
                for f in range(4 * g, 4 * g + 4):
                    ins = act.activation(h32[j][:, f, :], bank[2 * j + g][:, P * (f % 4):P * (f % 4) + P], ACT.Relu,
                                         bias=moe_b1[:, bass.ds(e, 1), f], scale=1.0 / W_SCALE)
                ins.then_inc(h32_ready, 1)

            def scaled(n, j):
                act.wait_ge(m2_done, n + 1)
                act.wait_ge(gates_ready, n + 1)
                act.wait_ge(ys_ready, n + 1)
                act.nop(nofuse=True)
                act.activation(ys_low[j], bank[4 + j][:, D:2 * D], ACT.Copy, scale=gates[:, bass.ds(n, 1)]
                               ).then_inc(ys_low_ready, 1)

            act.wait_ge(plan_ready, 1)
            def rows_after(n, j, r, e):
                act.wait_ge(xs_f_ready, n + 1)
                act.wait_ge(gates_ready, n + 1)
                load_rows(r, j, e)

            row_at = values_of(tile_ri, 0, 4, E * CAP)
            expert = values_of(tile_ei, 0, 4, E - 1)
            act.wait_ge(rest_out, 16 * (E + 1))
            act.wait_ge(rows_sent.sem, rows_sent.of(NCH, 0))
            for n in range(2):
                load_rows(row_at[n], n, expert[n])
            for n in range(2):
                rows_after(n, n, row_at[n + 2], expert[n + 2])
                hidden(n, n, expert[n], 0)
                hidden(n, n, expert[n], 1)
            with act.Fori(0, TURNS) as i:
                row_at = values_of(tile_ri, i * STEPS + 4, STEPS, E * CAP)
                expert = values_of(tile_ei, i * STEPS + 2, STEPS + 2, E - 1)
                for j in range(STEPS):
                    rows_after(i * STEPS + j + 2, j % 2, row_at[j], expert[j + 2])
                    hidden(i * STEPS + j + 2, j % 2, expert[j], 0)
                    scaled(i * STEPS + j, j % 2)
                    hidden(i * STEPS + j + 2, j % 2, expert[j], 1)
            row_at = values_of(tile_ri, LEFT + 2, TILES - LEFT, E * CAP)
            expert = values_of(tile_ei, LEFT, TILES - LEFT + 2, E - 1)
            for n in range(LEFT, TILES):
                rows_after(n, n % 2, row_at[n - LEFT], expert[n - LEFT + 2])
                hidden(n, n % 2, expert[n - LEFT], 0)
                scaled(n - 2, n % 2)
                hidden(n, n % 2, expert[n - LEFT], 1)
            for n in range(TILES - 2, TILES):
                scaled(n, n % 2)
            act.wait_ge(xs_in[TILES % 2], 16 * (TILES // 2 + 1))
            act.wait_ge(xs_in[(TILES + 1) % 2], 16 * ((TILES + 1) // 2 + 1))

        @block.vector
        def _(dve):
            for free_at_first in (y_ready, slot_ready, acc_ready, rows_ready, split_lo, biased[0], biased[1]):
                dve.sem_inc(free_at_first.sem, 1)
            done = [0]

            def step(ins):
                done[0] += 1
                ins.then_inc(setup, 1)
                dve.wait_ge(setup, done[0])

            dve.memset(v_bd[:], 0.0).then_inc(zeroed, 1)
            dve.memset(hid2[A:A + 1, :], 1.0).then_inc(zeroed, 1)
            dve.memset(ones[:], 1.0).then_inc(zeroed, 1)
            dve.memset(picks[:, TT, :], 0.0).then_inc(zeroed, 1)
            dve.memset(empty[:].bitcast(U32), 0).then_inc(zeroed, 1)
            dve.wait_ge(zeroed, 5)
            dve.memset(empty[:, D:D + 1].bitcast(U32), NO_TOKEN).then_inc(zeroed, 1)
            dve.wait_ge(early_in, N_EARLY)
            dve.tensor_copy(ident16[:], ident[:]).then_inc(zeroed, 1)
            dve.tensor_copy(next_row[:], region[:]).then_inc(zeroed, 1)
            step(dve.tensor_copy(dom_f[:], dom_i[:]))
            step(dve.tensor_scalar(dom_c[:], dom_f[:], 0.0, float(NDOM - 1), ALU.max, ALU.min))
            dve.tensor_copy(dom_at[:], dom_c[0:1, :]).then_inc(dom_ready, 1)
            step(dve.tensor_tensor(valid[:], dom_f[:], dom_c[:], ALU.is_equal))
            step(dve.tensor_scalar(hot_dom[:], dom_c[0:NDOM, :], iota_p[0:NDOM, 0:1], None, ALU.is_equal))
            step(dve.tensor_tensor(hot_val[:], hot_dom[:], valid[0:NDOM, :], ALU.mult))
            step(dve.tensor_scalar(invalid[:], valid[:], -1.0, 1.0, ALU.mult, ALU.add))
            dve.wait_ge(setup_pe, 1)
            step(dve.tensor_copy(add_o[:], bank[7][0:A, 0:B]))
            assert done[0] == SETUP_DOM
            dve.wait_ge(zeroed, 8)
            def split_low(c, q):
                dve.wait_ge(split_hi.sem, split_hi.of(c, q + 1))
                part, high, low = split_of(q)
                dve.scalar_tensor_tensor(low, part, W_SCALE, high, ALU.mult, ALU.subtract).then_inc(split_lo.sem, 1)

            def stepper(step, c):
                n = [0]

                def vec(ins):
                    n[0] += 1
                    ins.then_inc(step.sem, 1)
                    dve.wait_ge(step.sem, step.of(c, n[0]))

                def finish():
                    assert n[0] == step.per, (n, step.per)
                return vec, finish

            def rsqrt(vec, w, eps):
                v, r, a, b = var[:, 0:w], rstd[:, 0:w], newton[:, 0:w], newton2[:, 0:w]
                vec(dve.tensor_scalar(v, mv[:, 0:w, 1], eps, None, ALU.add))
                vec(dve.tensor_scalar(r.bitcast(I32), v.bitcast(I32), -0.5, RSQRT_SEED, ALU.mult, ALU.add))
                vec(dve.scalar_tensor_tensor(a, r, 0.375 ** 0.5, r, ALU.mult, ALU.mult))
                vec(dve.tensor_tensor(b, a, v, ALU.mult))
                vec(dve.scalar_tensor_tensor(a, b, -10 / 3 * 0.375 ** 0.5, b, ALU.add, ALU.mult))
                vec(dve.scalar_tensor_tensor(r, a, 1.875, r, ALU.add, ALU.mult))
                vec(dve.scalar_tensor_tensor(a, r, -0.5, r, ALU.mult, ALU.mult))
                vec(dve.tensor_tensor(b, a, v, ALU.mult))
                vec(dve.scalar_tensor_tensor(r, b, 1.5, r, ALU.add, ALU.mult))

            def token_stats(vec, z):
                for i in range(TT):
                    ins = dve.bn_stats(stats[:, i, :], z[:, i, :])
                vec(ins)
                dve.nop(nofuse=True)
                for i in range(TT):
                    ins = dve.bn_aggr(mv[:, i, :], stats[:, i, :])
                vec(ins)
                rsqrt(vec, TT, 1e-5)

            def normalise(dst, z):
                for i in range(TT):
                    ins = dve.tensor_scalar(dst[:, i, :], z[:, i, :], mv[:, i, 0:1], rstd[:, i:i + 1],
                                            ALU.subtract, ALU.mult)
                return ins

            def adapter(c):
                vec, finish = stepper(adapter_step, c)

                def hidden():
                    dve.wait_ge(expert_done.sem, expert_done.of(c, 1))
                    dve.tensor_tensor(hid2[0:A, :].rearrange("p (b s) -> p b s", s=S),
                                      bank[3][0:A, :].rearrange("p (b s) -> p b s", s=S),
                                      add_o[:, bass.ds(c * CB, CB)].unsqueeze(2).broadcast_to([A, CB, S]),
                                      ALU.add).then_inc(hid2_ready.sem, 1)

                def residual():
                    dve.wait_ge(x_t_in.sem, x_t_in.of(c, 16))
                    for g in range(2):
                        dve.wait_ge(up_done.sem, up_done.of(c, g + 1))
                        dve.tensor_tensor(y[:, 2 * g:2 * g + 2, :], bank[2 + g][:].rearrange("p (n d) -> p n d", d=D),
                                          x_t[:, 2 * g:2 * g + 2, :], ALU.add).then_inc(y_ready.sem, 1)

                def norms():
                    dve.wait_ge(y_ready.sem, y_ready.of(c, 2))
                    token_stats(vec, y)
                    for i in range(TT):
                        ins = dve.scalar_tensor_tensor(y[:, i, :], y[:, i, :], mv[:, i, 0:1], gamma0[:],
                                                       ALU.subtract, ALU.mult)
                    vec(ins)
                    for i in range(TT):
                        ins = dve.scalar_tensor_tensor(y[:, i, :], y[:, i, :], rstd[:, i:i + 1], beta0[:],
                                                       ALU.mult, ALU.add)
                    vec(ins)
                    token_stats(vec, y)
                    normalise(xn1, y).then_inc(xn1_ready.sem, 1)
                    finish()

                return hidden, residual, norms

            def attention(c):
                vec, finish = stepper(attention_step, c)

                def scale_norm():
                    for k in range(KD):
                        dve.wait_ge(turn1_done.sem, turn1_done.of(c, k + 1))
                        dve.tensor_tensor(ada_t[:, k, :].rearrange("p (b s) -> p b s", s=S),
                                          bank[k][:].rearrange("p (b s) -> p b s", s=S),
                                          ada[:, k, bass.ds(c * CB, CB)].unsqueeze(2).broadcast_to([P, CB, S]),
                                          ALU.mult).then_inc(ada_scaled.sem, 1)

                def values():
                    dve.wait_ge(v_done.sem, v_done.of(c, 2))
                    for s in range(2):
                        dve.tensor_copy(v_bd[64 * s:64 * s + 64, 4:8, :, s, :].rearrange("p b j d -> p (b j) d"),
                                        bank[1][64 * s:64 * s + 64, :].rearrange("p (j d) -> p j d", d=HD)
                                        ).then_inc(v1_ready.sem, 1)

                def scores(u):
                    for i, r in enumerate(BANK_ORDER):
                        dve.wait_ge(score_done[u].sem, score_done[u].of(c, i + 1))
                        dve.wait_ge(bias_masked[u].sem, bias_masked[u].of(c, i + 1))
                        v = sc[u][:, r].rearrange("p a h k -> p (a h k)")
                        dve.tensor_tensor(v, bank[r][:], v, ALU.add).then_inc(biased[u].sem, 1)
                    dve.wait_ge(biased[u].sem, biased[u].of(c, 4))
                    dve.tensor_reduce(sc_max[u][:], sc[u][:].rearrange("p r a h k -> p (r a h) k"), AX.X,
                                      ALU.max).then_inc(max_ready[u].sem, 1)

                def sums(u):
                    dve.wait_ge(exp_ready[u].sem, exp_ready[u].of(c, 1))
                    vec(dve.tensor_reduce(sc_sum[u][:], sc[u][:].rearrange("p r a h k -> p (r a h) k"), AX.X, ALU.add))
                    dve.reciprocal(sc_inv[u][:], sc_sum[u][:]).then_inc(inv_ready[u].sem, 1)
                    if u == 1:
                        finish()

                return scale_norm, values, scores, sums

            def second_half(c):
                vec, finish = stepper(second_step, c)

                def residual():
                    for g in range(2):
                        dve.wait_ge(wo_done.sem, wo_done.of(c, g + 1))
                        dve.tensor_tensor(x2[:, 2 * g:2 * g + 2, :], bank[6 + g][:].rearrange("p (n d) -> p n d", d=D),
                                          bo[:].unsqueeze(1).broadcast_to([P, 2, D]), ALU.add).then_inc(x2_ready.sem, 1)

                def norm2():
                    dve.wait_ge(x2_ready.sem, x2_ready.of(c, 2))
                    token_stats(vec, x2)
                    normalise(xn2, x2).then_inc(xn2_ready.sem, 1)

                def rotate():
                    dve.wait_ge(x2b_ready.sem, x2b_ready.of(c, 1))
                    for g in range(2):
                        dve.wait_ge(ff2_done.sem, ff2_done.of(c, g + 1))
                        dve.tensor_tensor(x3[:, 2 * g:2 * g + 2, :], bank[6 + g][:].rearrange("p (n d) -> p n d", d=D),
                                          x2[:, 2 * g:2 * g + 2, :], ALU.add).then_inc(x3_ready.sem, 1)
                    v3 = x3[:].rearrange("p n (i a e) -> p n i a e", a=2, e=2)
                    v4 = x4[:].rearrange("p n (i a e) -> p n i a e", a=2, e=2)
                    cs = cos_t[:, bass.ds(B + c * TT * 2, TT * 2)].rearrange("p (n a) -> p n a", a=2)
                    sn = sin_t[:, bass.ds(B + c * TT * 2, TT * 2)].rearrange("p (n a) -> p n a", a=2)
                    cs = cs.unsqueeze(2).broadcast_to([P, TT, S, 2])
                    sn = sn.unsqueeze(2).broadcast_to([P, TT, S, 2])
                    dve.wait_ge(x3_ready.sem, x3_ready.of(c, 2))
                    dve.tensor_tensor(rot[0], v3[:, :, :, :, 0], cs, ALU.mult)
                    vec(dve.tensor_tensor(rot[1], v3[:, :, :, :, 1], sn, ALU.mult))
                    vec(dve.tensor_tensor(v4[:, :, :, :, 0], rot[0], rot[1], ALU.add))

                def norm3():
                    dve.wait_ge(odd_ready.sem, odd_ready.of(c, 1))
                    token_stats(vec, x4)
                    normalise(xn3, x4).then_inc(xn3_ready.sem, 1)

                def style():
                    for k in range(KD):
                        dve.wait_ge(h0_ready.sem, h0_ready.of(c, k + 1))
                        for b in range(CB):
                            ins = dve.bn_stats(stats[:, k * CB + b, :], h0[:, k, S * b:S * b + S])
                    vec(ins)
                    dve.nop(nofuse=True)
                    for i in range(KD * CB):
                        ins = dve.bn_aggr(mv[:, i, :], stats[:, i, :])
                    vec(ins)
                    rsqrt(vec, KD * CB, 1e-8)
                    vec(dve.tensor_tensor(in_a[:].rearrange("p (k b) -> p k b", k=KD),
                                          rstd[:].rearrange("p (k b) -> p k b", k=KD),
                                          gamma3[:, :, bass.ds(c * CB, CB)], ALU.mult))
                    vec(dve.tensor_tensor(in_b[:], in_a[:], mv[:, :, 0], ALU.mult))
                    vec(dve.tensor_tensor(in_b[:].rearrange("p (k b) -> p k b", k=KD),
                                          sty[:, KD:2 * KD, bass.ds(c * CB, CB)],
                                          in_b[:].rearrange("p (k b) -> p k b", k=KD), ALU.subtract))
                    for k in range(KD):
                        for b in range(CB):
                            i = k * CB + b
                            ins = dve.tensor_scalar(h3[:, k, S * b:S * b + S], h0[:, k, S * b:S * b + S],
                                                    in_a[:, i:i + 1], in_b[:, i:i + 1], ALU.mult, ALU.add)
                    ins.then_inc(h3_ready.sem, 1)

                ie = iota_e[:].unsqueeze(1).broadcast_to([P, TT, E])

                def wide(x):
                    return x[:].unsqueeze(2).broadcast_to([P, TT, E])

                def largest(top, hot, values, first):
                    vec(dve.tensor_reduce(top[:], values[:], AX.X, ALU.max))
                    vec(dve.tensor_tensor(cand[:], values[:], wide(top), ALU.is_equal))
                    vec(dve.scalar_tensor_tensor(cand[:], cand[:], -100.0, ie, ALU.mult, ALU.add))
                    vec(dve.tensor_reduce(first[:], cand[:], AX.X, ALU.min))
                    vec(dve.tensor_tensor(hot[:], cand[:], wide(first), ALU.is_equal))

                def choose():
                    dve.wait_ge(logit_done.sem, logit_done.of(c, 1))
                    vec(dve.tensor_copy(logit[:], bank[6][:, 0:TT * E].rearrange("p (n e) -> p n e", e=E)))
                    largest(top1, hot1, logit, first1)
                    vec(dve.scalar_tensor_tensor(logit2[:], hot1[:], MASKED, logit[:], ALU.mult, ALU.add))
                    largest(top2, hot2, logit2, first2)
                    dve.tensor_tensor(gap[:], top2[:], top1[:], ALU.subtract).then_inc(gap_ready.sem, 1)
                    dve.tensor_tensor(picks[:, 0:TT, :], hot1[:], hot2[:], ALU.add).then_inc(picks_ready.sem, 1)

                def find_place():
                    dve.wait_ge(rank_done.sem, rank_done.of(c, 1))
                    vec(dve.tensor_tensor(place[:], bank[6][:, 0:TT * E].rearrange("p (n e) -> p n e", e=E),
                                          next_row[:].unsqueeze(1).broadcast_to([P, TT, E]), ALU.add))
                    dve.tensor_tensor(next_row[:], next_row[:], bank[6][:, TT * E:(TT + 1) * E], ALU.add)
                    dve.tensor_tensor(picked[:, 0], place[:], hot1[:], ALU.mult)
                    vec(dve.tensor_tensor(picked[:, 1], place[:], hot2[:], ALU.mult))
                    vec(dve.tensor_reduce(slot_f[:], picked[:], AX.X, ALU.add))
                    dve.tensor_copy(slot[:], slot_f[:]).then_inc(slot_ready.sem, 1)
                    finish()

                def token_gates():
                    dve.wait_ge(rows_sent.sem, rows_sent.of(c, 0))
                    dve.tensor_copy(disp[:, :, D].bitcast(I32), tok_id[:, bass.ds(c * TT, TT)])
                    dve.tensor_scalar(disp[:, :, D + 1], first1[:], 100.0, None, ALU.add)
                    dve.wait_ge(gap_exp.sem, gap_exp.of(c, 1))
                    vec(dve.tensor_scalar(gate_d[:], gap_e[:], 1.0, None, ALU.add))
                    vec(dve.reciprocal(gate1[:], gate_d[:]))
                    vec(dve.tensor_tensor(gate2[:], gap_e[:], gate1[:], ALU.mult))
                    vec(dve.tensor_scalar(disp[:, :, D + 2], gate2[:], 1.0 / W_SCALE, None, ALU.mult))
                    dve.scalar_tensor_tensor(disp[:, :, D + 3], gate1[:], 1.0 / W_SCALE, disp[:, :, D + 2], ALU.mult,
                                             ALU.subtract).then_inc(disp_ready.sem, 1)
                    dve.tensor_tensor(gated1[:], hot1[:], wide(gate1), ALU.mult)
                    vec(dve.tensor_tensor(gated2[:], hot2[:], wide(gate2), ALU.mult))
                    dve.tensor_tensor(gate[:], gated1[:], gated2[:], ALU.add).then_inc(gate_ready.sem, 1)

                def fill_rows():
                    for g in range(2):
                        dve.wait_ge(rows_hi.sem, rows_hi.of(c, g + 1))
                        dve.tensor_tensor(disp[:, 2 * g:2 * g + 2, P:D].bitcast(F16),
                                          bank[4 + g][:].rearrange("p (i d) -> p i d", d=D),
                                          disp[:, 2 * g:2 * g + 2, 0:P].bitcast(F16), ALU.subtract
                                          ).then_inc(rows_ready.sem, 1)

                def copy_gates():
                    dve.wait_ge(gate_turned.sem, gate_turned.of(c, 1))
                    dve.tensor_copy(gate_f[:], bank[2][0:E, :]).then_inc(gate_f_ready.sem, 1)

                def accumulate():
                    dve.wait_ge(x_stored.sem, x_stored.of(c, 0))
                    for g in range(2):
                        dve.wait_ge(b2_done.sem, b2_done.of(c, g + 1))
                        dve.tensor_tensor(x4b[:, 2 * g:2 * g + 2, :],
                                          bank[2 + g][:].rearrange("p (n d) -> p n d", d=D),
                                          x4[:, 2 * g:2 * g + 2, :], ALU.add).then_inc(acc_ready.sem, 1)

                return (residual, norm2, rotate, norm3, style, choose, token_gates, find_place, copy_gates, accumulate,
                        fill_rows)

            hidden, residual, norms = adapter(0)
            scale_norm, values, scores, sums = attention(0)
            step(dve.tensor_copy(time_f[:], time_i[:]))
            step(dve.tensor_scalar(quot[:], time_f[:], 0.01, None, ALU.mult))
            step(dve.tensor_scalar(q_hi[:], quot[:], 4097.0, None, ALU.mult))
            step(dve.tensor_tensor(q_lo[:], q_hi[:], quot[:], ALU.subtract))
            step(dve.tensor_tensor(q_hi[:], q_hi[:], q_lo[:], ALU.subtract))
            step(dve.tensor_tensor(q_lo[:], quot[:], q_hi[:], ALU.subtract))
            step(dve.scalar_tensor_tensor(time_f[:], q_hi[:], -100.0, time_f[:], ALU.mult, ALU.add))
            step(dve.scalar_tensor_tensor(time_f[:], q_lo[:], -100.0, time_f[:], ALU.mult, ALU.add))
            step(dve.scalar_tensor_tensor(time_f[:], time_f[:], 0.01, quot[:], ALU.mult, ALU.add))
            step(dve.tensor_scalar(angle[:, 0:B], time_f[:], 4000.0, freqs[:, 0:1], ALU.mult, ALU.mult))
            step(dve.tensor_scalar(turns[:], angle[:], INV_2PI, ROUND, ALU.mult, ALU.add))
            step(dve.tensor_scalar(turns[:], turns[:], ROUND, None, ALU.subtract))
            for part in TWO_PI_PARTS:
                step(dve.scalar_tensor_tensor(angle[:], turns[:], -part, angle[:], ALU.mult, ALU.add))
            step(dve.tensor_scalar(angle[:], angle[:], float(np.float32(3.1415925)), -float(np.float32(3.1415925)),
                                   ALU.min, ALU.max))
            step(dve.scalar_tensor_tensor(cos_in[:], angle[:], -1.0, angle[:], ALU.mult, ALU.max))
            step(dve.tensor_scalar(cos_in[:], cos_in[:], -1.0, HALF_PI, ALU.mult, ALU.add))
            assert done[0] == SETUP_ANGLES
            dve.wait_ge(cond_in, N_COND)
            step(dve.tensor_copy(sub_f[:], sub_i[:]))
            step(dve.tensor_scalar(sub_f[:], sub_f[:], 0.0, float(NSUB - 1), ALU.max, ALU.min))
            step(dve.tensor_scalar(hot_sub[:], sub_f[0:NSUB, :], iota_p[0:NSUB, 0:1], None, ALU.is_equal))
            assert done[0] == SETUP_SUB
            step(dve.tensor_scalar(bq4[:], bq[:], 0.25, None, ALU.mult))
            step(dve.tensor_tensor(bkp[:], bk[:].unsqueeze(2).broadcast_to([P, KD, 2]),
                                   parity[:].unsqueeze(1).broadcast_to([P, KD, 2]), ALU.mult))
            dve.wait_ge(setup_pe, 2)
            step(dve.tensor_copy(se[:], bank[4][0:SE, 0:B]))
            assert done[0] == SETUP_SE
            dve.wait_ge(setup_pe, 3)
            step(dve.tensor_scalar(hyp1[:], bank[5][0:SH, 0:B], hyp_b1[:, 0:1], 0.0, ALU.add, ALU.max))
            dve.wait_ge(setup_pe, 4)
            step(dve.tensor_scalar(hyp2[:], bank[6][0:SH, 0:B], hyp_b2[:, 0:1], None, ALU.add))
            dve.wait_ge(setup_pe, 5)
            step(dve.tensor_scalar(sty1[:], bank[7][0:SH // 2, 0:B], sty_b1[:, 0:1], 0.0, ALU.add, ALU.max))
            dve.wait_ge(setup_pe, 6)
            for m in range(2 * KD):
                step(dve.tensor_scalar(sty[:, m, :], bank[4][:, B * m:B * m + B], sty_b2[:, m:m + 1], None, ALU.add))
            step(dve.scalar_tensor_tensor(soft[:, 0], sty[:, 0:KD, :], -1.0, sty[:, 0:KD, :], ALU.mult, ALU.min))
            assert done[0] == SETUP_ABS
            dve.wait_ge(setup_act, 5)
            step(dve.tensor_scalar(soft[:, 2], soft[:, 1], 1.0, None, ALU.add))
            step(dve.tensor_scalar(gamma3[:], soft[:, 2], -1.0, None, ALU.add))
            step(dve.tensor_tensor(gamma3[:], soft[:, 1], gamma3[:], ALU.subtract))
            step(dve.scalar_tensor_tensor(gamma3[:], sty[:, 0:KD, :], 0.0, gamma3[:], ALU.max, ALU.add))
            dve.wait_ge(setup_act, 6)
            step(dve.tensor_tensor(gamma3[:], gamma3[:], soft[:, 3], ALU.add))
            step(dve.tensor_scalar(gamma3[:], gamma3[:], 1e-8, None, ALU.add))
            dve.wait_ge(setup_pe, 7)
            for m in range(2 * KD):
                step(dve.tensor_scalar(ada[:, m, :], bank[5][:, B * m:B * m + B], b_ada[:, m:m + 1],
                                       1.0 if m < KD else 0.0, ALU.add, ALU.add))
            dve.drain().then_inc(cond_ready, 1)
            hidden()
            residual()
            norms()
            scale_norm()
            dve.wait_ge(main_in, N_MAIN)
            split_low(0, 0)
            values()
            scores(0)
            split_low(0, 1)
            scores(1)
            hidden, adapter_residual, norms = adapter(1)
            hidden()
            sums(0)
            adapter_residual()
            sums(1)
            split_low(0, 2)
            norms()
            residual, *_ = second_half(0)
            residual()
            scale_norm, *_ = attention(1)
            scale_norm()
            split_low(0, 3)

            def beside(c, with_adapter):
                _, values, scores, sums = attention(c + 1)
                (_, norm2, rotate, norm3, style, choose, token_gates, find_place, copy_gates, accumulate,
                 fill_rows) = second_half(c)
                norm2()
                values()
                if with_adapter:
                    hidden, adapter_residual, norms = adapter(c + 2)
                    scale_norm, *_ = attention(c + 2)
                    hidden()
                    adapter_residual()
                    norms()
                scores(0)
                split_low(c + 1, 0)
                scores(1)
                sums(0)
                split_low(c + 1, 1)
                rotate()
                if with_adapter:
                    scale_norm()
                norm3()
                sums(1)
                style()
                split_low(c + 1, 2)
                choose()
                token_gates()
                find_place()
                copy_gates()
                fill_rows()
                split_low(c + 1, 3)
                residual, *_ = second_half(c + 1)
                residual()
                accumulate()

            with dve.Fori(0, NCH - 2) as c:
                beside(c, True)
            beside(NCH - 2, False)
            (_, norm2, rotate, norm3, style, choose, token_gates, find_place, copy_gates, accumulate,
             fill_rows) = second_half(NCH - 1)
            for run_stage in (norm2, rotate, norm3, style, choose, token_gates, fill_rows, find_place):
                run_stage()
            planned = [0]

            def plan_step(ins):
                planned[0] += 1
                ins.then_inc(plan, 1)
                dve.wait_ge(plan, planned[0])

            dve.tensor_copy(rest_i[:], next_row[0:1, :]).then_inc(rest_ready, 1)
            plan_step(dve.tensor_tensor(seen[:], next_row[:], region[:], ALU.subtract))
            plan_step(dve.tensor_tensor(over[:], seen[:].unsqueeze(2).broadcast_to([P, E, NT]),
                                        tile_m[:].unsqueeze(1).broadcast_to([P, E, NT]), ALU.is_gt))
            plan_step(dve.tensor_reduce(n_tiles[:], over[:], AX.X, ALU.add))
            plan_step(dve.tensor_copy(ends[:], n_tiles[:]))
            for e in range(1, E):
                plan_step(dve.tensor_tensor(ends[:, e:e + 1], ends[:, e:e + 1], ends[:, e - 1:e], ALU.add))
            plan_step(dve.tensor_tensor(past[:], iota_t[:].unsqueeze(2).broadcast_to([P, ENTRIES, E]),
                                        ends[:].unsqueeze(1).broadcast_to([P, ENTRIES, E]), ALU.is_ge))
            plan_step(dve.tensor_reduce(tile_e[:], past[:], AX.X, ALU.add))
            plan_step(dve.tensor_tensor(past_n[:], past[:], n_tiles[:].unsqueeze(1).broadcast_to([P, ENTRIES, E]), ALU.mult))
            plan_step(dve.tensor_reduce(tile_s[:], past_n[:], AX.X, ALU.add))
            plan_step(dve.tensor_tensor(tile_s[:], iota_t[:], tile_s[:], ALU.subtract))
            plan_step(dve.tensor_scalar(tile_l[:], tile_e[:], E - 0.5, None, ALU.is_lt))
            plan_step(dve.tensor_tensor(tile_s[:], tile_s[:], tile_l[:], ALU.mult))
            plan_step(dve.tensor_scalar(tile_r[:], tile_e[:], float(CAP), None, ALU.mult))
            plan_step(dve.scalar_tensor_tensor(tile_r[:], tile_s[:], float(P), tile_r[:], ALU.mult, ALU.add))
            plan_step(dve.tensor_scalar(tile_e[:], tile_e[:], float(E - 1), None, ALU.min))
            plan_step(dve.tensor_copy(tile_ri[:], tile_r[0:1, :]))
            plan_step(dve.tensor_copy(tile_ei[:], tile_e[0:1, :]))
            for j in range(STEPS + 1, -1, -1):
                of_turns = tile_e[:, j:j + TURNS * STEPS + 1:STEPS]
                if j == STEPS + 1:
                    plan_step(dve.tensor_copy(digits[:], of_turns))
                else:
                    plan_step(dve.scalar_tensor_tensor(digits[:], digits[:], float(DIGIT), of_turns, ALU.mult, ALU.add))
            dve.tensor_copy(turn_ei[:], digits[0:1, :]).then_inc(plan_ready, 1)
            copy_gates()
            accumulate()
            dve.wait_ge(acc_ready.sem, acc_ready.of(NCH, 0))
            dve.wait_ge(w_out.sem, w_out.of(NCH, 0))

            def rows_in(n, j):
                dve.wait_ge(turned, n + 1)
                dve.tensor_copy(xs_f[j][:].rearrange("p k n -> p (k n)"), bank[6 + j][:, 0:D].bitcast(F16)
                                ).then_inc(xs_f_ready, 1)
                dve.tensor_copy(meta[:, bass.ds(n, 1), :].rearrange("p a w -> p (a w)").bitcast(U32),
                                xs[j][:, D:ROW].bitcast(U32)).then_inc(gate_step, 1)
                dve.tensor_scalar(gates[:, bass.ds(n, 1)], xs[j][:, D + 1:D + 2], tile_e[:, bass.ds(n, 1)],
                                  xs[j][:, D + 3:D + 4], ALU.is_equal, ALU.mult).then_inc(gate_step, 1)
                dve.wait_ge(gate_step, n * 2 + 2)
                dve.tensor_tensor(gates[:, bass.ds(n, 1)], gates[:, bass.ds(n, 1)], xs[j][:, D + 2:D + 3],
                                  ALU.add).then_inc(gates_ready, 1)

            def outputs(n, j):
                dve.wait_ge(ys_low_ready, n + 1)
                dve.wait_ge(added, n + 1)
                dve.nop(nofuse=True)
                dve.scalar_tensor_tensor(ys[j], bank[4 + j][:, 0:D], gates[:, bass.ds(n, 1)], ys_low[j], ALU.mult,
                                         ALU.add).then_inc(ys_ready, 1)

            def halves(n, j, m, g):
                dve.wait_ge(h32_ready, n * 2 + g + 1)
                dve.tensor_copy(h_hi[m][:, 4 * g:4 * g + 4, :], h32[j][:, 4 * g:4 * g + 4, :]).then_inc(hi_ready, 1)
                dve.wait_ge(hi_ready, n * 2 + g + 1)
                dve.tensor_tensor(h_lo[m][:, 4 * g:4 * g + 4, :], h32[j][:, 4 * g:4 * g + 4, :],
                                  h_hi[m][:, 4 * g:4 * g + 4, :], ALU.subtract).then_inc(lo_ready, 1)

            dve.sem_inc(ys_ready, 2)
            rows_in(0, 0)
            rows_in(1, 1)
            for g in range(2):
                halves(0, 0, 0, g)
            rows_in(2, 0)
            for g in range(2):
                halves(1, 1, 1, g)
            with dve.Fori(0, TURNS) as i:
                for j in range(STEPS):
                    rows_in(i * STEPS + j + 3, (j + 1) % 2)
                    halves(i * STEPS + j + 2, j % 2, (j + 2) % 3, 0)
                    outputs(i * STEPS + j, j % 2)
                    halves(i * STEPS + j + 2, j % 2, (j + 2) % 3, 1)
            for n in range(LEFT, TILES):
                rows_in(n + 1, (n + 1) % 2)
                halves(n, n % 2, n % 3, 0)
                outputs(n - 2, n % 2)
                halves(n, n % 2, n % 3, 1)
            for n in range(TILES - 2, TILES):
                outputs(n, n % 2)

        @block.tensor
        def _(pe):
            for free_at_first in (down_done, expert_done, v_done, wo_done, prob_turned[0], prob_turned[1]):
                pe.sem_inc(free_at_first.sem, 1)
            pe.wait_ge(early_in, N_EARLY)
            pe.wait_ge(setup, SETUP_DOM - 1)
            pe.matmul(bank[7][0:A, 0:B], dom_emb[:], hot_dom[:], start=True, stop=False)
            pe.matmul(bank[7][0:A, 0:B], exp_b[:], hot_val[:], start=False, stop=True).then_inc(setup_pe, 1)
            def turn(z, k, first_bank, done):
                for i in range(TT):
                    mm = pe.transpose(bank[first_bank + k][:, P * i:P * i + P], z[:, i, P * k:P * k + P], ident[:])
                mm.then_inc(done.sem, 1)

            def down_projection(c):
                pe.wait_ge(x_f_in.sem, x_f_in.of(c, 16))
                for k in range(KD):
                    mm = pe.matmul(bank[2][0:A, :], down_w[:, k, :], x_f[:, k, :], start=(k == 0), stop=(k == KD - 1))
                mm.then_inc(down_done.sem, 1)

            def domain_experts(c):
                pe.wait_ge(hid_ready.sem, hid_ready.of(c, 1))
                pe.wait_ge(w_sel_ready.sem, w_sel_ready.of(c, 1))
                pe.nop(nofuse=True)
                for b in range(CB):
                    mm = pe.matmul(bank[3][0:A, S * b:S * b + S], w_sel[:, b, :], hid[:, S * b:S * b + S],
                                   start=True, stop=True)
                mm.then_inc(expert_done.sem, 1)

            def up_projection(c):
                pe.wait_ge(hid2_ready.sem, hid2_ready.of(c, 1))
                for i in range(TT):
                    mm = pe.matmul(bank[2 + i // 2][:, D * (i % 2):D * (i % 2) + D], hid2[:, P * i:P * i + P], up_w[:],
                                   start=True, stop=True)
                    if i % 2:
                        mm.then_inc(up_done.sem, 1)

            def turn1(c):
                pe.wait_ge(xn1_ready.sem, xn1_ready.of(c, 1))
                for k in range(KD):
                    turn(xn1, k, 0, turn1_done)

            def project(c, first_bank, w, done):
                for m in range(KD):
                    for k in range(KD):
                        mm = pe.matmul(bank[first_bank + m][:], w[:, k, P * m:P * m + P], x1[:, k, :],
                                       start=(k == 0), stop=(k == KD - 1))
                    mm.then_inc(done.sem, 1)

            def queries(c):
                pe.wait_ge(x1_ready.sem, x1_ready.of(c, 2))
                project(c, 0, wq, q_done)

            def keys(c):
                project(c, 2, wk, k_done)

            def values(c):
                pe.wait_ge(q_ready.sem, q_ready.of(c, 2))
                for b in range(CB):
                    for s in range(2):
                        for k in range(KD):
                            mm = pe.matmul(bank[b // 4][64 * s:64 * s + 64, P * (b % 4):P * (b % 4) + P],
                                           x1[:, k, S * b:S * b + S], wv[:, k, P * s:P * s + P],
                                           start=(k == 0), stop=(k == KD - 1))
                    if b % 4 == 3:
                        mm.then_inc(v_done.sem, 1)

            def scores(c, u):
                if u == 0:
                    pe.wait_ge(k_ready.sem, k_ready.of(c, 2))
                for i, r in enumerate(BANK_ORDER):
                    if u == 1:
                        pe.wait_ge(biased[0].sem, biased[0].of(c, i + 1))
                    elif i == 2:
                        pe.wait_ge(v0_ready.sem, v0_ready.of(c, 2))
                        pe.wait_ge(v1_ready.sem, v1_ready.of(c, 2))
                    for a in range(2):
                        for b2 in range(2):
                            b = 4 * u + 2 * a + b2
                            for h in range(2):
                                at = a * 256 + h * P
                                mm = pe.matmul(
                                    bank[r][64 * b2:64 * b2 + 64, at:at + P].rearrange("q (s k) -> q s k", s=2),
                                    q_f[32 * r:32 * r + 32, h, S * b:S * b + S],
                                    k_f[32 * r:32 * r + 32, h, :, S * b:S * b + S], start=True, stop=True)
                    mm.then_inc(score_done[u].sem, 1)

            def context(c, u):
                pe.wait_ge(prob_ready[u].sem, prob_ready[u].of(c, 1))
                if u == 0:
                    pe.wait_ge(biased[1].sem, biased[1].of(c, 4))
                for r in range(4):
                    if r >= 2:
                        pe.wait_ge(p_f_ready[u].sem, p_f_ready[u].of(c, r - 1))
                    elif u == 1:
                        pe.wait_ge(p_f_ready[0].sem, p_f_ready[0].of(c, 3 + r))
                    for i in range(4):
                        a, h = i // 2, i % 2
                        mm = pe.transpose(bank[r % 2][:, P * i:P * i + P],
                                          sc[u][:, r, a, 2 * h:2 * h + 2, :].rearrange("p s k -> p (s k)"), ident[:])
                    mm.then_inc(prob_turned[u].sem, 1)
                for r in range(4):
                    pe.wait_ge(p_f_ready[u].sem, p_f_ready[u].of(c, r + 1))
                    for a in range(2):
                        for b2 in range(2):
                            for h in range(2):
                                at = h * 256 + a * P + b2 * S
                                mm = pe.matmul(bank[2 + u][32 * r:32 * r + 32, at:at + S],
                                               v_bd[:, 4 * u + 2 * a + b2, 4 * h + r].rearrange("p s d -> p (s d)"),
                                               p_f[:, r, a, h, S * b2:S * b2 + S], start=True, stop=True)
                mm.then_inc(ctx_done[u].sem, 1)

            def output_projection(c):
                pe.wait_ge(kept_ready.sem, kept_ready.of(c, 1))
                pe.wait_ge(slot_ready.sem, slot_ready.of(c, 0))
                for u in range(2):
                    pe.wait_ge(ctx_ready[u].sem, ctx_ready[u].of(c, 2))
                for g in range(2):
                    for i in range(2):
                        at = P * (2 * g + i)
                        for k in range(KD):
                            pe.matmul(bank[6 + g][:, D * i:D * i + D], ctx_f[:, k, at:at + P], wo[:, k, :],
                                      start=(k == 0), stop=False, skip_group_check=True)
                        for k in range(KD):
                            mm = pe.matmul(bank[6 + g][:, D * i + P * k:D * i + P * k + P],
                                           x1_kept[:, k, at:at + P], ident[:],
                                           start=False, stop=True, skip_group_check=True)
                    mm.then_inc(wo_done.sem, 1)

            def turn2(c):
                pe.wait_ge(xn2_ready.sem, xn2_ready.of(c, 1))
                pe.wait_ge(rows_ready.sem, rows_ready.of(c, 0))
                for k in range(KD):
                    turn(xn2, k, 4, turn2_done)

            def feed_forward1(c, some):
                pe.wait_ge(h_ready.sem, h_ready.of(c, 2))
                for f in some:
                    if f >= 2:
                        pe.wait_ge(ff_ready.sem, ff_ready.of(c, f - 1))
                    for k in range(KD):
                        mm = pe.matmul(bank[4 + f % 2][:], w1[:, k, P * f:P * f + P], h_f[:, k, :],
                                       start=(k == 0), stop=(k == KD - 1))
                    mm.then_inc(ff1_done.sem, 1)

            def feed_forward2(c, some):
                pe.wait_ge(ff_ready.sem, ff_ready.of(c, KF))
                for i in some:
                    for f in range(KF):
                        mm = pe.matmul(bank[6 + i // 2][:, D * (i % 2):D * (i % 2) + D], ff[:, f, P * i:P * i + P],
                                       w2[:, f, :], start=(f == 0), stop=(f == KF - 1))
                    if i % 2:
                        mm.then_inc(ff2_done.sem, 1)

            def turn3(c):
                pe.wait_ge(xn3_ready.sem, xn3_ready.of(c, 1))
                for k in range(KD):
                    turn(xn3, k, 4, turn3_done)

            def route(c):
                pe.wait_ge(h3_ready.sem, h3_ready.of(c, 1))
                pe.wait_ge(x3_ready.sem, x3_ready.of(c, 2))
                for i in range(TT):
                    for k in range(KD):
                        mm = pe.matmul(bank[6][:, E * i:E * i + E], h3[:, k, P * i:P * i + P], router[:, k, :],
                                       start=(k == 0), stop=(k == KD - 1))
                mm.then_inc(logit_done.sem, 1)
                for g in range(2):
                    for i in range(2):
                        for k in range(KD):
                            mm = pe.transpose(bank[4 + g][:, D * i + P * k:D * i + P * k + P],
                                              h3[:, k, P * (2 * g + i):P * (2 * g + i) + P], ident[:])
                    mm.then_inc(rows_done.sem, 1)

            def rank(c):
                pe.wait_ge(picks_ready.sem, picks_ready.of(c, 1))
                pe.matmul(bank[6][:, 0:(TT + 1) * E], lower[:], picks[:].rearrange("p n e -> p (n e)"),
                          start=True, stop=False, skip_group_check=True)
                for i in range(TT):
                    mm = pe.matmul(bank[6][:, (i + 1) * E:(TT + 1) * E], ones[:],
                                   picks[:, i:i + 1, :].broadcast_to([P, TT - i, E]), start=False, stop=True,
                                   skip_group_check=True)
                mm.then_inc(rank_done.sem, 1)

            def turn_gates(c):
                pe.wait_ge(gate_ready.sem, gate_ready.of(c, 1))
                for i in range(TT):
                    mm = pe.transpose(bank[2][0:E, P * i:P * i + P], gate[:, i, :], ident[:])
                mm.then_inc(gate_turned.sem, 1)

            def expert_biases(c):
                pe.wait_ge(gate_f_ready.sem, gate_f_ready.of(c, 1))
                for i in range(TT):
                    mm = pe.matmul(bank[2 + i // 2][:, D * (i % 2):D * (i % 2) + D], gate_f[:, P * i:P * i + P], moe_b2[:],
                                   start=True, stop=True)
                    if i % 2:
                        mm.then_inc(b2_done.sem, 1)

            down_projection(0)
            pe.wait_ge(cond_in, N_COND)
            pe.wait_ge(setup, SETUP_SUB)
            pe.matmul(bank[4][0:SE, 0:B], subj_emb[:], hot_sub[:], start=True, stop=True).then_inc(setup_pe, 1)
            pe.wait_ge(setup, SETUP_SE)
            pe.matmul(bank[5][0:SH, 0:B], hyp_w1[:], se[:], start=True, stop=True).then_inc(setup_pe, 1)
            pe.wait_ge(setup, SETUP_SE + 1)
            pe.matmul(bank[6][0:SH, 0:B], hyp_w2[:], hyp1[:], start=True, stop=True).then_inc(setup_pe, 1)
            pe.wait_ge(setup, SETUP_SE + 2)
            pe.matmul(bank[7][0:SH // 2, 0:B], sty_w1[:], hyp2[:], start=True, stop=True).then_inc(setup_pe, 1)
            pe.wait_ge(setup, SETUP_SE + 3)
            for m in range(2 * KD):
                mm = pe.matmul(bank[4][:, B * m:B * m + B], sty_w2[:, P * m:P * m + P], sty1[:], start=True, stop=True)
            mm.then_inc(setup_pe, 1)
            pe.wait_ge(setup_act, 4)
            for m in range(2 * KD):
                for k in range(KD):
                    mm = pe.matmul(bank[5][:, B * m:B * m + B], w_ada[:, k, P * m:P * m + P], emb[:, k, :],
                                   start=(k == 0), stop=(k == KD - 1))
            mm.then_inc(setup_pe, 1)
            domain_experts(0)
            pe.wait_ge(zeroed, 8)
            up_projection(0)
            turn1(0)
            pe.wait_ge(cond_ready, 1)
            pe.wait_ge(main_in, N_MAIN)
            queries(0)
            keys(0)
            values(0)
            scores(0, 0)
            scores(0, 1)
            pe.wait_ge(biased[1].sem, biased[1].of(0, 4))
            down_projection(1)
            domain_experts(1)
            up_projection(1)
            pe.wait_ge(y_ready.sem, y_ready.of(1, 2))
            context(0, 0)
            context(0, 1)
            output_projection(0)
            turn1(1)
            queries(1)
            keys(1)

            def beside(c, adapter):
                values(c + 1)
                pe.wait_ge(k_ready.sem, k_ready.of(c + 1, 2))
                pe.wait_ge(acc_ready.sem, acc_ready.of(c, 0))
                if adapter:
                    down_projection(c + 2)
                turn2(c)
                feed_forward1(c, range(0, 2))
                if adapter:
                    domain_experts(c + 2)
                feed_forward1(c, range(2, 4))
                if adapter:
                    up_projection(c + 2)
                feed_forward1(c, range(4, KF))
                if adapter:
                    pe.wait_ge(y_ready.sem, y_ready.of(c + 2, 2))
                scores(c + 1, 0)
                feed_forward2(c, range(0, 2))
                scores(c + 1, 1)
                feed_forward2(c, range(2, TT))
                if adapter:
                    pe.wait_ge(biased[1].sem, biased[1].of(c + 1, 4))
                    turn1(c + 2)
                    queries(c + 2)
                turn3(c)
                if adapter:
                    keys(c + 2)
                    pe.wait_ge(q_ready.sem, q_ready.of(c + 2, 2))
                    pe.wait_ge(k_ready.sem, k_ready.of(c + 2, 1))
                context(c + 1, 0)
                if adapter:
                    pe.wait_ge(k_ready.sem, k_ready.of(c + 2, 2))
                context(c + 1, 1)
                route(c)
                rank(c)
                for u in range(2):
                    pe.wait_ge(ctx_ready[u].sem, ctx_ready[u].of(c + 1, 2))
                turn_gates(c)
                output_projection(c + 1)
                expert_biases(c)

            with pe.Fori(0, NCH - 2) as c:
                beside(c, True)
            beside(NCH - 2, False)
            turn2(NCH - 1)
            feed_forward1(NCH - 1, range(KF))
            feed_forward2(NCH - 1, range(TT))
            for run_stage in (turn3, route, rank, turn_gates, expert_biases):
                run_stage(NCH - 1)
            pe.wait_ge(acc_ready.sem, acc_ready.of(NCH, 0))
            pe.wait_ge(plan_ready, 1)

            def turn_rows(n, j, turn):
                pe.wait_ge(xs_in[j], turn * 16 + 16)
                for k in range(4):
                    mm = pe.transpose(bank[6 + j][:, 64 * k:64 * k + 64].bitcast(F16),
                                      xs[j][:, 64 * k:64 * k + 64].bitcast(F16), ident16[:])
                mm.then_inc(turned, 1)

            def up(j, e, f):
                o = bank[2 * j + f // 4][:, P * (f % 4):P * (f % 4) + P]
                for k in range(KD):
                    hi = w_moe[:, bass.ds(e * WE + (k * FF + f * P), P)]
                    lo = w_moe[:, bass.ds(e * WE + (WE // 4 + k * FF + f * P), P)]
                    pe.matmul(o, hi, xs_f[j][:, k, :], start=(k == 0), stop=False)
                    pe.matmul(o, hi, xs_f[j][:, KD + k, :], start=False, stop=False)
                    mm = pe.matmul(o, lo, xs_f[j][:, k, :], start=False, stop=(k == KD - 1))
                if f % 4 == 3:
                    mm.then_inc(m1_done, 1)

            def down(j, m, e, f):
                o = bank[4 + j][:, 0:2 * D]
                rows_of = w_moe[:, bass.ds(e * WE + (WE // 2 + f * 2 * D), 2 * D)]
                pe.matmul(o, h_hi[m][:, f, :], rows_of, start=(f == 0), stop=(f == KF - 1), skip_group_check=True)
                mm = pe.matmul(o[:, 0:D], h_lo[m][:, f, :], rows_of[:, 0:D], start=False, stop=(f == KF - 1),
                               skip_group_check=True)
                if f == KF - 1:
                    mm.then_inc(m2_done, 1)

            def experts_of(i, count):
                number = pe.value_load(turn_ei[0:1, bass.ds(i, 1)], min_val=0, max_val=DIGIT ** (STEPS + 2) - 1)
                return [(number >> (DIGIT.bit_length() - 1) * j) & (E - 1) for j in range(count)]

            def tile_in(n):
                pe.wait_ge(xs_f_ready, n + 1)
                pe.nop(nofuse=True)

            def step(n, j, m, turn, e, e_before):
                tile_in(n)
                for f in range(KF):
                    up(j, e, f)
                    down(j, (m + 1) % 3, e_before, f)
                    if f == KF // 2:
                        turn_rows(n + 1, 1 - j, turn)

            turn_rows(0, 0, 0)
            turn_rows(1, 1, 0)
            experts = experts_of(0, 2)
            for n in range(2):
                tile_in(n)
                for f in range(KF):
                    up(n, experts[n], f)
            turn_rows(2, 0, 1)
            with pe.Fori(0, TURNS) as i:
                experts = experts_of(i, STEPS + 2)
                for j in range(STEPS):
                    step(i * STEPS + j + 2, j % 2, (j + 2) % 3, i * (STEPS // 2) + (j + 3) // 2, experts[j + 2], experts[j])
            experts = experts_of(TURNS, TILES - LEFT + 2)
            for n in range(LEFT, TILES):
                step(n, n % 2, n % 3, (n + 1) // 2, experts[n - LEFT + 2], experts[n - LEFT])
            for n in range(TILES - 2, TILES):
                pe.wait_ge(lo_ready, n * 2 + 2)
                pe.wait_ge(ys_ready, n + 1)
                for f in range(KF):
                    down(n % 2, n % 3, experts[n - LEFT + 2], f)


SETUP_DOM = 7
SETUP_ANGLES = SETUP_DOM + 18
SETUP_SUB = SETUP_ANGLES + 3
SETUP_SE = SETUP_SUB + 3
SETUP_ABS = SETUP_SE + 8


def kernel(**inputs):
    import concourse.bacc as bacc
    from concourse.bass_utils import run_bass_kernel_spmd as run

    a = {k: np.ascontiguousarray(v) for k, v in inputs.items()}
    c_ = np.ascontiguousarray

    def cols(v):
        return c_(v.reshape(-1, P).T)

    def row(v):
        return v.reshape(1, -1)

    def every_lane(v):
        return np.broadcast_to(v.astype(np.float32), (P, len(v)))

    x = a["x"].reshape(N, D)
    bias = a["fside_Bx16xSxS_0"].reshape(B // 4, 2, 2, 2, 4, 2, S, S)
    bias = bias.transpose(0, 2, 6, 4, 1, 3, 5, 7).reshape(B // 4, P, 2048)
    mask = a["mask_Bx1xSxS_bk0"].reshape(NT, 2, S, S).transpose(1, 2, 0, 3).reshape(P, NT, S)
    wv = a["L1_cond_Wv"].reshape(D, H // 2, 2, HD).transpose(0, 2, 1, 3).reshape(D, D)
    th = np.stack([a["condB_theta"], a["condB_phi"]], -1).reshape(NT, 2, 2).transpose(1, 0, 2).reshape(2, 1, 2 * NT)
    angles = np.concatenate([np.zeros((P, B), np.float32), np.broadcast_to(th, (2, S, 2 * NT)).reshape(P, 2 * NT)], 1)
    half = D // 2
    freqs = np.exp(np.arange(half, dtype=np.float32) * np.float32(-np.log(10000.0) / (half - 1)))
    lane = np.arange(P)
    columns = {
        "iota_p": lane.astype(np.float32).reshape(P, 1),
        "parity": ((lane[:, None] // HD) % 2 == np.arange(2)[None, :]).astype(np.float32),
        "freqs": freqs.astype(np.float32).reshape(P, 1), "angles": angles, "down_b": a["L0_cond_down_b"].reshape(A, 1),
        "b_ada": cols(a["L1_cond_b_ada"]), "bq": cols(a["L1_cond_bq"]), "bk": cols(a["L1_cond_bk"]),
        "bv": cols(a["L1_cond_bv"]), "b1": cols(a["L1_cond_b1"]), "g2": cols(a["L1_cond_g2"]),
        "beta2": cols(a["L1_cond_beta2"]), "ln_g": cols(a["L3_cond_ln_g"]), "ln_b": cols(a["L3_cond_ln_b"]),
        "hyp_b1": a["L3_cond_hyp_b1"].reshape(-1, 1), "hyp_b2": a["L3_cond_hyp_b2"].reshape(-1, 1),
        "sty_b1": a["L3_cond_sty_b1"].reshape(-1, 1), "sty_b2": cols(a["L3_cond_sty_b2"]),
        "moe_b1": a["L3_cond_exp_b1"].reshape(E, KF, P).transpose(2, 0, 1).reshape(P, E * KF),
        "iota_e": every_lane(np.arange(E)), "iota_t": every_lane(np.arange(ENTRIES)),
        "tile_m": every_lane(np.arange(NT) * P), "region": every_lane(np.arange(E) * CAP),
    }
    packed = np.zeros((P, sum(width for _, _, width in COLS)), np.float32)
    at = 0
    for name, rows_of_it, width in COLS:
        packed[:rows_of_it, at:at + width] = columns[name]
        at += width
    tokens = np.stack([a["itok_B_0_15"], a["itok_B_34_63"], a["itok_B_6_14"]]).reshape(1, 3 * B)
    tok_id = np.arange(N, dtype=np.int32).reshape(NT, P).T
    laid = {
        "x_f": x.T, "x_t": x, "bias": bias, "mask": mask, "cols": packed,
        "ints": np.concatenate([np.broadcast_to(tokens, (P, 3 * B)), tok_id], 1),
        "mats": np.concatenate([np.eye(P, dtype=np.float32), np.triu(np.ones((P, P), np.float32), 1),
                                a["L3_cond_hyp_w2"], a["L3_cond_sty_w1"]], 1),
        "domains": np.concatenate([a["L0_cond_domain_emb"], a["L0_cond_expert_b"]], 1),
        "down_w": a["L0_cond_down_W"].T, "exp_w": a["L0_cond_expert_W"].transpose(0, 2, 1),
        "up_w": np.concatenate([a["L0_cond_up_W"].T, row(a["L0_cond_up_b"])], 0),
        "norm0": np.stack([a["L0_cond_ln_gamma"], a["L0_cond_ln_beta"]])[None],
        "w_ada": a["L1_cond_W_ada"], "w_qkv": np.concatenate([a["L1_cond_Wq"], a["L1_cond_Wk"], wv], 1),
        "wo": a["L1_cond_Wo"], "biases": np.stack([a["L1_cond_bo"], a["L1_cond_b2"]])[None],
        "w1": a["L1_cond_W1"], "w2": a["L1_cond_W2"], "subj_emb": a["L3_cond_subj_emb"],
        "hyp_w1": a["L3_cond_hyp_w1"], "sty_w2": a["L3_cond_sty_w2"], "router": a["L3_cond_router_w"],
        "moe_w1": a["L3_cond_exp_w1"], "moe_w2": a["L3_cond_exp_w2"], "moe_b2": a["L3_cond_exp_b2"],
    }
    nc = bacc.Bacc("TRN2", target_bir_lowering=False, num_devices=1)
    arrays, tensors = {}, {}
    for name, v in laid.items():
        arrays[f"in_{name}"] = c_(v)
        tensors[name] = nc.dram_tensor(f"in_{name}", v.shape, mybir.dt.from_np(v.dtype), kind="ExternalInput").ap()
    out = nc.dram_tensor("out_x", (N, D), F32, kind="ExternalOutput").ap()
    build(nc, tensors, out)
    r = run(nc, [arrays], core_ids=[0])
    return r.results[0]["out_x"].reshape(B, S, D)
```
